# Optimizing a Trainium2 kernel written in Bass

```python
import numpy as np
import jax
import jax.numpy as jnp

def _softmax(x, axis=-1):
    return jax.nn.softmax(x, axis=axis)

def _gelu(x):
    return jax.nn.gelu(x, approximate=True)

def _silu(x):
    return jax.nn.silu(x)

def _sigmoid(x):
    return jax.nn.sigmoid(x)

def _layernorm(x, axis=-1, eps=1e-05):
    m = jnp.mean(x, axis=axis, keepdims=True)
    v = jnp.var(x, axis=axis, keepdims=True)
    return (x - m) / jnp.sqrt(v + eps)

def _scatter_add(tgt, idx, src, axis=0):
    return tgt.at[idx].add(src)

def _segment_sum(src, seg, n):
    return jax.ops.segment_sum(src, seg, n)
kernel_name = 'mk_early_fusion_d4_tok_img768_r4_f5456f'

def setup_inputs(seed: int=0):
    np.random.seed(seed)
    _w = jnp.asarray

    def _rec_inputs():
        import jax
        import jax.numpy as jnp
        _rk = jax.random.key(seed)
        x = -0.000125008 + 0.999885 * jax.random.normal(jax.random.fold_in(_rk, 1), (16, 1, 256, 256), jnp.float32)
        txt = 0.000269139 + 0.577837 * jax.random.normal(jax.random.fold_in(_rk, 2), (16, 128, 192), jnp.float32)
        return (x, txt)
    x, txt = _rec_inputs()

    def _L0_tok_setup():
        import jax, jax.numpy as jnp
        import numpy as np
        C, H, W = (1, 256, 256)
        P = 32
        D_TOK = 192
        B = 32
        D_PATCH = C * P * P

        def _patchify(x):
            Bx = x.shape[0]
            x = x.reshape(Bx, C, H // P, P, W // P, P)
            x = x.transpose(0, 2, 4, 1, 3, 5)
            return x.reshape(Bx, H // P * (W // P), D_PATCH)
        key = jax.random.key(seed)
        k_x, k_w, k_b = jax.random.split(key, 3)
        x = jax.random.normal(k_x, (B, C, H, W), dtype=jnp.float32)
        bound = 1.0 / np.sqrt(D_PATCH)
        w = jax.random.uniform(k_w, (D_TOK, D_PATCH), jnp.float32, -bound, bound)
        b = jax.random.uniform(k_b, (D_TOK,), jnp.float32, -bound, bound)
        return {'x': x, 'w': w, 'b': b}
    _L0_tok_all = _L0_tok_setup()
    _L0_tok_in = {k: v for k, v in _L0_tok_all.items() if k in ('w', 'b')}
    del _L0_tok_all

    def _L0_attn_setup():
        import jax, jax.numpy as jnp
        import numpy as np
        B, N, D_IN, D_EMB = (8, 512, 192, 192)
        key = jax.random.key(seed)
        k1, k2, k3, k4 = jax.random.split(key, 4)
        x = jax.random.normal(k1, (B, N, D_IN), dtype=jnp.float32)
        Wq = jax.random.normal(k2, (D_EMB, D_IN), dtype=jnp.float32) * D_IN ** (-0.5)
        Wk = jax.random.normal(k3, (D_EMB, D_IN), dtype=jnp.float32) * D_IN ** (-0.5)
        Wv = jax.random.normal(k4, (D_EMB, D_IN), dtype=jnp.float32) * D_IN ** (-0.5)
        return {'x': x, 'Wq': Wq, 'Wk': Wk, 'Wv': Wv}
    _L0_attn_all = _L0_attn_setup()
    _L0_attn_in = {k: v for k, v in _L0_attn_all.items() if k in ('Wq', 'Wk', 'Wv')}
    del _L0_attn_all

    def _L0_ffn_setup():
        import jax, jax.numpy as jnp
        import numpy as np
        B, T, D, E, K = (4, 512, 192, 8, 2)
        H = 4 * D
        key = jax.random.key(seed)
        k0, k1, k2, k3, k4 = jax.random.split(key, 5)
        s = 0.02
        return {'x': jax.random.normal(k0, (B, T, D), jnp.float32), 'router_w': jax.random.uniform(k1, (E, D), jnp.float32, -s * 0.1, s * 0.1), 'Wg': jax.random.uniform(k2, (E, H, D), jnp.float32, -s * 0.4, s * 0.4), 'Wu': jax.random.uniform(k3, (E, H, D), jnp.float32, -s * 0.4, s * 0.4), 'Wd': jax.random.normal(k4, (E, D, H), jnp.float32) * 0.01}
    _L0_ffn_all = _L0_ffn_setup()
    _L0_ffn_in = {k: v for k, v in _L0_ffn_all.items() if k in ('router_w', 'Wg', 'Wu', 'Wd')}
    del _L0_ffn_all

    def _L1_attn_setup():
        import jax, jax.numpy as jnp
        import numpy as np
        LEVEL = 8
        NUM_HEADS = 12
        QN_SYM = float(-(LEVEL // 2))
        QP_SYM = float(LEVEL // 2 - 1)
        QN_ASYM = 0.0
        QP_ASYM = float(LEVEL - 1)

        def fake_quant(x, s, qn, qp):
            xc = jnp.clip(x / s, qn, qp)
            xr = xc + jax.lax.stop_gradient(jnp.round(xc) - xc)
            return s * xr
        key = jax.random.key(seed)
        k0, k1, k2 = jax.random.split(key, 3)
        B, N, C = (4, 512, 192)
        x = jax.random.normal(k0, (B, N, C), dtype=jnp.float32)
        Wqkv = jax.random.normal(k1, (3 * C, C), dtype=jnp.float32) * C ** (-0.5)
        Wproj = jax.random.normal(k2, (C, C), dtype=jnp.float32) * C ** (-0.5)
        bproj = jnp.zeros((C,), dtype=jnp.float32)
        s_q = jnp.asarray(1.0, dtype=jnp.float32)
        s_k = jnp.asarray(1.0, dtype=jnp.float32)
        s_v = jnp.asarray(1.0, dtype=jnp.float32)
        s_attn = jnp.asarray(1.0 / QP_ASYM, dtype=jnp.float32)
        s_after = jnp.asarray(1.0, dtype=jnp.float32)
        return {'x': x, 'Wqkv': Wqkv, 'Wproj': Wproj, 'bproj': bproj, 's_q': s_q, 's_k': s_k, 's_v': s_v, 's_attn': s_attn, 's_after': s_after}
    _L1_attn_all = _L1_attn_setup()
    _L1_attn_in = {k: v for k, v in _L1_attn_all.items() if k in ('Wqkv', 'Wproj', 'bproj', 's_q', 's_k', 's_v', 's_attn', 's_after')}
    del _L1_attn_all

    def _L1_ffn_setup():
        import jax, jax.numpy as jnp
        import numpy as np
        D_MODEL = 192
        N_EXPERTS = 16
        TOP_K = 2
        D_FF = 4 * D_MODEL
        B, L = (4, 512)
        key = jax.random.key(seed)
        ks = jax.random.split(key, 6)
        s_in = 1.0 / np.sqrt(D_MODEL)
        s_ff = 1.0 / np.sqrt(D_FF)
        x = jax.random.normal(ks[0], (B, L, D_MODEL), dtype=jnp.float32)
        Wr = jax.random.uniform(ks[1], (N_EXPERTS, D_MODEL), jnp.float32, -s_in, s_in)
        W1 = jax.random.uniform(ks[2], (N_EXPERTS, D_MODEL, D_FF), jnp.float32, -s_in, s_in)
        b1 = jax.random.uniform(ks[3], (N_EXPERTS, D_FF), jnp.float32, -s_in, s_in)
        W2 = jax.random.uniform(ks[4], (N_EXPERTS, D_FF, D_MODEL), jnp.float32, -s_ff, s_ff)
        b2 = jax.random.uniform(ks[5], (N_EXPERTS, D_MODEL), jnp.float32, -s_ff, s_ff)
        return {'x': x, 'Wr': Wr, 'W1': W1, 'b1': b1, 'W2': W2, 'b2': b2}
    _L1_ffn_all = _L1_ffn_setup()
    _L1_ffn_in = {k: v for k, v in _L1_ffn_all.items() if k in ('Wr', 'W1', 'b1', 'W2', 'b2')}
    del _L1_ffn_all

    def _L2_attn_setup():
        import jax, jax.numpy as jnp
        import numpy as np
        import math
        B, N, C = (8, 1024, 192)
        H = 12
        DH = C // H
        M = 64
        LN_EPS = 1e-05

        def _phi(t, random_features):
            norm_sq = 0.5 * jnp.sum(t * t, axis=-1, keepdims=True)
            proj = jnp.einsum('bhnd,md->bhnm', t, random_features)
            return jnp.exp(proj - norm_sq) * (1.0 / math.sqrt(M))
        key = jax.random.key(seed)
        ks = jax.random.split(key, 7)
        x = jax.random.normal(ks[0], (B, N, C), dtype=jnp.float32)
        W_qkv = jax.random.normal(ks[1], (C, 3 * C), dtype=jnp.float32) * (1.0 / math.sqrt(C))
        W_proj = jax.random.normal(ks[2], (C, C), dtype=jnp.float32) * (1.0 / math.sqrt(C))
        b_proj = jnp.zeros((C,), dtype=jnp.float32)
        gamma = jnp.ones((C,), dtype=jnp.float32)
        beta = jnp.zeros((C,), dtype=jnp.float32)
        random_features = jax.random.normal(ks[3], (M, DH), dtype=jnp.float32) / math.sqrt(DH)
        return {'x': x, 'W_qkv': W_qkv, 'W_proj': W_proj, 'b_proj': b_proj, 'gamma': gamma, 'beta': beta, 'random_features': random_features}
    _L2_attn_all = _L2_attn_setup()
    _L2_attn_in = {k: v for k, v in _L2_attn_all.items() if k in ('W_qkv', 'W_proj', 'b_proj', 'gamma', 'beta', 'random_features')}
    del _L2_attn_all

    def _L2_ffn_setup():
        import jax, jax.numpy as jnp
        import numpy as np
        DEPTH = 11

        def _fff_forward(inputs, weights_in, weights_out, depth=DEPTH):
            B, S, _ = inputs.shape
            n_nodes = weights_in.shape[0]
            max_index = n_nodes - 1
            all_logits = jnp.einsum('bsd,nd->bsn', inputs, weights_in)

            def step(prev_idx, _):
                sel = jnp.clip(prev_idx, 0, max_index)
                logits = jnp.take_along_axis(all_logits, sel[..., None], axis=-1)[..., 0]
                new_idx = jnp.clip(2 * sel + 1 + (logits > 0).astype(sel.dtype), 0, max_index)
                return (new_idx, (logits, new_idx))
            idx0 = jnp.zeros((B, S), dtype=jnp.int32)
            _, (logits_seq, idx_seq) = jax.lax.scan(step, idx0, None, length=depth - 1)
            logits = jnp.concatenate([jnp.zeros((1, B, S), all_logits.dtype), logits_seq], axis=0)
            node_idx = jnp.concatenate([idx0[None], idx_seq], axis=0)
            act = jax.nn.gelu(logits, approximate=False)
            onehot = jax.nn.one_hot(node_idx, n_nodes, dtype=act.dtype)
            coeff = jnp.einsum('dbs,dbsn->bsn', act, onehot)
            return jnp.einsum('bsn,nd->bsd', coeff, weights_out)
        key = jax.random.key(seed)
        k1, k2, k3 = jax.random.split(key, 3)
        B, S, D = (4, 1024, 192)
        n_nodes = 2 * DEPTH - 1
        return {'inputs': jax.random.normal(k1, (B, S, D), dtype=jnp.float32), 'weights_in': jax.random.normal(k2, (n_nodes, D), dtype=jnp.float32), 'weights_out': jax.random.normal(k3, (n_nodes, D), dtype=jnp.float32)}
    _L2_ffn_all = _L2_ffn_setup()
    _L2_ffn_in = {k: v for k, v in _L2_ffn_all.items() if k in ('weights_in', 'weights_out')}
    del _L2_ffn_all

    def _L3_attn_setup():
        import jax, jax.numpy as jnp
        import numpy as np
        DIM = 192
        NUM_HEADS = 12
        HEAD_DIM = DIM // NUM_HEADS
        SCALE = HEAD_DIM ** (-0.5)
        key = jax.random.key(seed)
        k1, k2, k3, k4 = jax.random.split(key, 4)
        B, N, C = (4, 512, DIM)
        x = jax.random.normal(k1, (B, N, C), dtype=jnp.float32)
        w_qkv = jax.random.normal(k2, (3 * C, C), dtype=jnp.float32) * C ** (-0.5)
        w_proj = jax.random.normal(k3, (C, C), dtype=jnp.float32) * C ** (-0.5)
        b_proj = jax.random.normal(k4, (C,), dtype=jnp.float32) * 0.02
        return {'x': x, 'w_qkv': w_qkv, 'w_proj': w_proj, 'b_proj': b_proj}
    _L3_attn_all = _L3_attn_setup()
    _L3_attn_in = {k: v for k, v in _L3_attn_all.items() if k in ('w_qkv', 'w_proj', 'b_proj')}
    del _L3_attn_all

    def _L3_ffn_setup():
        import jax, jax.numpy as jnp
        import numpy as np
        EPS_NORM = 1e-06
        EPS_LN = 1e-05

        def _layernorm(x, g, b):
            mu = jnp.mean(x, axis=-1, keepdims=True)
            var = jnp.mean(jnp.square(x - mu), axis=-1, keepdims=True)
            return (x - mu) * jax.lax.rsqrt(var + EPS_LN) * g + b
        key = jax.random.key(seed)
        ks = jax.random.split(key, 6)
        b, m, d = (8, 256, 192)
        n, p = (64, 16)
        h = 2 * d
        x = jax.random.normal(ks[0], (b, m, d), dtype=jnp.float32)
        phi = jax.random.normal(ks[1], (n, p, d), dtype=jnp.float32)
        ln_g = jnp.ones((n, d), dtype=jnp.float32)
        ln_b = jnp.zeros((n, d), dtype=jnp.float32)
        w1 = jax.random.normal(ks[2], (n, d, h), dtype=jnp.float32) * (1.0 / np.sqrt(d))
        b1 = jax.random.normal(ks[3], (n, h), dtype=jnp.float32) * 0.01
        w2 = jax.random.normal(ks[4], (n, h, d), dtype=jnp.float32) * (1.0 / np.sqrt(h))
        b2 = jax.random.normal(ks[5], (n, d), dtype=jnp.float32) * 0.01
        return {'x': x, 'phi': phi, 'ln_g': ln_g, 'ln_b': ln_b, 'w1': w1, 'b1': b1, 'w2': w2, 'b2': b2}
    _L3_ffn_all = _L3_ffn_setup()
    _L3_ffn_in = {k: v for k, v in _L3_ffn_all.items() if k in ('phi', 'ln_g', 'ln_b', 'w1', 'b1', 'w2', 'b2')}
    del _L3_ffn_all
    return {'x': x, 'txt': txt, 'L0_tok_w': _L0_tok_in['w'], 'L0_tok_b': _L0_tok_in['b'], 'L0_attn_Wq': _L0_attn_in['Wq'], 'L0_attn_Wk': _L0_attn_in['Wk'], 'L0_attn_Wv': _L0_attn_in['Wv'], 'L0_ffn_router_w': _L0_ffn_in['router_w'], 'L0_ffn_Wg': _L0_ffn_in['Wg'], 'L0_ffn_Wu': _L0_ffn_in['Wu'], 'L0_ffn_Wd': _L0_ffn_in['Wd'], 'L1_attn_Wqkv': _L1_attn_in['Wqkv'], 'L1_attn_Wproj': _L1_attn_in['Wproj'], 'L1_attn_bproj': _L1_attn_in['bproj'], 'L1_attn_s_q': _L1_attn_in['s_q'], 'L1_attn_s_k': _L1_attn_in['s_k'], 'L1_attn_s_v': _L1_attn_in['s_v'], 'L1_attn_s_attn': _L1_attn_in['s_attn'], 'L1_attn_s_after': _L1_attn_in['s_after'], 'L1_ffn_Wr': _L1_ffn_in['Wr'], 'L1_ffn_W1': _L1_ffn_in['W1'], 'L1_ffn_b1': _L1_ffn_in['b1'], 'L1_ffn_W2': _L1_ffn_in['W2'], 'L1_ffn_b2': _L1_ffn_in['b2'], 'L2_attn_W_qkv': _L2_attn_in['W_qkv'], 'L2_attn_W_proj': _L2_attn_in['W_proj'], 'L2_attn_b_proj': _L2_attn_in['b_proj'], 'L2_attn_gamma': _L2_attn_in['gamma'], 'L2_attn_beta': _L2_attn_in['beta'], 'L2_attn_random_features': _L2_attn_in['random_features'], 'L2_ffn_weights_in': _L2_ffn_in['weights_in'], 'L2_ffn_weights_out': _L2_ffn_in['weights_out'], 'L3_attn_w_qkv': _L3_attn_in['w_qkv'], 'L3_attn_w_proj': _L3_attn_in['w_proj'], 'L3_attn_b_proj': _L3_attn_in['b_proj'], 'L3_ffn_phi': _L3_ffn_in['phi'], 'L3_ffn_ln_g': _L3_ffn_in['ln_g'], 'L3_ffn_ln_b': _L3_ffn_in['ln_b'], 'L3_ffn_w1': _L3_ffn_in['w1'], 'L3_ffn_b1': _L3_ffn_in['b1'], 'L3_ffn_w2': _L3_ffn_in['w2'], 'L3_ffn_b2': _L3_ffn_in['b2']}

def reference(x, txt, L0_tok_w, L0_tok_b, L0_attn_Wq, L0_attn_Wk, L0_attn_Wv, L0_ffn_router_w, L0_ffn_Wg, L0_ffn_Wu, L0_ffn_Wd, L1_attn_Wqkv, L1_attn_Wproj, L1_attn_bproj, L1_attn_s_q, L1_attn_s_k, L1_attn_s_v, L1_attn_s_attn, L1_attn_s_after, L1_ffn_Wr, L1_ffn_W1, L1_ffn_b1, L1_ffn_W2, L1_ffn_b2, L2_attn_W_qkv, L2_attn_W_proj, L2_attn_b_proj, L2_attn_gamma, L2_attn_beta, L2_attn_random_features, L2_ffn_weights_in, L2_ffn_weights_out, L3_attn_w_qkv, L3_attn_w_proj, L3_attn_b_proj, L3_ffn_phi, L3_ffn_ln_g, L3_ffn_ln_b, L3_ffn_w1, L3_ffn_b1, L3_ffn_w2, L3_ffn_b2):
    import jax
    import jax.numpy as jnp

    def _L0_tok_ref(x, w, b):
        import jax, jax.numpy as jnp
        import numpy as np
        C, H, W = (1, 256, 256)
        P = 32
        D_TOK = 192
        B = 32
        D_PATCH = C * P * P

        def _patchify(x):
            Bx = x.shape[0]
            x = x.reshape(Bx, C, H // P, P, W // P, P)
            x = x.transpose(0, 2, 4, 1, 3, 5)
            return x.reshape(Bx, H // P * (W // P), D_PATCH)
        patches = _patchify(x)
        return jnp.einsum('bld,td->blt', patches, w) + b

    def _L0_attn_ref(x, Wq, Wk, Wv):
        import jax, jax.numpy as jnp
        import numpy as np
        B, N, D_IN, D_EMB = (8, 512, 192, 192)
        dim_sqrt = jnp.asarray(D_EMB ** 0.5, x.dtype)
        q = jnp.einsum('bnd,ed->bne', x, Wq)
        k = jnp.einsum('bnd,ed->bne', x, Wk)
        v = jnp.einsum('bnd,ed->bne', x, Wv)
        scores = jnp.einsum('bne,bme->bnm', q, k)
        attn = jax.nn.softmax(scores, axis=-1) / dim_sqrt
        out = jnp.einsum('bnm,bme->bne', attn, v)
        return out

    def _L0_ffn_ref(x, router_w, Wg, Wu, Wd):
        import jax, jax.numpy as jnp
        import numpy as np
        B, T, D, E, K = (4, 512, 192, 8, 2)
        H = 4 * D
        Bv, Tv, Dv = x.shape
        N = Bv * Tv
        xf = x.reshape(N, Dv)
        logits = (xf @ router_w.T).astype(jnp.float32)
        top_logits, top_idx = jax.lax.top_k(logits, K)
        top_w = jax.nn.softmax(top_logits, axis=-1).astype(x.dtype)
        out = jnp.zeros_like(xf)
        for e in range(E):
            w_e = jnp.sum(top_w * (top_idx == e), axis=-1)
            h = jax.nn.silu(xf @ Wg[e].T) * (xf @ Wu[e].T)
            out = out + h @ Wd[e].T * w_e[:, None]
        return out.reshape(Bv, Tv, Dv)

    def _L1_attn_ref(x, Wqkv, Wproj, bproj, s_q, s_k, s_v, s_attn, s_after):
        import jax, jax.numpy as jnp
        import numpy as np
        LEVEL = 8
        NUM_HEADS = 12
        QN_SYM = float(-(LEVEL // 2))
        QP_SYM = float(LEVEL // 2 - 1)
        QN_ASYM = 0.0
        QP_ASYM = float(LEVEL - 1)

        def fake_quant(x, s, qn, qp):
            xc = jnp.clip(x / s, qn, qp)
            xr = xc + jax.lax.stop_gradient(jnp.round(xc) - xc)
            return s * xr
        B, N, C = x.shape
        H = NUM_HEADS
        D = C // H
        scale = D ** (-0.5)
        qkv = jnp.einsum('bnc,dc->bnd', x, Wqkv).reshape(B, N, 3, H, D).transpose(2, 0, 3, 1, 4)
        q, k, v = (qkv[0], qkv[1], qkv[2])
        q = fake_quant(q, s_q, QN_SYM, QP_SYM) * scale
        k = fake_quant(k, s_k, QN_SYM, QP_SYM)
        v = fake_quant(v, s_v, QN_SYM, QP_SYM)
        attn = jnp.einsum('bhnd,bhmd->bhnm', q, k)
        attn = fake_quant(attn / N, s_attn, QN_ASYM, QP_ASYM)
        out = jnp.einsum('bhnm,bhmd->bhnd', attn, v)
        out = fake_quant(out, s_after, QN_SYM, QP_SYM)
        out = out.transpose(0, 2, 1, 3).reshape(B, N, C)
        return out @ Wproj.T + bproj

    def _L1_ffn_ref(x, Wr, W1, b1, W2, b2):
        import jax, jax.numpy as jnp
        import numpy as np
        D_MODEL = 192
        N_EXPERTS = 16
        TOP_K = 2
        D_FF = 4 * D_MODEL
        B, L = (4, 512)
        logits = jnp.einsum('bld,ed->ble', x, Wr)
        probs = jax.nn.softmax(logits, axis=-1)
        top_p, top_idx = jax.lax.top_k(probs, TOP_K)
        gating = jnp.sum(jax.nn.one_hot(top_idx, N_EXPERTS, dtype=probs.dtype) * top_p[..., None], axis=-2)
        gate_e = jnp.moveaxis(gating, -1, 0)

        def step(y, params):
            W1e, b1e, W2e, b2e, ge = params
            h = jax.nn.gelu(jnp.einsum('bld,df->blf', x, W1e) + b1e, approximate=False)
            out = jnp.einsum('blf,fd->bld', h, W2e) + b2e
            return (y + ge[..., None] * out, None)
        y0 = jnp.zeros_like(x)
        y, _ = jax.lax.scan(step, y0, (W1, b1, W2, b2, gate_e))
        return x + y

    def _L2_attn_ref(x, W_qkv, W_proj, b_proj, gamma, beta, random_features):
        import jax, jax.numpy as jnp
        import numpy as np
        import math
        B, N, C = (8, 1024, 192)
        H = 12
        DH = C // H
        M = 64
        LN_EPS = 1e-05

        def _phi(t, random_features):
            norm_sq = 0.5 * jnp.sum(t * t, axis=-1, keepdims=True)
            proj = jnp.einsum('bhnd,md->bhnm', t, random_features)
            return jnp.exp(proj - norm_sq) * (1.0 / math.sqrt(M))
        b, n, c = x.shape
        qkv = (x @ W_qkv).reshape(b, n, 3, H, DH)
        qkv = jnp.transpose(qkv, (2, 0, 3, 1, 4))
        q, k, v = (qkv[0], qkv[1], qkv[2])
        q_p = _phi(q, random_features)
        k_p = _phi(k, random_features)
        kv = jnp.einsum('bhnm,bhnd->bhmd', k_p, v)
        out = jnp.einsum('bhnm,bhmd->bhnd', q_p, kv)
        k_sum = jnp.sum(k_p, axis=2)
        normalizer = jnp.einsum('bhnm,bhm->bhn', q_p, k_sum)[..., None]
        out = out / (normalizer + 1e-06)
        x_attn = jnp.transpose(out, (0, 2, 1, 3)).reshape(b, n, c)
        x_attn = x_attn @ W_proj + b_proj
        y = x + x_attn
        mu = jnp.mean(y, axis=-1, keepdims=True)
        var = jnp.mean(jnp.square(y - mu), axis=-1, keepdims=True)
        return (y - mu) * jax.lax.rsqrt(var + LN_EPS) * gamma + beta

    def _L2_ffn_ref(inputs, weights_in, weights_out):
        import jax, jax.numpy as jnp
        import numpy as np
        DEPTH = 11

        def _fff_forward(inputs, weights_in, weights_out, depth=DEPTH):
            B, S, _ = inputs.shape
            n_nodes = weights_in.shape[0]
            max_index = n_nodes - 1
            all_logits = jnp.einsum('bsd,nd->bsn', inputs, weights_in)

            def step(prev_idx, _):
                sel = jnp.clip(prev_idx, 0, max_index)
                logits = jnp.take_along_axis(all_logits, sel[..., None], axis=-1)[..., 0]
                new_idx = jnp.clip(2 * sel + 1 + (logits > 0).astype(sel.dtype), 0, max_index)
                return (new_idx, (logits, new_idx))
            idx0 = jnp.zeros((B, S), dtype=jnp.int32)
            _, (logits_seq, idx_seq) = jax.lax.scan(step, idx0, None, length=depth - 1)
            logits = jnp.concatenate([jnp.zeros((1, B, S), all_logits.dtype), logits_seq], axis=0)
            node_idx = jnp.concatenate([idx0[None], idx_seq], axis=0)
            act = jax.nn.gelu(logits, approximate=False)
            onehot = jax.nn.one_hot(node_idx, n_nodes, dtype=act.dtype)
            coeff = jnp.einsum('dbs,dbsn->bsn', act, onehot)
            return jnp.einsum('bsn,nd->bsd', coeff, weights_out)
        return _fff_forward(inputs, weights_in, weights_out)

    def _L3_attn_ref(x, w_qkv, w_proj, b_proj):
        import jax, jax.numpy as jnp
        import numpy as np
        DIM = 192
        NUM_HEADS = 12
        HEAD_DIM = DIM // NUM_HEADS
        SCALE = HEAD_DIM ** (-0.5)
        B, N, C = x.shape
        H, D = (NUM_HEADS, HEAD_DIM)
        qkv = jnp.einsum('bnc,oc->bno', x, w_qkv)
        qkv = qkv.reshape(B, N, 3, H, D).transpose(2, 0, 3, 1, 4)
        q, k, v = (qkv[0], qkv[1], qkv[2])
        attn = jnp.einsum('bhnd,bhmd->bhnm', q, k) * jnp.float32(SCALE)
        attn = jax.nn.softmax(attn, axis=-1)
        out = jnp.einsum('bhnm,bhmd->bhnd', attn, v)
        out = out.transpose(0, 2, 1, 3).reshape(B, N, C)
        out = jnp.einsum('bnc,oc->bno', out, w_proj) + b_proj
        return out

    def _L3_ffn_ref(x, phi, ln_g, ln_b, w1, b1, w2, b2):
        import jax, jax.numpy as jnp
        import numpy as np
        EPS_NORM = 1e-06
        EPS_LN = 1e-05

        def _layernorm(x, g, b):
            mu = jnp.mean(x, axis=-1, keepdims=True)
            var = jnp.mean(jnp.square(x - mu), axis=-1, keepdims=True)
            return (x - mu) * jax.lax.rsqrt(var + EPS_LN) * g + b
        phi_n = phi * jax.lax.rsqrt(jnp.sum(jnp.square(phi), axis=0, keepdims=True) + EPS_NORM)
        bsz, m, d = x.shape
        n, p, _ = phi_n.shape
        logits = jnp.einsum('bmd,npd->bmnp', x, phi_n)
        D = jax.nn.softmax(logits, axis=1)
        C = jax.nn.softmax(logits.reshape(bsz, m, n * p), axis=-1)
        Xs = jnp.einsum('bmd,bmnp->bnpd', x, D)
        hdn = _layernorm(Xs, ln_g[:, None, :], ln_b[:, None, :])
        hdn = jnp.einsum('bnpd,ndh->bnph', hdn, w1) + b1[:, None, :]
        hdn = jax.nn.gelu(hdn, approximate=False)
        Ys = jnp.einsum('bnph,nhd->bnpd', hdn, w2) + b2[:, None, :]
        Ys = Ys.reshape(bsz, n * p, d)
        Y = jnp.einsum('bsd,bms->bmd', Ys, C)
        return Y
    h = _L0_tok_ref(x, L0_tok_w, L0_tok_b)
    h = jnp.concatenate([h, txt], axis=1)
    h = h + _L0_attn_ref(_layernorm(h, axis=-1), L0_attn_Wq, L0_attn_Wk, L0_attn_Wv)
    h = h + _L0_ffn_ref(_layernorm(h, axis=-1), L0_ffn_router_w, L0_ffn_Wg, L0_ffn_Wu, L0_ffn_Wd)
    h = h + _L1_attn_ref(_layernorm(h, axis=-1), L1_attn_Wqkv, L1_attn_Wproj, L1_attn_bproj, L1_attn_s_q, L1_attn_s_k, L1_attn_s_v, L1_attn_s_attn, L1_attn_s_after)
    h = h + _L1_ffn_ref(_layernorm(h, axis=-1), L1_ffn_Wr, L1_ffn_W1, L1_ffn_b1, L1_ffn_W2, L1_ffn_b2)
    h = h + _L2_attn_ref(_layernorm(h, axis=-1), L2_attn_W_qkv, L2_attn_W_proj, L2_attn_b_proj, L2_attn_gamma, L2_attn_beta, L2_attn_random_features)
    h = h + _L2_ffn_ref(_layernorm(h, axis=-1), L2_ffn_weights_in, L2_ffn_weights_out)
    h = h + _L3_attn_ref(_layernorm(h, axis=-1), L3_attn_w_qkv, L3_attn_w_proj, L3_attn_b_proj)
    h = h + _L3_ffn_ref(_layernorm(h, axis=-1), L3_ffn_phi, L3_ffn_ln_g, L3_ffn_ln_b, L3_ffn_w1, L3_ffn_b1, L3_ffn_w2, L3_ffn_b2)
    return h

_drawn_inputs = setup_inputs


def setup_inputs(seed=0):
    import zlib

    import numpy as np

    out = dict(_drawn_inputs(seed))
    spreads = {'L1_attn_bproj': (0.0, 0.1),
     'L2_attn_b_proj': (0.0, 0.1),
     'L2_attn_gamma': (1.0, 0.2),
     'L2_attn_beta': (0.0, 0.1),
     'L3_ffn_ln_g': (1.0, 0.6),
     'L3_ffn_ln_b': (0.0, 0.8)}
    factors = {'L0_ffn_router_w': 8.0,
     'L0_ffn_Wg': 7.517,
     'L0_ffn_Wu': 8.0,
     'L0_ffn_Wd': 6.182,
     'L1_ffn_b1': 4.54,
     'L1_ffn_b2': 3.351,
     'L3_attn_w_qkv': 5.876,
     'L3_attn_w_proj': 6.453,
     'L3_attn_b_proj': 200.0,
     'L3_ffn_phi': 8.0,
     'L3_ffn_w1': 8.0,
     'L3_ffn_b1': 200.0,
     'L3_ffn_w2': 8.0,
     'L3_ffn_b2': 200.0}
    for name, (base, spread) in spreads.items():
        noise = np.random.default_rng([zlib.crc32(name.encode()), seed]).standard_normal(out[name].shape)
        drawn = base * np.exp(spread * noise) if base else spread * noise
        out[name] = jnp.asarray(drawn.astype(out[name].dtype))
    for name, factor in factors.items():
        out[name] = (out[name] * factor).astype(out[name].dtype)
    return out
```

```python
from contextlib import ExitStack

import numpy as np

import concourse.bass as bass
from concourse import mybir

F32 = mybir.dt.float32
BF16 = mybir.dt.bfloat16
I32 = mybir.dt.int32
ALU = mybir.AluOpType
ACT = mybir.ActivationFunctionType
AXX = mybir.AxisListType.X

B, N, D = 16, 192, 192
H2 = 96
TILES = 2 * B
T = B * N
LANES = 2
TURNS = B // LANES
HEADS, DH = 12, 16
GROUPS = 3
ROUND = 12582912.0
EPS = 1e-5


def ds(start, size):
    return bass.ds(start, size)


class Core:

    def __init__(self, nc, ctx):
        self.nc, self.ctx, self.sems = nc, ctx, []
        self.h = self.sb("h", [H2, TILES, D])
        self.cent = self.sb("cent", [H2, TILES, D])
        self.rstd = self.sb("rstd", [H2, TILES])
        self.ident = self.sb("ident", [128, 128])

    def sb(self, name, shape, dt=F32, ctx=None):
        return (ctx or self.ctx).enter_context(self.nc.sbuf_tensor(name, shape, dt))

    def ps(self, name, shape, ctx, dt=F32):
        return ctx.enter_context(self.nc.psum_tensor(name, shape, dt))

    def sem(self, name):
        s = self.nc.alloc_semaphore(name=name)
        self.sems.append(s)
        return s

    def layer_done(self):
        if self.sems:
            self.nc.clear_and_free_semaphores(self.sems)
            self.nc.all_engine_barrier()
        self.sems = []


def halves(w):
    return w.rearrange("(a p) n -> p a n", p=H2)



def embed(k, patchesT, tok_wT, tok_b, txt):
    nc, h = k.nc, k.h
    PF, PT = 1024, 64
    FC = PF // 128
    with ExitStack() as ctx:
        pat = [k.sb(f"pat{u}", [128, FC, 128], ctx=ctx) for u in range(LANES)]
        w = k.sb("tok_w", [128, FC, D], ctx=ctx)
        bias = k.sb("tok_bias", [1, D], ctx=ctx)
        ones = k.sb("tok_ones", [1, 128], ctx=ctx)
        acc = [k.ps(f"tok_ps{u}", [128, 512], ctx) for u in range(LANES)]
        pat_in, w_in, txt_in = [k.sem(f"pat_in{u}") for u in range(LANES)], k.sem("tokw_in"), k.sem("txt_in")
        consts, embedded, stored = k.sem("tok_consts"), k.sem("embedded"), k.sem("emb_stored")
        turns = B // 2 // LANES
        src = patchesT.rearrange("(c p) t -> p c t", p=128)
        block = ctx.enter_context(nc.Block())

        @block.sync
        def _(sp):
            sp.dma_start(w[:], tok_wT.rearrange("(c p) n -> p c n", p=128)).then_inc(w_in, 16)
            sp.dma_start(bias[:], tok_b).then_inc(w_in, 16)
            with sp.Fori(0, turns) as i:
                for u in range(LANES):
                    sp.wait_ge(embedded, i * LANES + u + 1)
                    sp.dma_start(pat[u][:], src[:, :, ds((i * LANES + u) * 128, 128)]).then_inc(pat_in[u], 16)

        @block.scalar
        def _(act):
            tx = txt.rearrange("b t d -> t b d")
            hv = h[:, :, :].rearrange("p (b a) d -> p b a d", a=2)
            act.dma_start(hv[PT:H2, :, 0, :], tx[0:H2 - PT]).then_inc(txt_in, 16)
            act.dma_start(hv[:, :, 1, :], tx[H2 - PT:128]).then_inc(txt_in, 16)
            act.wait_ge(txt_in, 32)

        @block.gpsimd
        def _(pool):
            nc.gpsimd.memset(k.ident[:], 0.0).then_inc(consts, 1)
            pool.wait_ge(consts, 1)
            nc.gpsimd.affine_select(out=k.ident[:], in_=k.ident[:], compare_op=ALU.not_equal, fill=1.0,
                                    base=0, pattern=[[-1, 128]], channel_multiplier=1).then_inc(consts, 1)
            pool.wait_ge(consts, 2)
            nc.gpsimd.memset(ones[:], 1.0).then_inc(consts, 1)

        @block.tensor
        def _(pe):
            pe.wait_ge(w_in, 32)
            pe.wait_ge(consts, 3)
            with pe.Fori(0, turns) as i:
                for u in range(LANES):
                    pe.wait_ge(pat_in[u], i * 16 + 16)
                    pe.wait_ge(stored, i * LANES + u + 1)
                    pe.matmul(acc[u][:, 0:D], ones[:], bias[:], start=True, stop=False)
                    for c in range(FC):
                        last = pe.matmul(acc[u][:, 0:D], pat[u][:, c, :], w[:, c, :], start=False, stop=(c == FC - 1))
                    last.then_inc(embedded, 1)

        @block.vector
        def _(dve):
            nc.vector.memset(k.rstd[:, 0:1], 0.0).then_inc(stored, LANES)
            nc.vector.memset(k.rstd[:, 1:2], 0.0).then_inc(embedded, LANES)
            with dve.Fori(0, turns) as i:
                for u in range(LANES):
                    dve.wait_ge(embedded, LANES + i * LANES + u + 1)
                    t = (i * LANES + u) * 4
                    nc.vector.tensor_copy(h[0:PT, ds(t, 1), :], acc[u][0:PT, None, 0:D])
                    nc.vector.tensor_copy(h[0:PT, ds(t + 2, 1), :], acc[u][PT:2 * PT, None, 0:D]).then_inc(stored, 1)



def center(k, name, src=None, parts=4):
    nc, cent, rstd = k.nc, k.cent, k.rstd
    h = k.h if src is None else src
    with ExitStack() as ctx:
        sq = k.sb(f"{name}_sq", [H2, TILES, D], ctx=ctx)
        total = k.sb(f"{name}_sum", [H2, TILES], ctx=ctx)
        mean = k.sb(f"{name}_mean", [H2, TILES], ctx=ctx)
        var = k.sb(f"{name}_var", [H2, TILES], ctx=ctx)
        std = k.sb(f"{name}_std", [H2, TILES], ctx=ctx)
        summed, meaned, centered, squared = (k.sem(f"{name}_{x}") for x in ("summed", "meaned", "centered", "squared"))
        varied, rooted = k.sem(f"{name}_varied"), k.sem(f"{name}_rooted")
        n = TILES // parts
        block = ctx.enter_context(nc.Block())

        @block.vector
        def _(dve):
            for p in range(parts):
                at = slice(p * n, p * n + n)
                nc.vector.tensor_reduce(total[:, at], h[:, at, :], AXX, ALU.add).then_inc(summed, 1)
                dve.wait_ge(summed, p + 1)
                nc.vector.tensor_scalar(mean[:, at], total[:, at], 1.0 / D, None, ALU.mult).then_inc(meaned, 1)
                dve.wait_ge(meaned, p + 1)
                nc.vector.tensor_tensor(cent[:, at, :], h[:, at, :],
                                        mean[:, at].unsqueeze(2).broadcast_to([H2, n, D]),
                                        ALU.subtract).then_inc(centered, 1)
            for p in range(parts):
                at = slice(p * n, p * n + n)
                dve.wait_ge(squared, p + 1)
                nc.vector.tensor_reduce(total[:, at], sq[:, at, :], AXX, ALU.add).then_inc(summed, 1)
            dve.wait_ge(summed, 2 * parts)
            nc.vector.tensor_scalar(var[:], total[:], 1.0 / D, EPS, ALU.mult, ALU.add).then_inc(varied, 1)
            dve.wait_ge(rooted, 1)
            nc.vector.reciprocal(rstd[:], std[:])

        @block.scalar
        def _(act):
            for p in range(parts):
                at = slice(p * n, p * n + n)
                act.wait_ge(centered, p + 1)
                nc.scalar.activation(sq[:, at, :], cent[:, at, :], ACT.Square).then_inc(squared, 1)
            act.wait_ge(varied, 1)
            nc.scalar.activation(std[:], var[:], ACT.Sqrt).then_inc(rooted, 1)



def normed_rows(k, out, i, u):
    b2 = (i * LANES + u) * 2
    return k.nc.vector.tensor_tensor(out[:], k.cent[:, ds(b2, 2), :],
                                     k.rstd[:, ds(b2, 2)].unsqueeze(2).broadcast_to([H2, 2, D]), ALU.mult)


def turn(pe, k, out, rows):
    for dh in range(2):
        for th in range(2):
            last = pe.transpose(out[:, dh * N + th * H2:dh * N + th * H2 + H2],
                                rows[:, th, dh * H2:dh * H2 + H2], k.ident[0:H2, 0:H2])
    return last


def split2(x):
    return x.rearrange("p (a n) -> p a n", a=2)


def attention0(k, WqT, WkT, WvT):
    nc, h = k.nc, k.h
    with ExitStack() as ctx:
        wq, wk, wv = (k.sb(f"a0_w{x}", [H2, 2, D], ctx=ctx) for x in "qkv")

        def lanes(name, shape, dt=F32):
            return [k.sb(f"a0_{name}{u}", shape, dt, ctx=ctx) for u in range(LANES)]

        rows, xT, qT, kT, v = (lanes(x, [H2, 2, D]) for x in ("rows", "xT", "qT", "kT", "v"))
        prob, probT = (lanes(x, [H2, 2, N]) for x in ("prob", "probT"))
        nmax, psum_, den, rden = (lanes(x, [H2, 2]) for x in ("nmax", "psum", "den", "rden"))
        bank = [[k.ps(f"a0_bank{u}{j}", [128, 512], ctx) for j in range(4)] for u in range(LANES)]
        S = {x: k.sem(f"a0_{x}") for x in (
            "w_in", "rows", "turned", "xT", "qkv", "qT", "kT", "v", "scores", "nmax", "prob", "probs_turned",
            "probT", "out", "den", "rden", "added")}
        block = ctx.enter_context(nc.Block())

        def view(u, j):
            return split2(bank[u][j][0:H2, 0:2 * D])

        @block.sync
        def _(sp):
            for w, src in ((wq, WqT), (wk, WkT), (wv, WvT)):
                sp.dma_start(w[:], halves(src)).then_inc(S["w_in"], 16)

        @block.tensor
        def _(pe):
            pe.wait_ge(S["w_in"], 48)
            with pe.Fori(0, TURNS) as i:
                for u in range(LANES):
                    pe.wait_ge(S["rows"], i * LANES + u + 1)
                    turn(pe, k, bank[u][0][0:H2], rows[u]).then_inc(S["turned"], 1)
                for u in range(LANES):
                    pe.wait_ge(S["xT"], i * LANES + u + 1)
                    for j, w in ((1, wq), (2, wk)):
                        for e in range(2):
                            for d in range(2):
                                pe.matmul(view(u, j)[:, e, :], w[:, d, e * H2:e * H2 + H2], xT[u][:, d, :],
                                          start=(d == 0), stop=(d == 1))
                    for t in range(2):
                        for d in range(2):
                            last = pe.matmul(view(u, 3)[:, t, :], xT[u][:, d, t * H2:t * H2 + H2], wv[:, d, :],
                                             start=(d == 0), stop=(d == 1))
                    last.then_inc(S["qkv"], 1)
                for u in range(LANES):
                    pe.wait_ge(S["qT"], i * LANES + u + 1)
                    pe.wait_ge(S["kT"], i * LANES + u + 1)
                    for t in range(2):
                        for e in range(2):
                            last = pe.matmul(view(u, 0)[:, t, :], qT[u][:, e, t * H2:t * H2 + H2], kT[u][:, e, :],
                                             start=(e == 0), stop=(e == 1))
                    last.then_inc(S["scores"], 1)
                for u in range(LANES):
                    pe.wait_ge(S["prob"], i * LANES + u + 1)
                    turn(pe, k, bank[u][1][0:H2], prob[u]).then_inc(S["probs_turned"], 1)
                for u in range(LANES):
                    pe.wait_ge(S["probT"], i * LANES + u + 1)
                    pe.wait_ge(S["v"], i * LANES + u + 1)
                    for t in range(2):
                        for m in range(2):
                            last = pe.matmul(view(u, 2)[:, t, :], probT[u][:, m, t * H2:t * H2 + H2], v[u][:, m, :],
                                             start=(m == 0), stop=(m == 1))
                    last.then_inc(S["out"], 1)

        @block.scalar
        def _(act):
            with act.Fori(0, TURNS) as i:
                for u in range(LANES):
                    act.wait_ge(S["turned"], i * LANES + u + 1)
                    nc.scalar.activation(xT[u][:], view(u, 0), ACT.Copy).then_inc(S["xT"], 1)
                for u in range(LANES):
                    act.wait_ge(S["qkv"], i * LANES + u + 1)
                    nc.scalar.activation(qT[u][:], view(u, 1), ACT.Copy).then_inc(S["qT"], 1)
                    nc.scalar.activation(v[u][:], view(u, 3), ACT.Copy).then_inc(S["v"], 1)
                for u in range(LANES):
                    act.wait_ge(S["nmax"], i * LANES + u + 1)
                    for t in range(2):
                        last = nc.scalar.activation(prob[u][:, t, :], view(u, 0)[:, t, :], ACT.Exp,
                                                    bias=nmax[u][:, t:t + 1], accum_out=psum_[u][:, t:t + 1])
                    last.then_inc(S["prob"], 1)

        @block.vector
        def _(dve):
            with dve.Fori(0, TURNS) as i:
                for u in range(LANES):
                    normed_rows(k, rows[u], i, u).then_inc(S["rows"], 1)
                for u in range(LANES):
                    dve.wait_ge(S["qkv"], i * LANES + u + 1)
                    nc.vector.tensor_copy(kT[u][:], view(u, 2)).then_inc(S["kT"], 1)
                for u in range(LANES):
                    dve.wait_ge(S["scores"], i * LANES + u + 1)
                    nc.vector.tensor_reduce(nmax[u][:], view(u, 0), AXX, ALU.max, negate=True).then_inc(S["nmax"], 1)
                for u in range(LANES):
                    dve.wait_ge(S["probs_turned"], i * LANES + u + 1)
                    nc.vector.tensor_copy(probT[u][:], view(u, 1)).then_inc(S["probT"], 1)
                    nc.vector.tensor_scalar(den[u][:], psum_[u][:], float(D) ** 0.5, None, ALU.mult).then_inc(S["den"], 1)
                    dve.wait_ge(S["den"], i * LANES + u + 1)
                    nc.vector.reciprocal(rden[u][:], den[u][:]).then_inc(S["rden"], 1)
                for u in range(LANES):
                    dve.wait_ge(S["out"], i * LANES + u + 1)
                    dve.wait_ge(S["rden"], i * LANES + u + 1)
                    t0 = (i * LANES + u) * 2
                    for t in range(2):
                        nc.vector.scalar_tensor_tensor(out=h[:, ds(t0 + t, 1), :], in0=view(u, 2)[:, t:t + 1, :],
                                                       scalar=rden[u][:, t:t + 1], in1=h[:, ds(t0 + t, 1), :],
                                                       op0=ALU.mult, op1=ALU.add)



FF = 4 * D
FC = FF // 128
BLOCK = 2 * N
BLOCKS = T // BLOCK
BT = BLOCK // H2


def norm_and_score(k, name, xnT, routerT, logits, E, keep):
    nc, h = k.nc, k.h
    with ExitStack() as ctx:
        w = k.sb(f"{name}_router", [H2, 2, E], ctx=ctx)
        rows = [k.sb(f"{name}_rows{u}", [H2, 2, D], ctx=ctx) for u in range(LANES)]
        xT = [k.sb(f"{name}_xT{u}", [H2, 2, D], ctx=ctx) for u in range(LANES)]
        pT = [k.ps(f"{name}_pT{u}", [128, 512], ctx) for u in range(LANES)]
        pL = [k.ps(f"{name}_pL{u}", [128, 512], ctx) for u in range(LANES)]
        w_in, rowed, turned, copied, kept, scored, logged = (
            k.sem(f"{name}_{x}") for x in ("w_in", "rowed", "turned", "copied", "kept", "scored", "logged"))
        block = ctx.enter_context(nc.Block())

        @block.sync
        def _(sp):
            sp.dma_start(w[:], halves(routerT)).then_inc(w_in, 16)

        @block.vector
        def _(dve):
            with dve.Fori(0, TURNS) as i:
                for u in range(LANES):
                    normed_rows(k, rows[u], i, u).then_inc(rowed, 1)
                    if keep:
                        dve.wait_ge(rowed, i * LANES + u + 1)
                        hb = h[:, ds((i * LANES + u) * 2, 2), :]
                        nc.vector.tensor_tensor(hb, hb, rows[u][:], ALU.add)
                for u in range(LANES):
                    dve.wait_ge(scored, i * LANES + u + 1)
                    nc.vector.tensor_copy(logits[:, ds((i * LANES + u) * 2, 2), :],
                                          split2(pL[u][0:H2, 0:2 * E])).then_inc(logged, 1)

        @block.tensor
        def _(pe):
            pe.wait_ge(w_in, 16)
            with pe.Fori(0, TURNS) as i:
                for u in range(LANES):
                    pe.wait_ge(rowed, i * LANES + u + 1)
                    turn(pe, k, pT[u][0:H2], rows[u]).then_inc(turned, 1)
                for u in range(LANES):
                    pe.wait_ge(copied, i * LANES + u + 1)
                    for t in range(2):
                        for d in range(2):
                            last = pe.matmul(pL[u][0:H2, t * E:t * E + E], xT[u][:, d, t * H2:t * H2 + H2],
                                             w[:, d, :], start=(d == 0), stop=(d == 1))
                    last.then_inc(scored, 1)

        @block.scalar
        def _(act):
            with act.Fori(0, TURNS) as i:
                for u in range(LANES):
                    act.wait_ge(turned, i * LANES + u + 1)
                    if xnT is not None:
                        act.wait_ge(kept, i * LANES + u + 1)
                    nc.scalar.activation(xT[u][:], split2(pT[u][0:H2, 0:2 * D]), ACT.Copy).then_inc(copied, 1)

        @block.gpsimd
        def _(pool):
            if xnT is None:
                return
            nc.gpsimd.memset(xT[0][:, 0, 0:1], 0.0).then_inc(kept, LANES)
            with pool.Fori(0, TURNS) as i:
                for u in range(LANES):
                    pool.wait_ge(copied, i * LANES + u + 1)
                    nc.gpsimd.tensor_copy(xnT[:, :, ds((i * LANES + u) * N, N)], xT[u][:]).then_inc(kept, 1)


def route(k, name, logits, gate, E, probs_first):
    nc = k.nc
    with ExitStack() as ctx:
        def big(x, dt=F32):
            return k.sb(f"{name}_{x}", [H2, TILES, E], dt, ctx=ctx)

        iota_i = k.sb(f"{name}_iota_i", [H2, E], I32, ctx=ctx)
        iota = k.sb(f"{name}_iota", [H2, E], ctx=ctx)
        iota_less = k.sb(f"{name}_iota_less", [H2, E], ctx=ctx)
        best = [k.sb(f"{name}_best{r}", [H2, TILES], ctx=ctx) for r in range(2)]
        place = [k.sb(f"{name}_place{r}", [H2, TILES], ctx=ctx) for r in range(2)]
        hot = [big(f"hot{r}") for r in range(2)]
        score, shifted, same, cand, rest, part = (big(x) for x in ("score", "shifted", "same", "cand", "rest", "part"))
        gap, e, den, rden = (k.sb(f"{name}_{x}", [H2, TILES], ctx=ctx) for x in ("gap", "e", "den", "rden"))
        wt = [k.sb(f"{name}_wt{r}", [H2, TILES], ctx=ctx) for r in range(2)]
        step, counted, to_exp, exped = (k.sem(f"{name}_{x}") for x in ("step", "counted", "to_exp", "exped"))
        block = ctx.enter_context(nc.Block())

        def over_experts(x):
            return x[:].unsqueeze(2).broadcast_to([H2, TILES, E])

        def over_tiles(x):
            return x[:].unsqueeze(1).broadcast_to([H2, TILES, E])

        @block.gpsimd
        def _(pool):
            nc.gpsimd.iota(iota_i[:], pattern=[[1, E]], base=0, channel_multiplier=0).then_inc(counted, 1)

        @block.scalar
        def _(act):
            act.wait_ge(to_exp, 1)
            if probs_first:
                nc.scalar.activation(cand[:], shifted[:], ACT.Exp).then_inc(exped, 1)
            else:
                nc.scalar.activation(e[:], gap[:], ACT.Exp).then_inc(exped, 1)

        @block.vector
        def _(dve):
            done = [0]

            def link(ins):
                done[0] += 1
                ins.then_inc(step, 1)
                dve.wait_ge(step, done[0])

            dve.wait_ge(counted, 1)
            link(nc.vector.tensor_copy(iota[:], iota_i[:]))
            link(nc.vector.tensor_scalar(iota_less[:], iota[:], float(E), None, ALU.subtract))
            x = logits
            if probs_first:
                link(nc.vector.tensor_reduce(den[:], logits[:], AXX, ALU.max))
                link(nc.vector.tensor_tensor(shifted[:], logits[:], over_experts(den), ALU.subtract))
                nc.vector.memset(place[0][:], 0.0).then_inc(to_exp, 1)
                dve.wait_ge(exped, 1)
                link(nc.vector.tensor_reduce(e[:], cand[:], AXX, ALU.add))
                link(nc.vector.reciprocal(rden[:], e[:]))
                link(nc.vector.tensor_tensor(score[:], cand[:], over_experts(rden), ALU.mult))
                x = score
            for r in range(2):
                link(nc.vector.tensor_reduce(best[r][:], x[:], AXX, ALU.max))
                link(nc.vector.tensor_tensor(same[:], x[:], over_experts(best[r]), ALU.is_equal))
                link(nc.vector.tensor_tensor(cand[:], same[:], over_tiles(iota_less), ALU.mult))
                link(nc.vector.tensor_reduce(place[r][:], cand[:], AXX, ALU.min))
                link(nc.vector.tensor_tensor(hot[r][:], over_tiles(iota_less), over_experts(place[r]), ALU.is_equal))
                if r == 0:
                    link(nc.vector.scalar_tensor_tensor(out=rest[:], in0=hot[0][:], scalar=-1e30, in1=x[:],
                                                        op0=ALU.mult, op1=ALU.add))
                    x = rest
            if probs_first:
                w1, w2 = best
            else:
                link(nc.vector.tensor_tensor(gap[:], best[1][:], best[0][:], ALU.subtract))
                nc.vector.memset(score[:, 0, 0:1], 0.0).then_inc(to_exp, 1)
                dve.wait_ge(exped, 1)
                link(nc.vector.tensor_scalar(den[:], e[:], 1.0, None, ALU.add))
                link(nc.vector.reciprocal(wt[0][:], den[:]))
                link(nc.vector.tensor_tensor(wt[1][:], wt[0][:], e[:], ALU.mult))
                w1, w2 = wt
            link(nc.vector.tensor_tensor(part[:], hot[1][:], over_experts(w2), ALU.mult))
            link(nc.vector.tensor_tensor(same[:], hot[0][:], over_experts(w1), ALU.mult))
            nc.vector.tensor_tensor(gate[:], same[:], part[:], ALU.add)


def add_expert_biases(k, name, gate, b2, E):
    nc, h = k.nc, k.h
    with ExitStack() as ctx:
        w = k.sb(f"{name}_b2", [E, D], ctx=ctx)
        rows = [k.sb(f"{name}_g{u}", [H2, 2, E], ctx=ctx) for u in range(LANES)]
        gT = [k.sb(f"{name}_gT{u}", [E, N], ctx=ctx) for u in range(LANES)]
        pT = [k.ps(f"{name}_gp{u}", [128, 512], ctx) for u in range(LANES)]
        pO = [k.ps(f"{name}_go{u}", [128, 512], ctx) for u in range(LANES)]
        w_in, rowed, turned, copied, summed = (k.sem(f"{name}_g{x}") for x in ("w_in", "rowed", "turned", "copied", "summed"))
        block = ctx.enter_context(nc.Block())

        @block.sync
        def _(sp):
            sp.dma_start(w[:], b2).then_inc(w_in, 16)

        @block.vector
        def _(dve):
            with dve.Fori(0, TURNS) as i:
                for u in range(LANES):
                    nc.vector.tensor_copy(rows[u][:], gate[:, ds((i * LANES + u) * 2, 2), :]).then_inc(rowed, 1)
                for u in range(LANES):
                    dve.wait_ge(summed, i * LANES + u + 1)
                    hb = h[:, ds((i * LANES + u) * 2, 2), :]
                    nc.vector.tensor_tensor(hb, hb, split2(pO[u][0:H2, 0:2 * D]), ALU.add)

        @block.tensor
        def _(pe):
            pe.wait_ge(w_in, 16)
            with pe.Fori(0, TURNS) as i:
                for u in range(LANES):
                    pe.wait_ge(rowed, i * LANES + u + 1)
                    for t in range(2):
                        last = pe.transpose(pT[u][0:E, t * H2:t * H2 + H2], rows[u][:, t, :], k.ident[0:H2, 0:H2])
                    last.then_inc(turned, 1)
                for u in range(LANES):
                    pe.wait_ge(copied, i * LANES + u + 1)
                    for t in range(2):
                        last = pe.matmul(pO[u][0:H2, t * D:t * D + D], gT[u][:, t * H2:t * H2 + H2], w[:],
                                         start=True, stop=True)
                    last.then_inc(summed, 1)

        @block.scalar
        def _(act):
            with act.Fori(0, TURNS) as i:
                for u in range(LANES):
                    act.wait_ge(turned, i * LANES + u + 1)
                    nc.scalar.activation(gT[u][:], pT[u][0:E, 0:N], ACT.Copy).then_inc(copied, 1)


def experts(k, name, xnT, gate, E, w_in1, w_in2, w_down, b1):
    nc, h = k.nc, k.h
    gated = w_in2 is not None
    with ExitStack() as ctx:
        w1 = [k.sb(f"{name}_w1_{r}", [H2, 2, FF], ctx=ctx) for r in range(2)]
        w2 = [k.sb(f"{name}_w2_{r}", [H2, 2, FF], ctx=ctx) for r in range(2)] if gated else None
        bias = None if gated else [k.sb(f"{name}_b1_{r}", [128, FC], ctx=ctx) for r in range(2)]
        wd = [k.sb(f"{name}_wd_{r}", [128, FC, D], ctx=ctx) for r in range(2)]
        hid = [k.sb(f"{name}_hid{u}", [128, FC, BLOCK], ctx=ctx) for u in range(2)]
        silu = [k.sb(f"{name}_silu{j}", [128, BLOCK], ctx=ctx) for j in range(2)] if gated else None
        pg = [k.ps(f"{name}_pg{j}", [128, 512], ctx) for j in range(2)]
        pu = [k.ps(f"{name}_pu{j}", [128, 512], ctx) for j in range(2)] if gated else None
        po = [k.ps(f"{name}_po{t}", [128, 512], ctx) for t in range(BT)]
        loaded = [k.sem(f"{name}_loaded{r}") for r in range(2)]
        used, lifted, gates, hidden, lowered, added = (
            k.sem(f"{name}_{x}") for x in ("used", "lifted", "gates", "hidden", "lowered", "added"))
        LOADS = 3
        block = ctx.enter_context(nc.Block())

        @block.sync
        def _(sp):
            with sp.Fori(0, E // 2) as i:
                for r in range(2):
                    e = i * 2 + r
                    sp.wait_ge(used, e + 1)
                    sp.dma_start(w1[r][:], w_in1[ds(e, 1)].rearrange("o (a p) n -> p (o a) n", p=H2)).then_inc(loaded[r], 16)
                    if gated:
                        sp.dma_start(w2[r][:], w_in2[ds(e, 1)].rearrange("o (a p) n -> p (o a) n", p=H2)).then_inc(loaded[r], 16)
                    else:
                        sp.dma_start(bias[r][:], b1[ds(e, 1)].rearrange("o p c -> p (o c)")).then_inc(loaded[r], 16)
                    sp.dma_start(wd[r][:], w_down[ds(e, 1)].rearrange("o (c p) n -> p (o c) n", p=128)).then_inc(loaded[r], 16)

        def over_blocks(eng, body):
            with eng.Fori(0, E // 2) as i:
                for r in range(2):
                    with eng.Fori(0, BLOCKS // 2) as b:
                        for u in range(2):
                            body(i * 2 + r, r, b * 2 + u, u, (i, b))

        @block.tensor
        def _(pe):
            with pe.Fori(0, E // 2) as i:
                for r in range(2):
                    with pe.Fori(0, BLOCKS // 2) as b:
                        for u in range(2):
                            pe.wait_ge(loaded[r], (i + 1) * (16 * LOADS))
                            n = (i * 2 + r) * BLOCKS + b * 2 + u
                            for j in range(FC + 1):
                                if j < FC:
                                    pe.wait_ge(hidden, n * FC + j + 1)
                                    for w, p in ((w1, pg), (w2, pu)) if gated else ((w1, pg),):
                                        for d in range(2):
                                            last = pe.matmul(p[j % 2][:, 0:BLOCK], w[r][:, d, j * 128:(j + 1) * 128],
                                                             xnT[:, d, ds((b * 2 + u) * BLOCK, BLOCK)],
                                                             start=(d == 0), stop=(d == 1))
                                    last.then_inc(lifted, 1)
                                if j == 1:
                                    pe.wait_ge(added, n + 1)
                                if j > 0:
                                    pe.wait_ge(hidden, n * FC + j + 2)
                                    for t in range(BT):
                                        last = pe.matmul(po[t][0:H2, 0:D], hid[u][:, j - 1, t * H2:(t + 1) * H2],
                                                         wd[r][:, j - 1, :], start=(j == 1), stop=(j == FC))
                            last.then_inc(lowered, 1)
                    pe.matmul(pg[0][0:32, 0:2], k.ident[:, 0:32], k.ident[:, 0:2], start=True, stop=True).then_inc(used, 1)

        @block.scalar
        def _(act):
            def body(e, r, blk, u, _):
                n = e * BLOCKS + blk
                for j in range(FC):
                    act.wait_ge(lifted, n * FC + j + 1)
                    if gated:
                        nc.scalar.activation(silu[j % 2][:], pg[j % 2][:, 0:BLOCK], ACT.Silu).then_inc(gates, 1)
                    else:
                        nc.scalar.activation(hid[u][:, j, :], pg[j % 2][:, 0:BLOCK], ACT.Gelu,
                                             bias=bias[r][:, j:j + 1]).then_inc(hidden, 1)
            over_blocks(act, body)

        @block.vector
        def _(dve):
            nc.vector.memset(po[0][:, 0:1], 0.0).then_inc(used, 2)
            nc.vector.memset(po[0][:, 1:2], 0.0).then_inc(hidden, 2)
            nc.vector.memset(po[0][:, 2:3], 0.0).then_inc(added, 1)

            def body(e, r, blk, u, _):
                n = e * BLOCKS + blk
                if gated:
                    for j in range(FC):
                        dve.wait_ge(gates, n * FC + j + 1)
                        nc.vector.tensor_tensor(hid[u][:, j, :], silu[j % 2][:], pu[j % 2][:, 0:BLOCK],
                                                ALU.mult).then_inc(hidden, 1)
                dve.wait_ge(lowered, n + 1)
                for t in range(BT):
                    tile = blk * BT + t
                    last = nc.vector.scalar_tensor_tensor(
                        out=h[:, ds(tile, 1), :], in0=po[t][0:H2, None, 0:D], scalar=gate[:, ds(tile, 1), ds(e, 1)],
                        in1=h[:, ds(tile, 1), :], op0=ALU.mult, op1=ALU.add)
                last.then_inc(added, 1)
            over_blocks(dve, body)


def moe(k, name, E, routerT, w_in1, w_in2, w_down, b1, b2):
    with ExitStack() as ctx:
        xnT = k.sb(f"{name}_xnT", [H2, 2, T], ctx=ctx)
        logits = k.sb(f"{name}_logits", [H2, TILES, E], ctx=ctx)
        gate = k.sb(f"{name}_gate", [H2, TILES, E], ctx=ctx)
        norm_and_score(k, name, xnT, routerT, logits, E, keep=b2 is not None)
        route(k, name, logits, gate, E, probs_first=b2 is not None)
        if b2 is not None:
            add_expert_biases(k, name, gate, b2, E)
        experts(k, name, xnT, gate, E, w_in1, w_in2, w_down, b1)



PAD = GROUPS * 128
ROUNDS = 4
HR = HEADS // ROUNDS


def head_rows(x, hd):
    j = hd % 4
    return x[32 * j:32 * j + 32, hd // 4, :]


def project_padded(pe, bank, xT, wqk, wv):
    for g in range(GROUPS):
        for which in range(2):
            c = which * PAD + g * 128
            for d in range(2):
                pe.matmul(bank[:, g, which * N:which * N + N], wqk[:, d, c:c + 128], xT[:, d, :],
                          start=(d == 0), stop=(d == 1))
    for t in range(2):
        for d in range(2):
            last = pe.matmul(bank[0:H2, 3, t * D:t * D + D], xT[:, d, t * H2:t * H2 + H2], wv[:, d, :],
                             start=(d == 0), stop=(d == 1))
    return last


def times_turned(pe, out, turned_rows, w):
    for t in range(2):
        for d in range(2):
            last = pe.matmul(out[:, t, :], turned_rows[:, d, t * H2:t * H2 + H2], w[:, d, :],
                             start=(d == 0), stop=(d == 1))
    return last



def attention1(k, wqk_src, wv_src, wproj_src, bias_src, steps_src):
    nc, h = k.nc, k.h
    LO, HI, TOP = -4.0, 3.0, 7.0
    with ExitStack() as ctx:
        wqk = k.sb("a1_wqk", [H2, 2, 2 * PAD], ctx=ctx)
        wv = k.sb("a1_wv", [H2, 2, D], ctx=ctx)
        wp = k.sb("a1_wp", [H2, 2, D], ctx=ctx)
        bias = k.sb("a1_bias", [H2, D], ctx=ctx)
        s = k.sb("a1_s", [128, 5], ctx=ctx)
        inv = k.sb("a1_inv", [128, 5], ctx=ctx)
        fac = k.sb("a1_fac", [128, 4], ctx=ctx)

        def lanes(name, shape, dt=F32):
            return [k.sb(f"a1_{name}{u}", shape, dt, ctx=ctx) for u in range(LANES)]

        rows, xT = lanes("rows", [H2, 2, D]), lanes("xT", [H2, 2, D])
        qk_s, qk_c = lanes("qk_s", [128, 2 * GROUPS, N]), lanes("qk_c", [128, 2 * GROUPS, N])
        qk = lanes("qk", [128, 2 * GROUPS, N], BF16)
        v_s, v_c = lanes("v_s", [H2, 2, D]), lanes("v_c", [H2, 2, D])
        v = lanes("v", [H2, 2, D], BF16)
        at_s, at_c = lanes("at_s", [H2, HR, 2 * N]), lanes("at_c", [H2, HR, 2 * N])
        at = lanes("at", [H2, HR, 2 * N], BF16)
        o_s, o_c, o = lanes("o_s", [H2, 2, D]), lanes("o_c", [H2, 2, D]), lanes("o", [H2, 2, D])
        oT = lanes("oT", [H2, 2, D])
        bank = [k.ps(f"a1_bank{u}", [128, 4, 512], ctx) for u in range(LANES)]
        S = {x: k.sem(f"a1_{x}") for x in (
            "loaded", "consts", "biased", "rows", "turned", "xT", "qkv", "scaled", "clipped", "qkv_ready", "scores",
            "at_scaled", "at_clipped", "at_ready", "out", "o_scaled", "o_clipped", "o_ready", "o_turned",
            "oT", "projected")}
        block = ctx.enter_context(nc.Block())

        def both(u, j):
            return split2(bank[u][0:H2, j, 0:2 * D])

        @block.sync
        def _(sp):
            sp.dma_start(wqk[:], halves(wqk_src)).then_inc(S["loaded"], 16)
            sp.dma_start(wv[:], halves(wv_src)).then_inc(S["loaded"], 16)
            sp.dma_start(wp[:], halves(wproj_src)).then_inc(S["loaded"], 16)
            sp.dma_start(bias[:], bias_src.broadcast_to([H2, D])).then_inc(S["loaded"], 16)
            sp.dma_start(s[:], steps_src.broadcast_to([128, 5])).then_inc(S["loaded"], 16)

        @block.gpsimd
        def _(pool):
            pool.wait_ge(S["loaded"], 80)
            nc.gpsimd.tensor_tensor(h[:], h[:], bias[:].unsqueeze(1).broadcast_to([H2, TILES, D]),
                                    ALU.add).then_inc(S["biased"], 1)

        @block.tensor
        def _(pe):
            pe.wait_ge(S["loaded"], 80)
            with pe.Fori(0, TURNS) as i:
                for u in range(LANES):
                    pe.wait_ge(S["rows"], i * LANES + u + 1)
                    turn(pe, k, bank[u][0:H2, 3, :], rows[u]).then_inc(S["turned"], 1)
                for u in range(LANES):
                    pe.wait_ge(S["xT"], i * LANES + u + 1)
                    project_padded(pe, bank[u], xT[u], wqk, wv).then_inc(S["qkv"], 1)
                for r in range(ROUNDS):
                    for u in range(LANES):
                        if r == 0:
                            pe.wait_ge(S["qkv_ready"], i * LANES + u + 1)
                        for n in range(HR):
                            hd = r * HR + n
                            q, kk = (head_rows(qk[u][:, w * GROUPS:(w + 1) * GROUPS, :], hd) for w in range(2))
                            for m in range(2):
                                last = pe.matmul(bank[u][0:H2, n, m * N:m * N + N], kk[:, m * H2:m * H2 + H2], q,
                                                 start=True, stop=True)
                        last.then_inc(S["scores"], 1)
                    for u in range(LANES):
                        pe.wait_ge(S["at_ready"], (i * ROUNDS + r) * LANES + u + 1)
                        for n in range(HR):
                            c = (r * HR + n) * DH
                            for t in range(2):
                                for m in range(2):
                                    last = pe.matmul(bank[u][0:H2, 3, t * D + c:t * D + c + DH],
                                                     at[u][:, n, m * N + t * H2:m * N + t * H2 + H2],
                                                     v[u][:, m, c:c + DH], start=(m == 0), stop=(m == 1))
                        if r == ROUNDS - 1:
                            last.then_inc(S["out"], 1)
                for u in range(LANES):
                    pe.wait_ge(S["o_ready"], i * LANES + u + 1)
                    turn(pe, k, bank[u][0:H2, 0, :], o[u]).then_inc(S["o_turned"], 1)
                for u in range(LANES):
                    pe.wait_ge(S["oT"], i * LANES + u + 1)
                    times_turned(pe, both(u, 1), oT[u], wp).then_inc(S["projected"], 1)

        @block.scalar
        def _(act):
            act.wait_ge(S["consts"], 2)
            with act.Fori(0, TURNS) as i:
                for u in range(LANES):
                    act.wait_ge(S["turned"], i * LANES + u + 1)
                    nc.scalar.activation(xT[u][:], both(u, 3), ACT.Copy).then_inc(S["xT"], 1)
                for u in range(LANES):
                    act.wait_ge(S["qkv"], i * LANES + u + 1)
                    for w in range(2):
                        nc.scalar.activation(qk_s[u][:, w * GROUPS:(w + 1) * GROUPS, :],
                                             bank[u][:, 0:GROUPS, w * N:w * N + N], ACT.Identity, scale=inv[:, w:w + 1])
                    nc.scalar.activation(v_s[u][:], both(u, 3), ACT.Identity, scale=inv[0:H2, 2:3]).then_inc(S["scaled"], 1)
                for r in range(ROUNDS):
                    for u in range(LANES):
                        act.wait_ge(S["scores"], (i * ROUNDS + r) * LANES + u + 1)
                        nc.scalar.activation(at_s[u][:], bank[u][0:H2, 0:HR, 0:2 * N], ACT.Relu,
                                             scale=fac[0:H2, 1:2]).then_inc(S["at_scaled"], 1)
                for u in range(LANES):
                    act.wait_ge(S["out"], i * LANES + u + 1)
                    nc.scalar.activation(o_s[u][:], both(u, 3), ACT.Identity, scale=fac[0:H2, 3:4]).then_inc(S["o_scaled"], 1)
                for u in range(LANES):
                    act.wait_ge(S["o_turned"], i * LANES + u + 1)
                    nc.scalar.activation(oT[u][:], both(u, 0), ACT.Copy).then_inc(S["oT"], 1)

        @block.vector
        def _(dve):
            def rounded(out, x):
                return nc.vector.tensor_scalar(out, x, ROUND, ROUND, ALU.add, ALU.subtract)

            dve.wait_ge(S["loaded"], 80)
            nc.vector.reciprocal(inv[:], s[:]).then_inc(S["consts"], 1)
            nc.vector.tensor_scalar(fac[:, 0:1], s[:, 0:1], s[:, 1:2], DH ** -0.5 / N, ALU.mult, ALU.mult)
            nc.vector.tensor_scalar(fac[:, 2:3], s[:, 3:4], s[:, 2:3], None, ALU.mult).then_inc(S["clipped"], LANES)
            dve.wait_ge(S["consts"], 1)
            dve.wait_ge(S["clipped"], LANES)
            nc.vector.tensor_scalar(fac[:, 1:2], fac[:, 0:1], inv[:, 3:4], None, ALU.mult)
            nc.vector.tensor_scalar(fac[:, 3:4], fac[:, 2:3], inv[:, 4:5], None, ALU.mult).then_inc(S["consts"], 1)
            with dve.Fori(0, TURNS) as i:
                for u in range(LANES):
                    normed_rows(k, rows[u], i, u).then_inc(S["rows"], 1)
                for u in range(LANES):
                    dve.wait_ge(S["scaled"], i * LANES + u + 1)
                    nc.vector.tensor_scalar(qk_c[u][:], qk_s[u][:], LO, HI, ALU.max, ALU.min)
                    nc.vector.tensor_scalar(v_c[u][:], v_s[u][:], LO, HI, ALU.max, ALU.min).then_inc(S["clipped"], 1)
                for u in range(LANES):
                    dve.wait_ge(S["clipped"], LANES + i * LANES + u + 1)
                    rounded(qk[u][:], qk_c[u][:])
                    rounded(v[u][:], v_c[u][:]).then_inc(S["qkv_ready"], 1)
                for r in range(ROUNDS):
                    for u in range(LANES):
                        n = (i * ROUNDS + r) * LANES + u
                        dve.wait_ge(S["at_scaled"], n + 1)
                        nc.vector.tensor_scalar(at_c[u][:], at_s[u][:], TOP, ROUND, ALU.min, ALU.add).then_inc(S["at_clipped"], 1)
                        dve.wait_ge(S["at_clipped"], n + 1)
                        nc.vector.tensor_scalar(at[u][:], at_c[u][:], ROUND, None, ALU.subtract).then_inc(S["at_ready"], 1)
                for u in range(LANES):
                    dve.wait_ge(S["o_scaled"], i * LANES + u + 1)
                    nc.vector.tensor_scalar(o_c[u][:], o_s[u][:], LO, HI, ALU.max, ALU.min).then_inc(S["o_clipped"], 1)
                for u in range(LANES):
                    dve.wait_ge(S["o_clipped"], i * LANES + u + 1)
                    rounded(o[u][:], o_c[u][:]).then_inc(S["o_ready"], 1)
                for u in range(LANES):
                    dve.wait_ge(S["projected"], i * LANES + u + 1)
                    dve.wait_ge(S["biased"], 1)
                    hb = h[:, ds((i * LANES + u) * 2, 2), :]
                    nc.vector.scalar_tensor_tensor(out=hb, in0=both(u, 1), scalar=s[0:H2, 4:5], in1=hb,
                                                   op0=ALU.mult, op1=ALU.add)



VA = DH + 1


def attention3(k, wqk_src, wv_src, wproj_src, bias_src):
    nc, h = k.nc, k.h
    SCALE = DH ** -0.5
    with ExitStack() as ctx:
        wqk = k.sb("a3_wqk", [H2, 2, 2 * PAD], ctx=ctx)
        wv = k.sb("a3_wv", [H2, 2, D], ctx=ctx)
        wp = k.sb("a3_wp", [H2, 2, D], ctx=ctx)
        bias = k.sb("a3_bias", [H2, D], ctx=ctx)

        def lanes(name, shape, dt=F32):
            return [k.sb(f"a3_{name}{u}", shape, dt, ctx=ctx) for u in range(LANES)]

        rows, xT = lanes("rows", [H2, 2, D]), lanes("xT", [H2, 2, D])
        qT, kT = lanes("qT", [128, GROUPS, N]), lanes("kT", [128, GROUPS, N])
        v = lanes("v", [H2, 2, HEADS, VA])
        top = lanes("top", [H2, HR, 2])
        below, prob, probT = (lanes(x, [H2, HR, 2 * N]) for x in ("below", "prob", "probT"))
        rden, o, oT = lanes("rden", [H2, 2, HEADS]), lanes("o", [H2, 2, D]), lanes("oT", [H2, 2, D])
        bank = [k.ps(f"a3_bank{u}", [128, 4, 512], ctx) for u in range(LANES)]
        S = {x: k.sem(f"a3_{x}") for x in (
            "loaded", "biased", "ones", "rows", "turned", "xT", "qkv", "qkv_copied", "scores", "top", "below",
            "prob", "p_turned", "probT", "out", "rden", "o", "o_turned", "oT", "projected")}
        block = ctx.enter_context(nc.Block())

        def both(u, j):
            return split2(bank[u][0:H2, j, 0:2 * D])

        def three(u):
            return bank[u][0:H2, 0:HR, 0:2 * N]

        def sums(u):
            return bank[u][0:H2, 3, 0:2 * HEADS * VA].rearrange("p (t h e) -> p t h e", t=2, h=HEADS)

        @block.sync
        def _(sp):
            sp.dma_start(wqk[:], halves(wqk_src)).then_inc(S["loaded"], 16)
            sp.dma_start(wv[:], halves(wv_src)).then_inc(S["loaded"], 16)
            sp.dma_start(wp[:], halves(wproj_src)).then_inc(S["loaded"], 16)
            sp.dma_start(bias[:], bias_src.broadcast_to([H2, D])).then_inc(S["loaded"], 16)

        @block.gpsimd
        def _(pool):
            for u in range(LANES):
                nc.gpsimd.memset(v[u][:], 1.0).then_inc(S["ones"], 1)
            pool.wait_ge(S["loaded"], 64)
            nc.gpsimd.tensor_tensor(h[:], h[:], bias[:].unsqueeze(1).broadcast_to([H2, TILES, D]),
                                    ALU.add).then_inc(S["biased"], 1)

        @block.tensor
        def _(pe):
            pe.wait_ge(S["loaded"], 64)
            with pe.Fori(0, TURNS) as i:
                for u in range(LANES):
                    pe.wait_ge(S["rows"], i * LANES + u + 1)
                    turn(pe, k, bank[u][0:H2, 3, :], rows[u]).then_inc(S["turned"], 1)
                for u in range(LANES):
                    pe.wait_ge(S["xT"], i * LANES + u + 1)
                    project_padded(pe, bank[u], xT[u], wqk, wv).then_inc(S["qkv"], 1)
                for r in range(ROUNDS):
                    for u in range(LANES):
                        if r == 0:
                            pe.wait_ge(S["qkv_copied"], i * LANES + u + 1)
                        for n in range(HR):
                            q, kk = head_rows(qT[u], r * HR + n), head_rows(kT[u], r * HR + n)
                            for t in range(2):
                                last = pe.matmul(bank[u][0:H2, n, t * N:t * N + N], q[:, t * H2:t * H2 + H2], kk,
                                                 start=True, stop=True)
                        last.then_inc(S["scores"], 1)
                    for u in range(LANES):
                        pe.wait_ge(S["prob"], (i * ROUNDS + r) * LANES + u + 1)
                        for n in range(HR):
                            last = turn(pe, k, bank[u][0:H2, n, :], split2(prob[u][:, n, :]))
                        last.then_inc(S["p_turned"], 1)
                    for u in range(LANES):
                        pe.wait_ge(S["probT"], (i * ROUNDS + r) * LANES + u + 1)
                        for n in range(HR):
                            hd = r * HR + n
                            for t in range(2):
                                for m in range(2):
                                    last = pe.matmul(sums(u)[:, t, hd, :],
                                                     probT[u][:, n, m * N + t * H2:m * N + t * H2 + H2],
                                                     v[u][:, m, hd, :], start=(m == 0), stop=(m == 1))
                        if r == ROUNDS - 1:
                            last.then_inc(S["out"], 1)
                for u in range(LANES):
                    pe.wait_ge(S["o"], i * LANES + u + 1)
                    turn(pe, k, bank[u][0:H2, 0, :], o[u]).then_inc(S["o_turned"], 1)
                for u in range(LANES):
                    pe.wait_ge(S["oT"], i * LANES + u + 1)
                    times_turned(pe, both(u, 1), oT[u], wp).then_inc(S["projected"], 1)

        @block.scalar
        def _(act):
            act.wait_ge(S["ones"], LANES)
            with act.Fori(0, TURNS) as i:
                for u in range(LANES):
                    act.wait_ge(S["turned"], i * LANES + u + 1)
                    nc.scalar.activation(xT[u][:], both(u, 3), ACT.Copy).then_inc(S["xT"], 1)
                for u in range(LANES):
                    act.wait_ge(S["qkv"], i * LANES + u + 1)
                    nc.scalar.activation(qT[u][:], bank[u][:, 0:GROUPS, 0:N], ACT.Copy)
                    nc.scalar.activation(kT[u][:], bank[u][:, 0:GROUPS, N:2 * N], ACT.Copy)
                    nc.scalar.activation(v[u][:, :, :, 0:DH], both(u, 3).rearrange("p t (h e) -> p t h e", h=HEADS),
                                         ACT.Copy).then_inc(S["qkv_copied"], 1)
                for r in range(ROUNDS):
                    for u in range(LANES):
                        act.wait_ge(S["below"], (i * ROUNDS + r) * LANES + u + 1)
                        nc.scalar.activation(prob[u][:], below[u][:], ACT.Exp, scale=SCALE).then_inc(S["prob"], 1)
                    for u in range(LANES):
                        act.wait_ge(S["p_turned"], (i * ROUNDS + r) * LANES + u + 1)
                        nc.scalar.activation(probT[u][:], three(u), ACT.Copy).then_inc(S["probT"], 1)
                for u in range(LANES):
                    act.wait_ge(S["o_turned"], i * LANES + u + 1)
                    nc.scalar.activation(oT[u][:], both(u, 0), ACT.Copy).then_inc(S["oT"], 1)

        @block.vector
        def _(dve):
            with dve.Fori(0, TURNS) as i:
                for u in range(LANES):
                    normed_rows(k, rows[u], i, u).then_inc(S["rows"], 1)
                for r in range(ROUNDS):
                    for u in range(LANES):
                        n = (i * ROUNDS + r) * LANES + u
                        dve.wait_ge(S["scores"], n + 1)
                        s4 = three(u).rearrange("p n (t m) -> p n t m", t=2)
                        nc.vector.tensor_reduce(top[u][:], s4, AXX, ALU.max).then_inc(S["top"], 1)
                        dve.wait_ge(S["top"], n + 1)
                        nc.vector.tensor_tensor(below[u][:].rearrange("p n (t m) -> p n t m", t=2), s4,
                                                top[u][:].unsqueeze(3).broadcast_to([H2, HR, 2, N]),
                                                ALU.subtract).then_inc(S["below"], 1)
                for u in range(LANES):
                    dve.wait_ge(S["out"], i * LANES + u + 1)
                    nc.vector.reciprocal(rden[u][:], sums(u)[:, :, :, DH]).then_inc(S["rden"], 1)
                    dve.wait_ge(S["rden"], i * LANES + u + 1)
                    nc.vector.tensor_tensor(o[u][:].rearrange("p t (h e) -> p t h e", h=HEADS),
                                            sums(u)[:, :, :, 0:DH],
                                            rden[u][:].unsqueeze(3).broadcast_to([H2, 2, HEADS, DH]),
                                            ALU.mult).then_inc(S["o"], 1)
                for u in range(LANES):
                    dve.wait_ge(S["projected"], i * LANES + u + 1)
                    dve.wait_ge(S["biased"], 1)
                    hb = h[:, ds((i * LANES + u) * 2, 2), :]
                    nc.vector.tensor_tensor(hb, both(u, 1), hb, ALU.add)



FEATURES = 64
HALF_HEADS = HEADS // 2
PAIRS = HEADS // 2


def attention2(k, wqkv_src, feat_src, wproj_src, bias_src):
    nc, cent = k.nc, k.cent
    EPS_N = 1e-6 * FEATURES
    with ExitStack() as ctx:
        w = k.sb("a2_w", [H2, 2, 3 * D], ctx=ctx)
        wp = k.sb("a2_wp", [H2, 2, D], ctx=ctx)
        bias = k.sb("a2_bias", [H2, D], ctx=ctx)
        feat = k.sb("a2_feat", [H2, HALF_HEADS * FEATURES], ctx=ctx)
        less = k.sb("a2_less", [H2, HALF_HEADS * FEATURES], ctx=ctx)

        def lanes(name, shape, dt=F32):
            return [k.sb(f"a2_{name}{u}", shape, dt, ctx=ctx) for u in range(LANES)]

        rows, xT, qT, kT, q2, k2 = (lanes(x, [H2, 2, D]) for x in ("rows", "xT", "qT", "kT", "q2", "k2"))
        v = lanes("v", [H2, 2, HEADS, VA])
        qp = lanes("qp", [128, PAIRS, N])
        kp = lanes("kp", [H2, 2, HEADS * FEATURES])
        kv = lanes("kv", [128, PAIRS, 2 * VA])
        den, rden = lanes("den", [H2, 2, HEADS]), lanes("rden", [H2, 2, HEADS])
        o, oT, y = lanes("o", [H2, 2, D]), lanes("oT", [H2, 2, D]), lanes("y", [H2, 2, D])
        bank = [k.ps(f"a2_bank{u}", [128, 4, 512], ctx) for u in range(LANES)]
        S = {x: k.sem(f"a2_{x}") for x in (
            "loaded", "preset", "rows", "turned", "xT", "qkv", "copied", "q_feat", "qp", "k_feat", "kp", "kv_sums",
            "kv", "out", "den", "rden", "o", "o_turned", "oT", "projected", "y")}
        block = ctx.enter_context(nc.Block())

        def both(u, j):
            return split2(bank[u][0:H2, j, 0:2 * D])

        def sums(u):
            return bank[u][0:H2, 1, 0:2 * HEADS * VA].rearrange("p (t h e) -> p t h e", t=2, h=HEADS)

        @block.sync
        def _(sp):
            sp.dma_start(w[:], halves(wqkv_src)).then_inc(S["loaded"], 16)
            sp.dma_start(wp[:], halves(wproj_src)).then_inc(S["loaded"], 16)
            sp.dma_start(bias[:], bias_src.broadcast_to([H2, D])).then_inc(S["loaded"], 16)
            sp.dma_start(feat[:], feat_src[0]).then_inc(S["loaded"], 16)
            sp.dma_start(less[:], feat_src[1]).then_inc(S["loaded"], 16)

        @block.gpsimd
        def _(pool):
            for u in range(LANES):
                nc.gpsimd.memset(v[u][:], 1.0).then_inc(S["preset"], 1)
                nc.gpsimd.memset(kv[u][:], 0.0).then_inc(S["preset"], 1)

        @block.tensor
        def _(pe):
            pe.wait_ge(S["loaded"], 80)
            with pe.Fori(0, TURNS) as i:
                for u in range(LANES):
                    pe.wait_ge(S["rows"], i * LANES + u + 1)
                    turn(pe, k, bank[u][0:H2, 0, :], rows[u]).then_inc(S["turned"], 1)
                for u in range(LANES):
                    pe.wait_ge(S["xT"], i * LANES + u + 1)
                    for j in range(2):
                        for e in range(2):
                            for d in range(2):
                                c = j * D + e * H2
                                pe.matmul(both(u, j)[:, e, :], w[:, d, c:c + H2], xT[u][:, d, :],
                                          start=(d == 0), stop=(d == 1))
                    times_turned(pe, both(u, 2), xT[u], w[:, :, 2 * D:3 * D]).then_inc(S["qkv"], 1)
                for u in range(LANES):
                    pe.wait_ge(S["copied"], i * LANES + u + 1)
                    for pair in range(PAIRS):
                        e, c = pair // 3, pair % 3 * 128
                        out = bank[u][:, pair // 2, pair % 2 * N:pair % 2 * N + N]
                        pe.matmul(out, feat[:, c:c + 128], qT[u][:, e, :], start=True, stop=False)
                        last = pe.matmul(out, less[:, c:c + 128], q2[u][:, e, :], start=False, stop=True)
                    last.then_inc(S["q_feat"], 1)
                for u in range(LANES):
                    pe.wait_ge(S["qp"], i * LANES + u + 1)
                    for t in range(2):
                        for e in range(2):
                            out = bank[u][0:H2, 2 * t + e, 0:384]
                            pe.matmul(out, kT[u][:, e, t * H2:t * H2 + H2], feat[:], start=True, stop=False)
                            last = pe.matmul(out, k2[u][:, e, t * H2:t * H2 + H2], less[:], start=False, stop=True)
                    last.then_inc(S["k_feat"], 1)
                for u in range(LANES):
                    pe.wait_ge(S["kp"], i * LANES + u + 1)
                    for pair in range(PAIRS):
                        for m in range(2):
                            last = pe.matmul(bank[u][:, 0, pair * 2 * VA:(pair + 1) * 2 * VA],
                                             kp[u][:, m, pair * 128:pair * 128 + 128],
                                             v[u][:, m, 2 * pair:2 * pair + 2, :].rearrange("p h e -> p (h e)"),
                                             start=(m == 0), stop=(m == 1))
                    last.then_inc(S["kv_sums"], 1)
                for u in range(LANES):
                    pe.wait_ge(S["kv"], i * LANES + u + 1)
                    for t in range(2):
                        for pair in range(PAIRS):
                            c = (t * PAIRS + pair) * 2 * VA
                            last = pe.matmul(bank[u][0:H2, 1, c:c + 2 * VA], qp[u][:, pair, t * H2:t * H2 + H2],
                                             kv[u][:, pair, :], start=True, stop=True)
                    last.then_inc(S["out"], 1)
                for u in range(LANES):
                    pe.wait_ge(S["o"], i * LANES + u + 1)
                    turn(pe, k, bank[u][0:H2, 2, :], o[u]).then_inc(S["o_turned"], 1)
                for u in range(LANES):
                    pe.wait_ge(S["oT"], i * LANES + u + 1)
                    times_turned(pe, both(u, 3), oT[u], wp).then_inc(S["projected"], 1)

        @block.scalar
        def _(act):
            act.wait_ge(S["preset"], 2 * LANES)
            with act.Fori(0, TURNS) as i:
                for u in range(LANES):
                    act.wait_ge(S["turned"], i * LANES + u + 1)
                    nc.scalar.activation(xT[u][:], both(u, 0), ACT.Copy).then_inc(S["xT"], 1)
                for u in range(LANES):
                    act.wait_ge(S["qkv"], i * LANES + u + 1)
                    nc.scalar.activation(qT[u][:], both(u, 0), ACT.Copy)
                    nc.scalar.activation(kT[u][:], both(u, 1), ACT.Copy)
                    nc.scalar.activation(q2[u][:], both(u, 0), ACT.Square)
                    nc.scalar.activation(k2[u][:], both(u, 1), ACT.Square)
                    nc.scalar.activation(v[u][:, :, :, 0:DH], both(u, 2).rearrange("p t (h e) -> p t h e", h=HEADS),
                                         ACT.Copy).then_inc(S["copied"], 1)
                for u in range(LANES):
                    act.wait_ge(S["q_feat"], i * LANES + u + 1)
                    nc.scalar.activation(qp[u][:].rearrange("p (b a) n -> p b (a n)", a=2),
                                         bank[u][:, 0:3, 0:2 * N], ACT.Exp).then_inc(S["qp"], 1)
                for u in range(LANES):
                    act.wait_ge(S["k_feat"], i * LANES + u + 1)
                    nc.scalar.activation(kp[u][:].rearrange("p t (e n) -> p (t e) n", e=2),
                                         bank[u][0:H2, :, 0:384], ACT.Exp).then_inc(S["kp"], 1)
                for u in range(LANES):
                    act.wait_ge(S["o_turned"], i * LANES + u + 1)
                    nc.scalar.activation(oT[u][:], both(u, 2), ACT.Copy).then_inc(S["oT"], 1)

        @block.vector
        def _(dve):
            dve.wait_ge(S["preset"], 2 * LANES)
            with dve.Fori(0, TURNS) as i:
                for u in range(LANES):
                    normed_rows(k, rows[u], i, u).then_inc(S["rows"], 1)
                for u in range(LANES):
                    dve.wait_ge(S["kv_sums"], i * LANES + u + 1)
                    src = bank[u][:, 0, 0:PAIRS * 2 * VA].rearrange("p (a e) -> p a e", a=PAIRS)
                    nc.vector.tensor_copy(kv[u][0:64, :, 0:VA], src[0:64, :, 0:VA])
                    nc.vector.tensor_copy(kv[u][64:128, :, VA:2 * VA], src[64:128, :, VA:2 * VA]).then_inc(S["kv"], 1)
                for u in range(LANES):
                    dve.wait_ge(S["out"], i * LANES + u + 1)
                    nc.vector.tensor_scalar(den[u][:], sums(u)[:, :, :, DH], EPS_N, None, ALU.add).then_inc(S["den"], 1)
                    dve.wait_ge(S["den"], i * LANES + u + 1)
                    nc.vector.reciprocal(rden[u][:], den[u][:]).then_inc(S["rden"], 1)
                    dve.wait_ge(S["rden"], i * LANES + u + 1)
                    nc.vector.tensor_tensor(o[u][:].rearrange("p t (h e) -> p t h e", h=HEADS),
                                            sums(u)[:, :, :, 0:DH],
                                            rden[u][:].unsqueeze(3).broadcast_to([H2, 2, HEADS, DH]),
                                            ALU.mult).then_inc(S["o"], 1)
                for u in range(LANES):
                    dve.wait_ge(S["projected"], i * LANES + u + 1)
                    nc.vector.tensor_tensor(y[u][:], both(u, 3), rows[u][:], ALU.add).then_inc(S["y"], 1)
                    dve.wait_ge(S["y"], i * LANES + u + 1)
                    nc.vector.tensor_tensor(cent[:, ds((i * LANES + u) * 2, 2), :], y[u][:],
                                            bias[:].unsqueeze(1).broadcast_to([H2, 2, D]), ALU.add)


def add_normed(k, gamma_src, beta_src, parts=4):
    nc, h, cent = k.nc, k.h, k.cent
    with ExitStack() as ctx:
        gamma = k.sb("gamma", [H2, D], ctx=ctx)
        beta = k.sb("beta", [H2, D], ctx=ctx)
        scaled = k.sb("an_scaled", [H2, TILES, D], ctx=ctx)
        loaded, step, moved = k.sem("an_loaded"), k.sem("an_step"), k.sem("an_moved")
        n = TILES // parts
        block = ctx.enter_context(nc.Block())

        @block.sync
        def _(sp):
            sp.dma_start(gamma[:], gamma_src.broadcast_to([H2, D])).then_inc(loaded, 16)
            sp.dma_start(beta[:], beta_src.broadcast_to([H2, D])).then_inc(loaded, 16)

        @block.gpsimd
        def _(pool):
            pool.wait_ge(loaded, 32)
            for p in range(parts):
                at = slice(p * n, p * n + n)
                nc.gpsimd.tensor_tensor(h[:, at, :], h[:, at, :], beta[:].unsqueeze(1).broadcast_to([H2, n, D]),
                                        ALU.add).then_inc(moved, 1)

        @block.vector
        def _(dve):
            for p in range(parts):
                at = slice(p * n, p * n + n)
                nc.vector.tensor_tensor(scaled[:, at, :], cent[:, at, :],
                                        k.rstd[:, at].unsqueeze(2).broadcast_to([H2, n, D]), ALU.mult).then_inc(step, 1)
            dve.wait_ge(loaded, 32)
            for p in range(parts):
                at = slice(p * n, p * n + n)
                dve.wait_ge(step, p + 1)
                nc.vector.tensor_tensor(cent[:, at, :], scaled[:, at, :], gamma[:].unsqueeze(1).broadcast_to([H2, n, D]),
                                        ALU.mult).then_inc(step, 1)
            for p in range(parts):
                at = slice(p * n, p * n + n)
                dve.wait_ge(step, parts + p + 1)
                dve.wait_ge(moved, p + 1)
                nc.vector.tensor_tensor(h[:, at, :], h[:, at, :], cent[:, at, :], ALU.add)



NODES = 21
DEPTH = 11


def walk_tree(k, logits, coeff):
    nc = k.nc
    LAST = NODES - 1
    with ExitStack() as ctx:
        def big(x, n=NODES):
            return k.sb(f"tree_{x}", [H2, TILES, n], ctx=ctx)

        seen, right, act, got = big("seen"), big("right"), big("gelu"), big("got")
        a, b = big("a", 1), big("b", 1)
        step, gelued = k.sem("tree_step"), k.sem("tree_gelued")
        block = ctx.enter_context(nc.Block())

        @block.scalar
        def _(eng):
            nc.scalar.activation(act[:], logits[:], ACT.Gelu).then_inc(gelued, 1)

        @block.vector
        def _(dve):
            done = [0]

            def link(ins):
                done[0] += 1
                ins.then_inc(step, 1)
                dve.wait_ge(step, done[0])

            tt = nc.vector.tensor_tensor
            link(nc.vector.tensor_scalar(right[:], logits[:], 0.0, None, ALU.is_gt))
            link(nc.vector.memset(coeff[:], 0.0))
            link(nc.vector.memset(seen[:], 1.0))
            dve.wait_ge(gelued, 1)
            first, level = 0, 0
            while first <= LAST:
                end = min(2 * first + 1, NODES)
                here = slice(first, end)
                link(tt(got[:, :, here], seen[:, :, here], act[:, :, here], ALU.mult))
                whole = min(end, (NODES - 1) // 2)
                if whole > first:
                    up = slice(first, whole)
                    lo, hi = 2 * first + 1, 2 * whole + 1
                    for x, out in ((seen, seen), (got, coeff)):
                        link(tt(out[:, :, lo + 1:hi:2], x[:, :, up], right[:, :, up], ALU.mult))
                        link(tt(out[:, :, lo:hi:2], x[:, :, up], out[:, :, lo + 1:hi:2], ALU.subtract))
                if end > max(whole, first):
                    up = slice(max(whole, first), end)
                    if 2 * first + 1 <= LAST:
                        link(nc.vector.tensor_reduce(a[:], seen[:, :, up], AXX, ALU.add))
                        link(tt(seen[:, :, LAST:NODES], seen[:, :, LAST:NODES], a[:], ALU.add))
                    link(nc.vector.tensor_reduce(b[:], got[:, :, up], AXX, ALU.add))
                    link(tt(coeff[:, :, LAST:NODES], coeff[:, :, LAST:NODES], b[:], ALU.add))
                first, level = 2 * first + 1, level + 1
            link(nc.vector.scalar_tensor_tensor(out=coeff[:, :, LAST:NODES], in0=act[:, :, LAST:NODES],
                                                scalar=float(DEPTH - 1 - level), in1=coeff[:, :, LAST:NODES],
                                                op0=ALU.mult, op1=ALU.add))


def tree_ffn(k, in_T, out_w):
    with ExitStack() as ctx:
        logits = k.sb("tree_logits", [H2, TILES, NODES], ctx=ctx)
        coeff = k.sb("tree_coeff", [H2, TILES, NODES], ctx=ctx)
        norm_and_score(k, "tree", None, in_T, logits, NODES, keep=False)
        walk_tree(k, logits, coeff)
        add_expert_biases(k, "tree", coeff, out_w, NODES)


EXPERTS3, PER = 64, 16
SLOTS = EXPERTS3 * PER



QUARTERS = 4
QE = EXPERTS3 // QUARTERS
QS = SLOTS // QUARTERS
QC = QS // 128
HID3 = 2 * D
HC3 = HID3 // 128
XA = D + 1


def slots_prepare(k, phiT, xnT, xr, phi, token_row):
    nc = k.nc
    EPS_PHI = 1e-6
    with ExitStack() as ctx:
        sq = k.sb("sp_sq", [H2, 2, SLOTS], ctx=ctx)
        norm, root, scale = (k.sb(f"sp_{x}", [H2, 2, PER], ctx=ctx) for x in ("norm", "root", "scale"))
        rows = [k.sb(f"sp_rows{u}", [H2, 2, D], ctx=ctx) for u in range(LANES)]
        xT = [k.sb(f"sp_xT{u}", [H2, 2, D], ctx=ctx) for u in range(LANES)]
        low = [k.sb(f"sp_low{u}", [H2, 2], ctx=ctx) for u in range(LANES)]
        bank = [k.ps(f"sp_bank{u}", [128, 4, 512], ctx) for u in range(LANES)]
        S = {x: k.sem(f"sp_{x}") for x in ("loaded", "squared", "normed", "step", "rooted", "scaled", "ones", "rows",
                                          "turned", "xT", "kept", "logits", "low", "low_turned")}
        raw = k.sb("sp_raw", [H2, 2, SLOTS], ctx=ctx)
        block = ctx.enter_context(nc.Block())

        @block.sync
        def _(sp):
            sp.dma_start(raw[:], halves(phiT)).then_inc(S["loaded"], 16)

        @block.scalar
        def _(act):
            act.wait_ge(S["loaded"], 16)
            nc.scalar.activation(sq[:], raw[:], ACT.Square).then_inc(S["squared"], 1)
            act.wait_ge(S["normed"], 1)
            nc.scalar.activation(root[:], norm[:], ACT.Sqrt).then_inc(S["rooted"], 1)
            with act.Fori(0, TURNS) as i:
                for u in range(LANES):
                    act.wait_ge(S["turned"], i * LANES + u + 1)
                    act.wait_ge(S["kept"], i * LANES + u + 1)
                    nc.scalar.activation(xT[u][:], split2(bank[u][0:H2, 0, 0:2 * D]), ACT.Copy).then_inc(S["xT"], 1)

        @block.gpsimd
        def _(pool):
            nc.gpsimd.memset(xr[:, :, D:XA], 1.0).then_inc(S["kept"], LANES)
            with pool.Fori(0, TURNS) as i:
                for u in range(LANES):
                    b = i * LANES + u
                    pool.wait_ge(S["rows"], b + 1)
                    nc.gpsimd.tensor_copy(xr[:, ds(b * 2, 2), 0:D], rows[u][:])
                    pool.wait_ge(S["xT"], b + 1)
                    nc.gpsimd.tensor_copy(xnT[:, :, ds(b * N, N)], xT[u][:]).then_inc(S["kept"], 1)

        @block.tensor
        def _(pe):
            with pe.Fori(0, TURNS) as i:
                for u in range(LANES):
                    pe.wait_ge(S["rows"], i * LANES + u + 1)
                    turn(pe, k, bank[u][0:H2, 0, :], rows[u]).then_inc(S["turned"], 1)
                for u in range(LANES):
                    pe.wait_ge(S["scaled"], 1)
                    pe.wait_ge(S["xT"], i * LANES + u + 1)
                    for t in range(2):
                        for s in range(2):
                            for d in range(2):
                                last = pe.matmul(bank[u][0:H2, 2 * t + s, :], xT[u][:, d, t * H2:t * H2 + H2],
                                                 phi[:, d, s * 512:s * 512 + 512], start=(d == 0), stop=(d == 1))
                    last.then_inc(S["logits"], 1)
                for u in range(LANES):
                    pe.wait_ge(S["low"], i * LANES + u + 1)
                    pe.transpose(bank[u][0:2, 0, 0:H2], low[u][:], k.ident[0:H2, 0:H2]).then_inc(S["low_turned"], 1)

        @block.vector
        def _(dve):
            dve.wait_ge(S["squared"], 1)
            nc.vector.tensor_reduce(scale[:], sq[:].rearrange("c a (n p) -> c a p n", p=PER), AXX, ALU.add).then_inc(S["step"], 1)
            dve.wait_ge(S["step"], 1)
            nc.vector.tensor_scalar(norm[:], scale[:], EPS_PHI, None, ALU.add).then_inc(S["normed"], 1)
            dve.wait_ge(S["rooted"], 1)
            nc.vector.reciprocal(scale[:], root[:]).then_inc(S["step"], 1)
            dve.wait_ge(S["step"], 2)
            for a in range(2):
                last = nc.vector.tensor_tensor(phi[:, a, :].rearrange("c (n p) -> c n p", p=PER),
                                               raw[:, a, :].rearrange("c (n p) -> c n p", p=PER),
                                               scale[:, a, :].unsqueeze(1).broadcast_to([H2, EXPERTS3, PER]), ALU.mult)
            last.then_inc(S["scaled"], 1)
            with dve.Fori(0, TURNS) as i:
                for u in range(LANES):
                    dve.wait_ge(S["kept"], i * LANES + u + 1)
                    normed_rows(k, rows[u], i, u).then_inc(S["rows"], 1)
                for u in range(LANES):
                    dve.wait_ge(S["logits"], i * LANES + u + 1)
                    nc.vector.tensor_reduce(low[u][:], bank[u][0:H2, :, :].rearrange("p (t s) n -> p t s n", t=2),
                                            mybir.AxisListType.XY, ALU.max, negate=True).then_inc(S["low"], 1)
                for u in range(LANES):
                    dve.wait_ge(S["low_turned"], i * LANES + u + 1)
                    b = i * LANES + u
                    nc.vector.tensor_tensor(token_row[:, ds(b, 1), :].rearrange("r o (t n) -> r (o t) n", t=2),
                                            bank[u][0:2, 0, 0:H2].unsqueeze(1).broadcast_to([2, 2, H2]),
                                            k.ident[0:2, 0:2].unsqueeze(2).broadcast_to([2, 2, H2]), ALU.mult)


def slots_ffn(k, a):
    nc, h, cent = k.nc, k.h, k.cent
    with ExitStack() as ctx:
        xnT = k.sb("s_xnT", [H2, 2, T], ctx=ctx)
        xr = k.sb("s_xr", [H2, TILES, XA], ctx=ctx)
        phi = k.sb("s_phi", [H2, 2, SLOTS], ctx=ctx)
        token_row = k.sb("s_token_row", [2, B, N], ctx=ctx)
        slots_prepare(k, a["phiT"], xnT, xr, phi, token_row)

        def lanes(name, shape, dt=F32):
            return [k.sb(f"s_{name}{u}", shape, dt, ctx=ctx) for u in range(LANES)]

        quarter = k.sb("s_quarter", [H2, 2, QS], ctx=ctx)
        combine = k.sb("s_combine", [128, B, QC, N], ctx=ctx)
        rowsT = k.sb("s_rowsT", [H2, 2, QE, B, PER], ctx=ctx)
        total = k.sb("s_total", [H2, TILES], ctx=ctx)
        rtotal = k.sb("s_rtotal", [H2, TILES], ctx=ctx)
        ones = k.sb("s_ones", [2, 128], ctx=ctx)
        half = k.sb("s_half", [128, QC], ctx=ctx)
        ln_g, ln_b, b2 = (k.sb(f"s_{n}", [H2, 2, EXPERTS3], ctx=ctx) for n in ("ln_g", "ln_b", "b2"))
        b1 = k.sb("s_b1", [128, HC3, EXPERTS3], ctx=ctx)
        w1, w2 = lanes("w1_", [H2, 2, HID3]), lanes("w2_", [128, HC3, D])
        xT = lanes("xT", [H2, 2, N])
        slot_low, slot_row = lanes("slot_low", [128, QC]), lanes("slot_row", [2, QC, 128])
        disp = lanes("disp", [H2, 2, QS])
        stats, mv = lanes("stats", [128, QC, 6]), lanes("mv", [128, QC, 2])
        ssum, ssq, var, rstd = (lanes(x, [128, QC]) for x in ("ssum", "ssq", "var", "rstd"))
        work = lanes("work", [128, HC3, B * PER])
        hid = work
        normed, comb = ([w[:].rearrange("p c n -> p (c n)")[:, at * QC * D:(at + 1) * QC * D].rearrange(
            "p (c n) -> p c n", c=QC) for w in work] for at in range(2))
        xa = yT = disp
        ys = lanes("ys", [128, QC, XA])
        bank = [k.ps(f"s_bank{u}", [128, 4, 512], ctx) for u in range(LANES)]
        S = {x: k.sem(f"s_{x}") for x in (
            "small", "ones", "cleared", "quarter", "xT", "logits", "slot_low", "c_shifted", "low_turned", "slot_row",
            "d_shifted", "disp", "slots", "step", "aggr", "var", "rstd", "normed", "normed_turned", "rowsT",
            "affine", "lifted", "hid", "lowered", "outT", "yT", "comb", "y_turned", "ys", "summed",
            "added", "finish")}
        loaded = [k.sem(f"s_loaded{r}") for r in range(2)]
        block = ctx.enter_context(nc.Block())

        def pair(u, j, rows=128, n=N):
            return bank[u][0:rows, j, 0:2 * n].rearrange("p (a n) -> p a n", a=2)

        @block.sync
        def _(sp):
            for x, n in ((ln_g, "ln_g"), (ln_b, "ln_b"), (b2, "b2"), (b1, "b1")):
                sp.dma_start(x[:], a[n]).then_inc(S["small"], 16)
            with sp.Fori(0, EXPERTS3 // 2) as i:
                for r in range(2):
                    e = i * 2 + r
                    sp.wait_ge(S["lowered"], e + 1)
                    sp.dma_start(w1[r][:], a["w1"][ds(e, 1)].rearrange("o (a p) n -> p (o a) n", p=H2)).then_inc(loaded[r], 16)
                    sp.dma_start(w2[r][:], a["w2"][ds(e, 1)].rearrange("o (c p) n -> p (o c) n", p=128)).then_inc(loaded[r], 16)

        @block.gpsimd
        def _(pool):
            nc.gpsimd.memset(ones[:], 1.0)
            nc.gpsimd.memset(half[:], -0.5)
            for u in range(LANES):
                nc.gpsimd.memset(ys[u][:, :, D:XA], 1.0).then_inc(S["ones"], 1)
            pool.wait_ge(S["ones"], LANES)
            with pool.Fori(0, QUARTERS) as q:
                with pool.Fori(0, TURNS) as i:
                    for u in range(LANES):
                        n = q * B + i * LANES + u
                        pool.wait_ge(S["slots"], n + 1)
                        nc.gpsimd.tensor_copy(xT[u][:], xnT[:, :, ds((i * LANES + u) * N, N)]).then_inc(S["xT"], 1)
                    for u in range(LANES):
                        n = q * B + i * LANES + u
                        pool.wait_ge(S["var"], n + 1)
                        nc.gpsimd.tensor_tensor(rstd[u][:], var[u][:], half[:], ALU.pow).then_inc(S["rstd"], 1)
                with pool.Fori(0, TURNS) as i:
                    for u in range(LANES):
                        n = q * B + i * LANES + u
                        pool.wait_ge(S["summed"], n + 1)
                        pool.wait_ge(S["outT"], (q + 1) * QE)
                        nc.gpsimd.tensor_copy(comb[u][:], combine[:, ds(i * LANES + u, 1), :, :].rearrange(
                            "p o c n -> p (o c) n")).then_inc(S["comb"], 1)

        @block.tensor
        def _(pe):
            pe.wait_ge(S["ones"], LANES)
            with pe.Fori(0, QUARTERS) as q:
                with pe.Fori(0, TURNS) as i:
                    for u in range(LANES):
                        pe.wait_ge(S["quarter"], q + 1)
                        pe.wait_ge(S["xT"], q * B + i * LANES + u + 1)
                        for c in range(QC):
                            for d in range(2):
                                pe.matmul(pair(u, 0)[:, c, :], quarter[:, d, c * 128:c * 128 + 128], xT[u][:, d, :],
                                          start=(c == 0 and d == 0), stop=False, skip_group_check=True)
                        for t in range(2):
                            for d in range(2):
                                last = pe.matmul(pair(u, 1, H2, QS)[:, t, :], xT[u][:, d, t * H2:t * H2 + H2],
                                                 quarter[:, d, :], start=(t == 0 and d == 0), stop=False,
                                                 skip_group_check=True)
                        last.then_inc(S["logits"], 1)
                    for u in range(LANES):
                        pe.wait_ge(S["slot_low"], q * B + i * LANES + u + 1)
                        for c in range(QC):
                            last = pe.matmul(pair(u, 0)[:, c, :], ones[:],
                                             token_row[:, ds(i * LANES + u, 1), :].rearrange("r o n -> r (o n)"),
                                             start=False, stop=(c == QC - 1), skip_group_check=True)
                        last.then_inc(S["c_shifted"], 1)
                        pe.transpose(bank[u][0:QC, 2, 0:128], slot_low[u][:], k.ident[:]).then_inc(S["low_turned"], 1)
                    for u in range(LANES):
                        pe.wait_ge(S["slot_row"], q * B + i * LANES + u + 1)
                        for t in range(2):
                            last = pe.matmul(pair(u, 1, H2, QS)[:, t, :], ones[:, 0:H2],
                                             slot_row[u][:].rearrange("r c n -> r (c n)"),
                                             start=False, stop=(t == 1), skip_group_check=True)
                        last.then_inc(S["d_shifted"], 1)
                    for u in range(LANES):
                        pe.wait_ge(S["disp"], q * B + i * LANES + u + 1)
                        for c in range(QC):
                            for t in range(2):
                                last = pe.matmul(pair(u, 2, 128, XA)[:, c, :], disp[u][:, t, c * 128:c * 128 + 128],
                                                 xr[:, ds((i * LANES + u) * 2 + t, 1), :].rearrange("p o n -> p (o n)"),
                                                 start=(t == 0), stop=(t == 1))
                        last.then_inc(S["slots"], 1)
                    for u in range(LANES):
                        pe.wait_ge(S["normed"], q * B + i * LANES + u + 1)
                        for d in range(2):
                            for c in range(QC):
                                last = pe.transpose(pair(u, 3, H2, QS)[:, d, c * 128:c * 128 + 128],
                                                    normed[u][:, c, d * H2:d * H2 + H2], k.ident[:])
                        last.then_inc(S["normed_turned"], 1)
                with pe.Fori(0, QE // 2) as i:
                    for r in range(2):
                        n = q * QE + i * 2 + r
                        pe.wait_ge(loaded[r], (q * (QE // 2) + i + 1) * 32)
                        pe.wait_ge(S["affine"], n + 1)
                        for c in range(HC3):
                            for d in range(2):
                                last = pe.matmul(bank[r][:, c // 2, c % 2 * 256:c % 2 * 256 + 256],
                                                 w1[r][:, d, c * 128:c * 128 + 128], xa[r][:, d, :],
                                                 start=(d == 0), stop=(d == 1))
                        last.then_inc(S["lifted"], 1)
                    for r in range(2):
                        n = q * QE + i * 2 + r
                        pe.wait_ge(S["hid"], n + 1)
                        for d in range(2):
                            for c in range(HC3):
                                last = pe.matmul(pair(r, 2, H2, 256)[:, d, :], w2[r][:, c, d * H2:d * H2 + H2],
                                                 hid[r][:, c, :], start=(c == 0), stop=(c == HC3 - 1))
                        last.then_inc(S["lowered"], 1)
                with pe.Fori(0, TURNS) as i:
                    for u in range(LANES):
                        pe.wait_ge(S["yT"], q * B + i * LANES + u + 1)
                        for c in range(QC):
                            for d in range(2):
                                last = pe.transpose(pair(u, 0)[:, c, d * H2:d * H2 + H2],
                                                    yT[u][:, d, c * 128:c * 128 + 128], k.ident[0:H2, 0:H2])
                        last.then_inc(S["y_turned"], 1)
                    for u in range(LANES):
                        pe.wait_ge(S["ys"], q * B + i * LANES + u + 1)
                        pe.wait_ge(S["comb"], q * B + i * LANES + u + 1)
                        for t in range(2):
                            for c in range(QC):
                                last = pe.matmul(pair(u, 1, H2, XA)[:, t, :], comb[u][:, c, t * H2:t * H2 + H2],
                                                 ys[u][:, c, :], start=(c == 0), stop=(c == QC - 1))
                        last.then_inc(S["summed"], 1)

        @block.scalar
        def _(act):
            act.wait_ge(S["small"], 64)
            with act.Fori(0, QUARTERS) as q:
                with act.Fori(0, TURNS) as i:
                    for u in range(LANES):
                        act.wait_ge(S["c_shifted"], q * B + i * LANES + u + 1)
                        nc.scalar.activation(combine[:, ds(i * LANES + u, 1), :, :].rearrange("p o c n -> p (o c) n"),
                                             pair(u, 0), ACT.Exp)
                    for u in range(LANES):
                        act.wait_ge(S["d_shifted"], q * B + i * LANES + u + 1)
                        nc.scalar.activation(disp[u][:], pair(u, 1, H2, QS), ACT.Exp).then_inc(S["disp"], 1)
                    for u in range(LANES):
                        act.wait_ge(S["normed_turned"], q * B + i * LANES + u + 1)
                        nc.scalar.activation(rowsT[:, :, :, ds(i * LANES + u, 1), :].rearrange("c a n o p -> c (a n) (o p)"),
                                             bank[u][0:H2, 3, :].rearrange("c (n p) -> c n p", p=PER),
                                             ACT.Copy).then_inc(S["rowsT"], 1)
                with act.Fori(0, QE // 2) as i:
                    for r in range(2):
                        n = q * QE + i * 2 + r
                        act.wait_ge(S["lifted"], n + 1)
                        for c in range(HC3):
                            last = nc.scalar.activation(hid[r][:, c, :], bank[r][:, c // 2, c % 2 * 256:c % 2 * 256 + 256],
                                                        ACT.Gelu, bias=b1[:, c, ds(n, 1)])
                        last.then_inc(S["hid"], 1)
                    for r in range(2):
                        n = q * QE + i * 2 + r
                        act.wait_ge(S["lowered"], 2 + n + 1)
                        for d in range(2):
                            last = nc.scalar.activation(rowsT[:, d, ds(i * 2 + r, 1), :, :].rearrange("c o b p -> c (o b p)"),
                                                        pair(r, 2, H2, 256)[:, d, :], ACT.Identity, bias=b2[:, d, ds(n, 1)])
                        last.then_inc(S["outT"], 1)
                with act.Fori(0, TURNS) as i:
                    for u in range(LANES):
                        act.wait_ge(S["y_turned"], q * B + i * LANES + u + 1)
                        nc.scalar.activation(ys[u][:, :, 0:D], pair(u, 0), ACT.Copy).then_inc(S["ys"], 1)

        @block.vector
        def _(dve):
            nc.vector.memset(cent[:], 0.0)
            nc.vector.memset(total[:], 0.0).then_inc(S["cleared"], 1)
            nc.vector.memset(ssum[0][:], 0.0).then_inc(S["slots"], LANES)
            nc.vector.memset(ssum[1][:], 0.0).then_inc(S["summed"], LANES)
            nc.vector.memset(ssq[0][:], 0.0).then_inc(S["lowered"], 2)
            dve.wait_ge(S["small"], 64)
            dve.wait_ge(S["cleared"], 1)
            with dve.Fori(0, QUARTERS) as q:
                nc.vector.tensor_copy(quarter[:], phi[:, :, ds(q * QS, QS)]).then_inc(S["quarter"], 1)
                with dve.Fori(0, TURNS) as i:
                    for u in range(LANES):
                        dve.wait_ge(S["logits"], q * B + i * LANES + u + 1)
                        nc.vector.tensor_reduce(slot_low[u][:], pair(u, 0), AXX, ALU.max, negate=True).then_inc(S["slot_low"], 1)
                    for u in range(LANES):
                        dve.wait_ge(S["low_turned"], q * B + i * LANES + u + 1)
                        nc.vector.tensor_tensor(slot_row[u][:], bank[u][0:QC, 2, 0:128].unsqueeze(1).broadcast_to([QC, QC, 128]),
                                                k.ident[0:QC, 0:QC].unsqueeze(2).broadcast_to([QC, QC, 128]),
                                                ALU.mult).then_inc(S["slot_row"], 1)
                    for u in range(LANES):
                        n = q * B + i * LANES + u
                        dve.wait_ge(S["slots"], LANES + n + 1)
                        for c in range(QC):
                            nc.vector.bn_stats(stats[u][:, c, :], pair(u, 2, 128, XA)[:, c, 0:D])
                        nc.vector.tensor_copy(ssum[u][:], pair(u, 2, 128, XA)[:, :, D]).then_inc(S["step"], 1)
                        dve.wait_ge(S["step"], n + 1)
                        nc.vector.scalar_tensor_tensor(out=ssq[u][:], in0=ssum[u][:], scalar=EPS, in1=ssum[u][:],
                                                       op0=ALU.mult, op1=ALU.mult)
                        for c in range(QC):
                            last = nc.vector.bn_aggr(mv[u][:, c, :], stats[u][:, c, :])
                        last.then_inc(S["aggr"], 1)
                    for u in range(LANES):
                        n = q * B + i * LANES + u
                        dve.wait_ge(S["aggr"], n + 1)
                        nc.vector.tensor_tensor(var[u][:], mv[u][:, :, 1], ssq[u][:], ALU.add).then_inc(S["var"], 1)
                    for u in range(LANES):
                        n = q * B + i * LANES + u
                        dve.wait_ge(S["rstd"], n + 1)
                        for c in range(QC):
                            last = nc.vector.tensor_scalar(normed[u][:, c, :], pair(u, 2, 128, XA)[:, c, 0:D],
                                                           mv[u][:, c, 0:1], rstd[u][:, c:c + 1], ALU.subtract, ALU.mult)
                        last.then_inc(S["normed"], 1)
                with dve.Fori(0, QE // 2) as i:
                    for r in range(2):
                        dve.wait_ge(S["rowsT"], (q + 1) * B)
                        e = q * QE + i * 2 + r
                        dve.wait_ge(S["lowered"], e + 1)
                        for d in range(2):
                            last = nc.vector.tensor_scalar(xa[r][:, d, :],
                                                           rowsT[:, d, ds(i * 2 + r, 1), :, :].rearrange("c o b p -> c (o b p)"),
                                                           ln_g[:, d, ds(e, 1)], ln_b[:, d, ds(e, 1)], ALU.mult, ALU.add)
                        last.then_inc(S["affine"], 1)
                with dve.Fori(0, TURNS) as i:
                    for u in range(LANES):
                        dve.wait_ge(S["outT"], (q + 1) * QE)
                        nc.vector.tensor_copy(yT[u][:].rearrange("c a (n p) -> c (a n) p", p=PER),
                                              rowsT[:, :, :, ds(i * LANES + u, 1), :].rearrange("c a n o p -> c (a n) (o p)"),
                                              ).then_inc(S["yT"], 1)
                    for u in range(LANES):
                        n = q * B + i * LANES + u
                        dve.wait_ge(S["summed"], LANES + n + 1)
                        at = ds((i * LANES + u) * 2, 2)
                        got = pair(u, 1, H2, XA)
                        nc.vector.tensor_tensor(cent[:, at, :], cent[:, at, :], got[:, :, 0:D], ALU.add)
                        nc.vector.tensor_tensor(total[:, at], total[:, at], got[:, :, D], ALU.add).then_inc(S["added"], 1)
            dve.wait_ge(S["added"], QUARTERS * B)
            nc.vector.reciprocal(rtotal[:], total[:]).then_inc(S["finish"], 1)
            dve.wait_ge(S["finish"], 1)
            nc.vector.tensor_tensor(cent[:], cent[:], rtotal[:].unsqueeze(2).broadcast_to([H2, TILES, D]),
                                    ALU.mult).then_inc(S["finish"], 1)
            dve.wait_ge(S["finish"], 2)
            nc.vector.tensor_tensor(h[:], h[:], cent[:], ALU.add)



def build(nc, a, out):
    with ExitStack() as ctx:
        k = Core(nc, ctx)
        steps = [
            lambda: embed(k, a["patchesT"], a["L0_tok_wT"], a["L0_tok_b"], a["txt"]),
            lambda: center(k, "n0"),
            lambda: attention0(k, a["L0_attn_WqT"], a["L0_attn_WkT"], a["L0_attn_WvT"]),
            lambda: center(k, "n1"),
            lambda: moe(k, "f0", 8, a["L0_ffn_router_wT"], a["L0_ffn_WgT"], a["L0_ffn_WuT"], a["L0_ffn_WdT"], None, None),
            lambda: center(k, "n2"),
            lambda: attention1(k, a["L1_attn_WqkT"], a["L1_attn_WvT"], a["L1_attn_WprojT"], a["L1_attn_bproj"], a["L1_attn_steps"]),
            lambda: center(k, "n3"),
            lambda: moe(k, "f1", 16, a["L1_ffn_WrT"], a["L1_ffn_W1"], None, a["L1_ffn_W2"], a["L1_ffn_b1"], a["L1_ffn_b2"]),
            lambda: center(k, "n4"),
            lambda: attention2(k, a["L2_attn_Wqkv"], a["L2_attn_features"], a["L2_attn_Wproj"], a["L2_attn_b_proj"]),
            lambda: center(k, "n5", src=k.cent),
            lambda: add_normed(k, a["L2_attn_gamma"], a["L2_attn_beta"]),
            lambda: center(k, "n6"),
            lambda: tree_ffn(k, a["L2_ffn_weights_inT"], a["L2_ffn_weights_out"]),
            lambda: center(k, "n7"),
            lambda: attention3(k, a["L3_attn_WqkT"], a["L3_attn_WvT"], a["L3_attn_WprojT"], a["L3_attn_b_proj"]),
            lambda: center(k, "n8"),
            lambda: slots_ffn(k, a),
        ]
        for step in steps:
            step()
            if len(nc.free_semaphores) < 60:
                k.layer_done()
        stored = k.sem("out_stored")
        block = ctx.enter_context(nc.Block())

        @block.sync
        def _(sp):
            sp.dma_start(out.rearrange("b (a p) d -> p (b a) d", p=H2), k.h[:]).then_inc(stored, 16)
            sp.wait_ge(stored, 16)



def layout(x):
    x = {n: np.asarray(v) for n, v in x.items()}
    P, G = 32, 8
    img = x["x"].reshape(B, G, P, G, P)
    a = {
        "patchesT": img.transpose(2, 4, 0, 1, 3).reshape(P * P, B * G * G),
        "txt": x["txt"],
        "L0_tok_wT": x["L0_tok_w"].T,
        "L0_tok_b": x["L0_tok_b"].reshape(1, D),
    }
    for n in ("Wq", "Wk", "Wv"):
        a[f"L0_attn_{n}T"] = x[f"L0_attn_{n}"].T
    for n in ("router_w", "Wg", "Wu", "Wd"):
        a[f"L0_ffn_{n}T"] = np.swapaxes(x[f"L0_ffn_{n}"], -1, -2)
    a["L1_ffn_WrT"] = x["L1_ffn_Wr"].T
    a["L1_ffn_b1"] = x["L1_ffn_b1"].reshape(16, FC, 128).transpose(0, 2, 1)
    for n in ("W1", "W2", "b2"):
        a[f"L1_ffn_{n}"] = x[f"L1_ffn_{n}"]
    def padded(w):
        z = np.zeros((2 * HEADS, 32, D), w.dtype)
        z[:, 0:DH] = w.reshape(2 * HEADS, DH, D)
        return z.reshape(2 * PAD, D).T

    for at, qkv, proj, bias in (("L1_attn", "Wqkv", "Wproj", "bproj"), ("L3_attn", "w_qkv", "w_proj", "b_proj")):
        a[f"{at}_WqkT"] = padded(x[f"{at}_{qkv}"][0:2 * D])
        a[f"{at}_WvT"] = x[f"{at}_{qkv}"][2 * D:].T
        a[f"{at}_WprojT"] = x[f"{at}_{proj}"].T
        a[f"{at}_{bias}"] = x[f"{at}_{bias}"].reshape(1, D)
    a["L2_attn_Wqkv"], a["L2_attn_Wproj"] = x["L2_attn_W_qkv"], x["L2_attn_W_proj"]
    for n in ("b_proj", "gamma", "beta"):
        a[f"L2_attn_{n}"] = x[f"L2_attn_{n}"].reshape(1, D)
    f = x["L2_attn_random_features"]
    blocks = np.zeros((2, HALF_HEADS, DH, HALF_HEADS, FEATURES), f.dtype)
    for n in range(HALF_HEADS):
        blocks[0, n, :, n, :] = f.T
        blocks[1, n, :, n, :] = -0.5
    a["L2_attn_features"] = blocks.reshape(2, H2, HALF_HEADS * FEATURES)
    a["L2_ffn_weights_inT"] = x["L2_ffn_weights_in"].T
    a["L2_ffn_weights_out"] = x["L2_ffn_weights_out"]
    a["phiT"] = x["L3_ffn_phi"].transpose(2, 0, 1).reshape(D, SLOTS)
    for n in ("w1", "w2"):
        a[n] = x[f"L3_ffn_{n}"]
    for n, c in (("ln_g", H2), ("ln_b", H2), ("b1", 128), ("b2", H2)):
        w = x[f"L3_ffn_{n}"]
        a[n] = w.reshape(EXPERTS3, -1, c).transpose(2, 1, 0)
    a["L1_attn_steps"] = np.stack([x[f"L1_attn_{n}"] for n in ("s_q", "s_k", "s_v", "s_attn", "s_after")]).reshape(1, 5)
    return {n: np.ascontiguousarray(v) for n, v in a.items()}


def kernel(**inputs):
    import concourse.bacc as bacc
    from concourse.bass_utils import run_bass_kernel_spmd

    nc = bacc.Bacc("TRN2", target_bir_lowering=False, num_devices=1)
    arrays = layout(inputs)
    aps = {n: nc.dram_tensor(f"in_{n}", v.shape, mybir.dt.from_np(v.dtype), kind="ExternalInput").ap()
           for n, v in arrays.items()}
    out = nc.dram_tensor("out", (B, N, D), F32, kind="ExternalOutput").ap()
    build(nc, aps, out)
    r = run_bass_kernel_spmd(nc, [{f"in_{n}": v for n, v in arrays.items()}], core_ids=[0])
    return r.results[0]["out"]
```

```python
from contextlib import ExitStack

import numpy as np

import concourse.bass as bass
from concourse import mybir

F32 = mybir.dt.float32
BF16 = mybir.dt.bfloat16
I32 = mybir.dt.int32
U32 = mybir.dt.uint32
ALU = mybir.AluOpType
ACT = mybir.ActivationFunctionType
AXX = mybir.AxisListType.X

B, N, D = 16, 192, 192
H2 = 96
TILES = 2 * B
T = B * N
LANES = 2
TURNS = B // LANES
HEADS, DH = 12, 16
GROUPS = 3
ROUND = 12582912.0
EPS = 1e-5


def ds(start, size):
    return bass.ds(start, size)


class Core:

    def __init__(self, nc, ctx):
        self.nc, self.ctx, self.sems = nc, ctx, []
        self.h = self.sb("h", [H2, TILES, D])
        self.cent = self.sb("cent", [H2, TILES, D])
        self.rstd = self.sb("rstd", [H2, TILES])
        self.ident = self.sb("ident", [128, 128])

    def sb(self, name, shape, dt=F32, ctx=None):
        return (ctx or self.ctx).enter_context(self.nc.sbuf_tensor(name, shape, dt))

    def ps(self, name, shape, ctx, dt=F32):
        return ctx.enter_context(self.nc.psum_tensor(name, shape, dt))

    def sem(self, name):
        s = self.nc.alloc_semaphore(name=name)
        self.sems.append(s)
        return s

    def layer_done(self):
        if self.sems:
            self.nc.clear_and_free_semaphores(self.sems)
            self.nc.all_engine_barrier()
        self.sems = []


def halves(w):
    return w.rearrange("(a p) n -> p a n", p=H2)



def embed(k, patchesT, tok_wT, tok_b, txt, visits):
    nc, h = k.nc, k.h
    PF, PT = 1024, 64
    FC = PF // 128
    with ExitStack() as ctx:
        pat = [k.sb(f"pat{u}", [128, FC, 128], ctx=ctx) for u in range(LANES)]
        w = k.sb("tok_w", [128, FC, D], ctx=ctx)
        bias = k.sb("tok_bias", [1, D], ctx=ctx)
        zeros = k.sb("tok_zeros", [128, 8 * D], ctx=ctx)
        ones = k.sb("tok_ones", [1, 128], ctx=ctx)
        acc = [k.ps(f"tok_ps{u}", [128, 512], ctx) for u in range(LANES)]
        pat_in, w_in, txt_in = [k.sem(f"pat_in{u}") for u in range(LANES)], k.sem("tokw_in"), k.sem("txt_in")
        consts, embedded, stored = k.sem("tok_consts"), k.sem("embedded"), k.sem("emb_stored")
        turns = B // 2 // LANES
        src = patchesT.rearrange("(c p) t -> p c t", p=128)
        block = ctx.enter_context(nc.Block())

        @block.sync
        def _(sp):
            sp.dma_start(w[:], tok_wT.rearrange("(c p) n -> p c n", p=128)).then_inc(w_in, 16)
            sp.dma_start(bias[:], tok_b).then_inc(w_in, 16)
            with sp.Fori(0, turns) as i:
                for u in range(LANES):
                    sp.wait_ge(embedded, i * LANES + u + 1)
                    sp.dma_start(pat[u][:], src[:, :, ds((i * LANES + u) * 128, 128)]).then_inc(pat_in[u], 16)

        @block.scalar
        def _(act):
            tx = txt.rearrange("b t d -> t b d")
            hv = h[:, :, :].rearrange("p (b a) d -> p b a d", a=2)
            act.dma_start(hv[PT:H2, :, 0, :], tx[0:H2 - PT]).then_inc(txt_in, 16)
            act.dma_start(hv[:, :, 1, :], tx[H2 - PT:128]).then_inc(txt_in, 16)
            act.wait_ge(consts, 4)
            for n in range(visits.shape[0] // 1024):
                act.dma_start(visits[n * 1024:(n + 1) * 1024].rearrange("(p c) d -> p (c d)", p=128), zeros[:]).then_inc(txt_in, 16)
            act.wait_ge(txt_in, 32 + 16 * (visits.shape[0] // 1024))

        @block.gpsimd
        def _(pool):
            nc.gpsimd.memset(k.ident[:], 0.0).then_inc(consts, 1)
            pool.wait_ge(consts, 1)
            nc.gpsimd.affine_select(out=k.ident[:], in_=k.ident[:], compare_op=ALU.not_equal, fill=1.0,
                                    base=0, pattern=[[-1, 128]], channel_multiplier=1).then_inc(consts, 1)
            pool.wait_ge(consts, 2)
            nc.gpsimd.memset(ones[:], 1.0).then_inc(consts, 1)
            nc.gpsimd.memset(zeros[:], 0.0).then_inc(consts, 1)

        @block.tensor
        def _(pe):
            pe.wait_ge(w_in, 32)
            pe.wait_ge(consts, 3)
            with pe.Fori(0, turns) as i:
                for u in range(LANES):
                    pe.wait_ge(pat_in[u], i * 16 + 16)
                    pe.wait_ge(stored, i * LANES + u + 1)
                    pe.matmul(acc[u][:, 0:D], ones[:], bias[:], start=True, stop=False)
                    for c in range(FC):
                        last = pe.matmul(acc[u][:, 0:D], pat[u][:, c, :], w[:, c, :], start=False, stop=(c == FC - 1))
                    last.then_inc(embedded, 1)

        @block.vector
        def _(dve):
            nc.vector.memset(k.rstd[:, 0:1], 0.0).then_inc(stored, LANES)
            nc.vector.memset(k.rstd[:, 1:2], 0.0).then_inc(embedded, LANES)
            with dve.Fori(0, turns) as i:
                for u in range(LANES):
                    dve.wait_ge(embedded, LANES + i * LANES + u + 1)
                    t = (i * LANES + u) * 4
                    nc.vector.tensor_copy(h[0:PT, ds(t, 1), :], acc[u][0:PT, None, 0:D])
                    nc.vector.tensor_copy(h[0:PT, ds(t + 2, 1), :], acc[u][PT:2 * PT, None, 0:D]).then_inc(stored, 1)



def center(k, name, src=None, parts=4):
    nc, cent, rstd = k.nc, k.cent, k.rstd
    h = k.h if src is None else src
    with ExitStack() as ctx:
        sq = k.sb(f"{name}_sq", [H2, TILES, D], ctx=ctx)
        total = k.sb(f"{name}_sum", [H2, TILES], ctx=ctx)
        mean = k.sb(f"{name}_mean", [H2, TILES], ctx=ctx)
        var = k.sb(f"{name}_var", [H2, TILES], ctx=ctx)
        std = k.sb(f"{name}_std", [H2, TILES], ctx=ctx)
        summed, meaned, centered, squared = (k.sem(f"{name}_{x}") for x in ("summed", "meaned", "centered", "squared"))
        varied, rooted = k.sem(f"{name}_varied"), k.sem(f"{name}_rooted")
        n = TILES // parts
        block = ctx.enter_context(nc.Block())

        @block.vector
        def _(dve):
            for p in range(parts):
                at = slice(p * n, p * n + n)
                nc.vector.tensor_reduce(total[:, at], h[:, at, :], AXX, ALU.add).then_inc(summed, 1)
                dve.wait_ge(summed, p + 1)
                nc.vector.tensor_scalar(mean[:, at], total[:, at], 1.0 / D, None, ALU.mult).then_inc(meaned, 1)
                dve.wait_ge(meaned, p + 1)
                nc.vector.tensor_tensor(cent[:, at, :], h[:, at, :],
                                        mean[:, at].unsqueeze(2).broadcast_to([H2, n, D]),
                                        ALU.subtract).then_inc(centered, 1)
            for p in range(parts):
                at = slice(p * n, p * n + n)
                dve.wait_ge(squared, p + 1)
                nc.vector.tensor_reduce(total[:, at], sq[:, at, :], AXX, ALU.add).then_inc(summed, 1)
            dve.wait_ge(summed, 2 * parts)
            nc.vector.tensor_scalar(var[:], total[:], 1.0 / D, EPS, ALU.mult, ALU.add).then_inc(varied, 1)
            dve.wait_ge(rooted, 1)
            nc.vector.reciprocal(rstd[:], std[:])

        @block.scalar
        def _(act):
            for p in range(parts):
                at = slice(p * n, p * n + n)
                act.wait_ge(centered, p + 1)
                nc.scalar.activation(sq[:, at, :], cent[:, at, :], ACT.Square).then_inc(squared, 1)
            act.wait_ge(varied, 1)
            nc.scalar.activation(std[:], var[:], ACT.Sqrt).then_inc(rooted, 1)



def normed_rows(k, out, i, u):
    b2 = (i * LANES + u) * 2
    return k.nc.vector.tensor_tensor(out[:], k.cent[:, ds(b2, 2), :],
                                     k.rstd[:, ds(b2, 2)].unsqueeze(2).broadcast_to([H2, 2, D]), ALU.mult)


def turn(pe, k, out, rows):
    for dh in range(2):
        for th in range(2):
            last = pe.transpose(out[:, dh * N + th * H2:dh * N + th * H2 + H2],
                                rows[:, th, dh * H2:dh * H2 + H2], k.ident[0:H2, 0:H2])
    return last


def split2(x):
    return x.rearrange("p (a n) -> p a n", a=2)


def attention0(k, WqT, WkT, WvT):
    nc, h = k.nc, k.h
    with ExitStack() as ctx:
        wq, wk, wv = (k.sb(f"a0_w{x}", [H2, 2, D], ctx=ctx) for x in "qkv")

        def lanes(name, shape, dt=F32):
            return [k.sb(f"a0_{name}{u}", shape, dt, ctx=ctx) for u in range(LANES)]

        rows, xT, qT, kT, v = (lanes(x, [H2, 2, D]) for x in ("rows", "xT", "qT", "kT", "v"))
        prob, probT = (lanes(x, [H2, 2, N]) for x in ("prob", "probT"))
        nmax, psum_, den, rden = (lanes(x, [H2, 2]) for x in ("nmax", "psum", "den", "rden"))
        bank = [[k.ps(f"a0_bank{u}{j}", [128, 512], ctx) for j in range(4)] for u in range(LANES)]
        S = {x: k.sem(f"a0_{x}") for x in (
            "w_in", "rows", "turned", "xT", "qkv", "qT", "kT", "v", "scores", "nmax", "prob", "probs_turned",
            "probT", "out", "den", "rden", "added")}
        block = ctx.enter_context(nc.Block())

        def view(u, j):
            return split2(bank[u][j][0:H2, 0:2 * D])

        @block.sync
        def _(sp):
            for w, src in ((wq, WqT), (wk, WkT), (wv, WvT)):
                sp.dma_start(w[:], halves(src)).then_inc(S["w_in"], 16)

        @block.tensor
        def _(pe):
            pe.wait_ge(S["w_in"], 48)
            with pe.Fori(0, TURNS) as i:
                for u in range(LANES):
                    pe.wait_ge(S["rows"], i * LANES + u + 1)
                    turn(pe, k, bank[u][0][0:H2], rows[u]).then_inc(S["turned"], 1)
                for u in range(LANES):
                    pe.wait_ge(S["xT"], i * LANES + u + 1)
                    for j, w in ((1, wq), (2, wk)):
                        for e in range(2):
                            for d in range(2):
                                pe.matmul(view(u, j)[:, e, :], w[:, d, e * H2:e * H2 + H2], xT[u][:, d, :],
                                          start=(d == 0), stop=(d == 1))
                    for t in range(2):
                        for d in range(2):
                            last = pe.matmul(view(u, 3)[:, t, :], xT[u][:, d, t * H2:t * H2 + H2], wv[:, d, :],
                                             start=(d == 0), stop=(d == 1))
                    last.then_inc(S["qkv"], 1)
                for u in range(LANES):
                    pe.wait_ge(S["qT"], i * LANES + u + 1)
                    pe.wait_ge(S["kT"], i * LANES + u + 1)
                    for t in range(2):
                        for e in range(2):
                            last = pe.matmul(view(u, 0)[:, t, :], qT[u][:, e, t * H2:t * H2 + H2], kT[u][:, e, :],
                                             start=(e == 0), stop=(e == 1))
                    last.then_inc(S["scores"], 1)
                for u in range(LANES):
                    pe.wait_ge(S["prob"], i * LANES + u + 1)
                    turn(pe, k, bank[u][1][0:H2], prob[u]).then_inc(S["probs_turned"], 1)
                for u in range(LANES):
                    pe.wait_ge(S["probT"], i * LANES + u + 1)
                    pe.wait_ge(S["v"], i * LANES + u + 1)
                    for t in range(2):
                        for m in range(2):
                            last = pe.matmul(view(u, 2)[:, t, :], probT[u][:, m, t * H2:t * H2 + H2], v[u][:, m, :],
                                             start=(m == 0), stop=(m == 1))
                    last.then_inc(S["out"], 1)

        @block.scalar
        def _(act):
            with act.Fori(0, TURNS) as i:
                for u in range(LANES):
                    act.wait_ge(S["turned"], i * LANES + u + 1)
                    nc.scalar.activation(xT[u][:], view(u, 0), ACT.Copy).then_inc(S["xT"], 1)
                for u in range(LANES):
                    act.wait_ge(S["qkv"], i * LANES + u + 1)
                    nc.scalar.activation(qT[u][:], view(u, 1), ACT.Copy).then_inc(S["qT"], 1)
                    nc.scalar.activation(v[u][:], view(u, 3), ACT.Copy).then_inc(S["v"], 1)
                for u in range(LANES):
                    act.wait_ge(S["nmax"], i * LANES + u + 1)
                    for t in range(2):
                        last = nc.scalar.activation(prob[u][:, t, :], view(u, 0)[:, t, :], ACT.Exp,
                                                    bias=nmax[u][:, t:t + 1], accum_out=psum_[u][:, t:t + 1])
                    last.then_inc(S["prob"], 1)

        @block.vector
        def _(dve):
            with dve.Fori(0, TURNS) as i:
                for u in range(LANES):
                    normed_rows(k, rows[u], i, u).then_inc(S["rows"], 1)
                for u in range(LANES):
                    dve.wait_ge(S["qkv"], i * LANES + u + 1)
                    nc.vector.tensor_copy(kT[u][:], view(u, 2)).then_inc(S["kT"], 1)
                for u in range(LANES):
                    dve.wait_ge(S["scores"], i * LANES + u + 1)
                    nc.vector.tensor_reduce(nmax[u][:], view(u, 0), AXX, ALU.max, negate=True).then_inc(S["nmax"], 1)
                for u in range(LANES):
                    dve.wait_ge(S["probs_turned"], i * LANES + u + 1)
                    nc.vector.tensor_copy(probT[u][:], view(u, 1)).then_inc(S["probT"], 1)
                    nc.vector.tensor_scalar(den[u][:], psum_[u][:], float(D) ** 0.5, None, ALU.mult).then_inc(S["den"], 1)
                    dve.wait_ge(S["den"], i * LANES + u + 1)
                    nc.vector.reciprocal(rden[u][:], den[u][:]).then_inc(S["rden"], 1)
                for u in range(LANES):
                    dve.wait_ge(S["out"], i * LANES + u + 1)
                    dve.wait_ge(S["rden"], i * LANES + u + 1)
                    t0 = (i * LANES + u) * 2
                    for t in range(2):
                        nc.vector.scalar_tensor_tensor(out=h[:, ds(t0 + t, 1), :], in0=view(u, 2)[:, t:t + 1, :],
                                                       scalar=rden[u][:, t:t + 1], in1=h[:, ds(t0 + t, 1), :],
                                                       op0=ALU.mult, op1=ALU.add)



FF = 4 * D
FC = FF // 128
ROWS = 256


def tiles_of(E):
    return 2 * T // ROWS + E


def norm_and_score(k, name, routerT, logits, E, keep):
    nc, h = k.nc, k.h
    with ExitStack() as ctx:
        w = k.sb(f"{name}_router", [H2, 2, E], ctx=ctx)
        rows = [k.sb(f"{name}_rows{u}", [H2, 2, D], ctx=ctx) for u in range(LANES)]
        xT = [k.sb(f"{name}_xT{u}", [H2, 2, D], ctx=ctx) for u in range(LANES)]
        pT = [k.ps(f"{name}_pT{u}", [128, 512], ctx) for u in range(LANES)]
        pL = [k.ps(f"{name}_pL{u}", [128, 512], ctx) for u in range(LANES)]
        w_in, rowed, turned, copied, kept, scored, logged = (
            k.sem(f"{name}_{x}") for x in ("w_in", "rowed", "turned", "copied", "kept", "scored", "logged"))
        block = ctx.enter_context(nc.Block())

        @block.sync
        def _(sp):
            sp.dma_start(w[:], halves(routerT)).then_inc(w_in, 16)

        @block.vector
        def _(dve):
            nc.vector.memset(rows[0][:, 0, 0:1], 0.0).then_inc(kept, LANES)
            with dve.Fori(0, TURNS) as i:
                for u in range(LANES):
                    dve.wait_ge(kept, i * LANES + u + 1)
                    normed_rows(k, rows[u], i, u).then_inc(rowed, 1)
                    if keep:
                        dve.wait_ge(rowed, i * LANES + u + 1)
                        hb = h[:, ds((i * LANES + u) * 2, 2), :]
                        nc.vector.tensor_tensor(hb, hb, rows[u][:], ALU.add)
                for u in range(LANES):
                    dve.wait_ge(scored, i * LANES + u + 1)
                    nc.vector.tensor_copy(logits[:, ds((i * LANES + u) * 2, 2), :],
                                          split2(pL[u][0:H2, 0:2 * E])).then_inc(logged, 1)

        @block.gpsimd
        def _(pool):
            with pool.Fori(0, TURNS) as i:
                for u in range(LANES):
                    pool.wait_ge(rowed, i * LANES + u + 1)
                    nc.gpsimd.tensor_copy(k.cent[:, ds((i * LANES + u) * 2, 2), :], rows[u][:]).then_inc(kept, 1)

        @block.tensor
        def _(pe):
            pe.wait_ge(w_in, 16)
            with pe.Fori(0, TURNS) as i:
                for u in range(LANES):
                    pe.wait_ge(rowed, i * LANES + u + 1)
                    turn(pe, k, pT[u][0:H2], rows[u]).then_inc(turned, 1)
                for u in range(LANES):
                    pe.wait_ge(copied, i * LANES + u + 1)
                    for t in range(2):
                        for d in range(2):
                            last = pe.matmul(pL[u][0:H2, t * E:t * E + E], xT[u][:, d, t * H2:t * H2 + H2],
                                             w[:, d, :], start=(d == 0), stop=(d == 1))
                    last.then_inc(scored, 1)

        @block.scalar
        def _(act):
            with act.Fori(0, TURNS) as i:
                for u in range(LANES):
                    act.wait_ge(turned, i * LANES + u + 1)
                    nc.scalar.activation(xT[u][:], split2(pT[u][0:H2, 0:2 * D]), ACT.Copy).then_inc(copied, 1)


def route(k, name, logits, gate, wts, place_of, expert_of, E, probs_first):
    nc = k.nc
    NT = tiles_of(E)
    MOST = T // ROWS
    with ExitStack() as ctx:
        def big(x, dt=F32):
            return k.sb(f"{name}_{x}", [H2, TILES, E], dt, ctx=ctx)

        def small(x, n=TILES, dt=F32):
            return k.sb(f"{name}_{x}", [H2, n], dt, ctx=ctx)

        iota_i, tri, ones = small("iota_i", NT, I32), small("tri", H2), small("ones", H2)
        iota, iota_less = small("iota", NT), small("iota_less", E)
        best = [small(f"best{r}") for r in range(2)]
        place = [small(f"place{r}") for r in range(2)]
        hot = [big(f"hot{r}") for r in range(2)]
        score, shifted, same, cand, rest, part = (big(x) for x in ("score", "shifted", "same", "cand", "rest", "part"))
        gap, e, den, rden = (small(x) for x in ("gap", "e", "den", "rden"))
        mask, run0, run1, rank = (big(x) for x in ("mask", "run0", "run1", "rank"))
        over = k.sb(f"{name}_over", [H2, E, MOST], ctx=ctx)
        fills, tiles = k.sb(f"{name}_fills", [H2, MOST], ctx=ctx), small("tiles", E)
        end0, end1, begin = small("end0", E), small("end1", E), small("begin", E)
        past = k.sb(f"{name}_past", [H2, NT, E], ctx=ctx)
        passed, tile_expert = small("passed", NT), small("tile_expert", NT)
        before = k.ps(f"{name}_before", [128, 512], ctx)
        total = k.ps(f"{name}_total", [128, 512], ctx)
        step, counted, to_exp, exped, masked, summed = (
            k.sem(f"{name}_{x}") for x in ("step", "counted", "to_exp", "exped", "masked", "summed"))
        block = ctx.enter_context(nc.Block())

        def over_experts(x):
            return x[:].unsqueeze(2).broadcast_to([H2, TILES, E])

        def over_tiles(x):
            return x[:].unsqueeze(1).broadcast_to([H2, TILES, E])

        def by_tile(x):
            return x[0:H2, 0:TILES * E].rearrange("p (t e) -> p t e", e=E)

        @block.gpsimd
        def _(pool):
            nc.gpsimd.iota(iota_i[:], pattern=[[1, NT]], base=0, channel_multiplier=0).then_inc(counted, 1)
            nc.gpsimd.memset(ones[:], 1.0).then_inc(counted, 1)
            pool.wait_ge(counted, 2)
            nc.gpsimd.affine_select(out=tri[:], in_=ones[:], compare_op=ALU.is_gt, fill=0.0, base=0,
                                    pattern=[[1, H2]], channel_multiplier=-1).then_inc(counted, 1)

        @block.scalar
        def _(act):
            act.wait_ge(to_exp, 1)
            if probs_first:
                nc.scalar.activation(cand[:], shifted[:], ACT.Exp).then_inc(exped, 1)
            else:
                nc.scalar.activation(e[:], gap[:], ACT.Exp).then_inc(exped, 1)

        @block.tensor
        def _(pe):
            pe.wait_ge(masked, 1)
            flat = mask[:].rearrange("p t e -> p (t e)")
            pe.matmul(before[0:H2, 0:TILES * E], tri[:], flat, start=True, stop=True)
            pe.matmul(total[0:H2, 0:TILES * E], ones[:], flat, start=True, stop=True).then_inc(summed, 1)

        @block.vector
        def _(dve):
            done = [0]

            def link(ins):
                done[0] += 1
                ins.then_inc(step, 1)
                dve.wait_ge(step, done[0])

            def running_sum(a, b, n, axis):
                d = 1
                while d < n:
                    at = (lambda x, lo, hi: x[:, lo:hi]) if axis == 1 else None
                    nc.vector.tensor_copy(at(b, 0, d), at(a, 0, d))
                    link(nc.vector.tensor_tensor(at(b, d, n), at(a, d, n), at(a, 0, n - d), ALU.add))
                    a, b, d = b, a, 2 * d
                return a

            dve.wait_ge(counted, 3)
            link(nc.vector.tensor_copy(iota[:], iota_i[:]))
            nc.vector.tensor_scalar(fills[:], iota[:, 0:MOST], float(ROWS), None, ALU.mult)
            link(nc.vector.tensor_scalar(iota_less[:], iota[:, 0:E], float(E), None, ALU.subtract))
            x = logits
            if probs_first:
                link(nc.vector.tensor_reduce(den[:], logits[:], AXX, ALU.max))
                link(nc.vector.tensor_tensor(shifted[:], logits[:], over_experts(den), ALU.subtract))
                nc.vector.memset(place[0][:], 0.0).then_inc(to_exp, 1)
                dve.wait_ge(exped, 1)
                link(nc.vector.tensor_reduce(e[:], cand[:], AXX, ALU.add))
                link(nc.vector.reciprocal(rden[:], e[:]))
                link(nc.vector.tensor_tensor(score[:], cand[:], over_experts(rden), ALU.mult))
                x = score
            for r in range(2):
                top = wts[r] if probs_first else best[r]
                link(nc.vector.tensor_reduce(top[:], x[:], AXX, ALU.max))
                link(nc.vector.tensor_tensor(same[:], x[:], over_experts(top), ALU.is_equal))
                link(nc.vector.tensor_tensor(cand[:], same[:], over_tiles(iota_less), ALU.mult))
                link(nc.vector.tensor_reduce(place[r][:], cand[:], AXX, ALU.min))
                link(nc.vector.tensor_tensor(hot[r][:], over_tiles(iota_less), over_experts(place[r]), ALU.is_equal))
                if r == 0:
                    link(nc.vector.scalar_tensor_tensor(out=rest[:], in0=hot[0][:], scalar=-1e30, in1=x[:],
                                                        op0=ALU.mult, op1=ALU.add))
                    x = rest
            nc.vector.tensor_tensor(mask[:], hot[0][:], hot[1][:], ALU.add).then_inc(masked, 1)
            if not probs_first:
                link(nc.vector.tensor_tensor(gap[:], best[1][:], best[0][:], ALU.subtract))
                nc.vector.memset(score[:, 0, 0:1], 0.0).then_inc(to_exp, 1)
                dve.wait_ge(exped, 1)
                link(nc.vector.tensor_scalar(den[:], e[:], 1.0, None, ALU.add))
                link(nc.vector.reciprocal(wts[0][:], den[:]))
                link(nc.vector.tensor_tensor(wts[1][:], wts[0][:], e[:], ALU.mult))
            link(nc.vector.tensor_tensor(part[:], hot[1][:], over_experts(wts[1]), ALU.mult))
            link(nc.vector.tensor_tensor(same[:], hot[0][:], over_experts(wts[0]), ALU.mult))
            nc.vector.tensor_tensor(gate[:], same[:], part[:], ALU.add)

            dve.wait_ge(summed, 1)
            link(nc.vector.tensor_copy(run0[:], by_tile(total)))
            run = running_sum(run0, run1, TILES, 1)
            other = run1 if run is run0 else run0
            link(nc.vector.tensor_tensor(over[:], run[:, TILES - 1, :].unsqueeze(2).broadcast_to([H2, E, MOST]),
                                         fills[:].unsqueeze(1).broadcast_to([H2, E, MOST]), ALU.is_gt))
            link(nc.vector.tensor_reduce(tiles[:], over[:], AXX, ALU.add))
            link(nc.vector.tensor_copy(end0[:], tiles[:]))
            end = running_sum(end0, end1, E, 1)
            link(nc.vector.tensor_tensor(begin[:], end[:], tiles[:], ALU.subtract))
            link(nc.vector.tensor_tensor(rank[:], run[:], by_tile(total), ALU.subtract))
            link(nc.vector.tensor_tensor(other[:], rank[:], by_tile(before), ALU.add))
            link(nc.vector.scalar_tensor_tensor(out=rank[:], in0=over_tiles(begin), scalar=float(ROWS), in1=other[:],
                                                op0=ALU.mult, op1=ALU.add))
            for r in range(2):
                link(nc.vector.tensor_tensor(cand[:], hot[r][:], rank[:], ALU.mult))
                link(nc.vector.tensor_reduce(place[r][:], cand[:], AXX, ALU.add))
                nc.vector.tensor_copy(place_of[:, r, :], place[r][:])
            link(nc.vector.tensor_tensor(past[:], iota[:].unsqueeze(2).broadcast_to([H2, NT, E]),
                                         end[:].unsqueeze(1).broadcast_to([H2, NT, E]), ALU.is_ge))
            link(nc.vector.tensor_reduce(passed[:], past[:], AXX, ALU.add))
            link(nc.vector.tensor_scalar(tile_expert[:], passed[:], float(E - 1), None, ALU.min))
            nc.vector.tensor_copy(expert_of[:], tile_expert[:])


def add_expert_biases(k, name, gate, b2, E):
    nc, h = k.nc, k.h
    with ExitStack() as ctx:
        w = k.sb(f"{name}_b2", [E, D], ctx=ctx)
        rows = [k.sb(f"{name}_g{u}", [H2, 2, E], ctx=ctx) for u in range(LANES)]
        gT = [k.sb(f"{name}_gT{u}", [E, N], ctx=ctx) for u in range(LANES)]
        pT = [k.ps(f"{name}_gp{u}", [128, 512], ctx) for u in range(LANES)]
        pO = [k.ps(f"{name}_go{u}", [128, 512], ctx) for u in range(LANES)]
        w_in, rowed, turned, copied, summed = (k.sem(f"{name}_g{x}") for x in ("w_in", "rowed", "turned", "copied", "summed"))
        block = ctx.enter_context(nc.Block())

        @block.sync
        def _(sp):
            sp.dma_start(w[:], b2).then_inc(w_in, 16)

        @block.vector
        def _(dve):
            with dve.Fori(0, TURNS) as i:
                for u in range(LANES):
                    nc.vector.tensor_copy(rows[u][:], gate[:, ds((i * LANES + u) * 2, 2), :]).then_inc(rowed, 1)
                for u in range(LANES):
                    dve.wait_ge(summed, i * LANES + u + 1)
                    hb = h[:, ds((i * LANES + u) * 2, 2), :]
                    nc.vector.tensor_tensor(hb, hb, split2(pO[u][0:H2, 0:2 * D]), ALU.add)

        @block.tensor
        def _(pe):
            pe.wait_ge(w_in, 16)
            with pe.Fori(0, TURNS) as i:
                for u in range(LANES):
                    pe.wait_ge(rowed, i * LANES + u + 1)
                    for t in range(2):
                        last = pe.transpose(pT[u][0:E, t * H2:t * H2 + H2], rows[u][:, t, :], k.ident[0:H2, 0:H2])
                    last.then_inc(turned, 1)
                for u in range(LANES):
                    pe.wait_ge(copied, i * LANES + u + 1)
                    for t in range(2):
                        last = pe.matmul(pO[u][0:H2, t * D:t * D + D], gT[u][:, t * H2:t * H2 + H2], w[:],
                                         start=True, stop=True)
                    last.then_inc(summed, 1)

        @block.scalar
        def _(act):
            with act.Fori(0, TURNS) as i:
                for u in range(LANES):
                    act.wait_ge(turned, i * LANES + u + 1)
                    nc.scalar.activation(gT[u][:], pT[u][0:E, 0:N], ACT.Copy).then_inc(copied, 1)


def send(k, name, visits, place_of):
    nc = k.nc
    with ExitStack() as ctx:
        sent = k.sem(f"{name}_sent")
        block = ctx.enter_context(nc.Block())

        @block.gpsimd
        def _(pool):
            for t in range(TILES):
                for r in range(2):
                    pool.indirect_dma_start(out=visits, out_offset=bass.IndirectOffsetOnAxis(ap=place_of[:, r, t:t + 1], axis=0),
                                            in_=k.cent[:, t, :], in_offset=None).then_inc(sent, 16)
            pool.wait_ge(sent, 16 * 2 * TILES)


def experts(k, name, visits, answers, expert_of, E, w_in1, w_in2, w_down, b1):
    nc = k.nc
    gated = w_in2 is not None
    NT = tiles_of(E)
    RC = ROWS // 128
    with ExitStack() as ctx:
        def two(x, shape):
            return [k.sb(f"{name}_{x}{r}", shape, ctx=ctx) for r in range(2)]

        w1, wd = two("w1_", [H2, 2, FF]), two("wd_", [128, FC, D])
        w2 = two("w2_", [H2, 2, FF]) if gated else None
        bias = None if gated else two("b1_", [128, FC])
        rows, xT = two("vrows", [128, RC, D]), two("vxT", [H2, 2, ROWS])
        hid, out = two("hid", [128, FC, ROWS]), two("vout", [128, RC, D])
        silu = two("silu", [128, ROWS]) if gated else None
        pt = [k.ps(f"{name}_pt{r}", [128, 512], ctx) for r in range(2)]
        pg = [k.ps(f"{name}_pg{j}", [128, 512], ctx) for j in range(3)]
        po = [k.ps(f"{name}_po{r}", [128, 512], ctx) for r in range(2)]
        loaded = [k.sem(f"{name}_loaded{r}") for r in range(2)]
        rowed = [k.sem(f"{name}_vrowed{r}") for r in range(2)]
        stored = [k.sem(f"{name}_vstored{r}") for r in range(2)]
        turned, copied, lifted, gates, hidden, lowered, outed = (
            k.sem(f"{name}_v{x}") for x in ("turned", "copied", "lifted", "gates", "hidden", "lowered", "outed"))
        LOADS = 3
        block = ctx.enter_context(nc.Block())

        @block.sync
        def _(sp):
            with sp.Fori(0, NT // 2) as i:
                for r in range(2):
                    n = i * 2 + r
                    sp.wait_ge(lowered, n + 1)
                    sp.dma_start(rows[r][:], visits[ds(n * ROWS, ROWS), :].rearrange("(c p) d -> p c d", p=128)).then_inc(rowed[r], 16)
                    e = sp.value_load(expert_of[0:1, ds(n, 1)], min_val=0, max_val=E - 1)
                    sp.dma_start(w1[r][:], w_in1[ds(e, 1)].rearrange("o (a p) n -> p (o a) n", p=H2)).then_inc(loaded[r], 16)
                    if gated:
                        sp.dma_start(w2[r][:], w_in2[ds(e, 1)].rearrange("o (a p) n -> p (o a) n", p=H2)).then_inc(loaded[r], 16)
                    else:
                        sp.dma_start(bias[r][:], b1[ds(e, 1)].rearrange("o p c -> p (o c)")).then_inc(loaded[r], 16)
                    sp.dma_start(wd[r][:], w_down[ds(e, 1)].rearrange("o (c p) n -> p (o c) n", p=128)).then_inc(loaded[r], 16)

        @block.tensor
        def _(pe):
            with pe.Fori(0, NT // 2) as i:
                for r in range(2):
                    pe.wait_ge(rowed[r], i * 16 + 16)
                    for d in range(2):
                        for c in range(RC):
                            last = pe.transpose(pt[r][0:H2, d * ROWS + c * 128:d * ROWS + c * 128 + 128],
                                                rows[r][:, c, d * H2:d * H2 + H2], k.ident[:])
                    last.then_inc(turned, 1)
                for r in range(2):
                    n = i * 2 + r
                    pe.wait_ge(loaded[r], (i + 1) * (16 * LOADS))
                    pe.wait_ge(copied, n + 1)
                    for j in range(FC):
                        pe.wait_ge(hidden, n * FC + j + 1)
                        for a, w in enumerate((w1, w2) if gated else (w1,)):
                            for d in range(2):
                                last = pe.matmul(pg[j % 3][:, a * ROWS:(a + 1) * ROWS], w[r][:, d, j * 128:(j + 1) * 128],
                                                 xT[r][:, d, :], start=(d == 0), stop=(d == 1))
                        last.then_inc(lifted, 1)
                for r in range(2):
                    n = i * 2 + r
                    pe.wait_ge(hidden, (n + 1) * FC + 3)
                    pe.wait_ge(outed, n + 1)
                    for c in range(RC):
                        for j in range(FC):
                            last = pe.matmul(po[r][:, c * D:c * D + D], hid[r][:, j, c * 128:c * 128 + 128],
                                             wd[r][:, j, :], start=(j == 0), stop=(j == FC - 1))
                    last.then_inc(lowered, 1)

        @block.scalar
        def _(act):
            with act.Fori(0, NT // 2) as i:
                for r in range(2):
                    act.wait_ge(turned, i * 2 + r + 1)
                    nc.scalar.activation(xT[r][:], pt[r][0:H2, :].rearrange("p (a n) -> p a n", a=2), ACT.Copy).then_inc(copied, 1)
                for r in range(2):
                    n = i * 2 + r
                    for j in range(FC):
                        act.wait_ge(lifted, n * FC + j + 1)
                        if gated:
                            act.wait_ge(hidden, n * FC + j + 2)
                            nc.scalar.activation(silu[j % 2][:], pg[j % 3][:, 0:ROWS], ACT.Silu).then_inc(gates, 1)
                        else:
                            nc.scalar.activation(hid[r][:, j, :], pg[j % 3][:, 0:ROWS], ACT.Gelu,
                                                 bias=bias[r][:, j:j + 1]).then_inc(hidden, 1)
                for r in range(2):
                    act.wait_ge(outed, 2 + i * 2 + r + 1)
                    act.dma_start(answers[ds((i * 2 + r) * ROWS, ROWS), :].rearrange("(c p) d -> p c d", p=128),
                                  out[r][:]).then_inc(stored[r], 16)
            for r in range(2):
                act.wait_ge(stored[r], 16 + 16 * (NT // 2))

        @block.vector
        def _(dve):
            for at, (of, ahead) in enumerate(((stored[0], 16), (stored[1], 16), (lowered, 2), (outed, 2), (hidden, 3))):
                nc.vector.memset(out[0][:, 0, at:at + 1], 0.0).then_inc(of, ahead)
            with dve.Fori(0, NT // 2) as i:
                for r in range(2):
                    n = i * 2 + r
                    if gated:
                        for j in range(FC):
                            dve.wait_ge(gates, n * FC + j + 1)
                            nc.vector.tensor_tensor(hid[r][:, j, :], silu[j % 2][:], pg[j % 3][:, ROWS:2 * ROWS],
                                                    ALU.mult).then_inc(hidden, 1)
                for r in range(2):
                    n = i * 2 + r
                    dve.wait_ge(lowered, 2 + n + 1)
                    dve.wait_ge(stored[r], i * 16 + 16)
                    nc.vector.tensor_copy(out[r][:], po[r][:, 0:RC * D].rearrange("p (c d) -> p c d", c=RC)).then_inc(outed, 1)


def collect(k, name, answers, wts, place_of, parts=4):
    nc, h = k.nc, k.h
    with ExitStack() as ctx:
        got = [k.sb(f"{name}_got{r}", [H2, TILES, D], ctx=ctx) for r in range(2)]
        come = [k.sem(f"{name}_come{p}") for p in range(parts)]
        scaled, added = k.sem(f"{name}_scaled"), k.sem(f"{name}_added")
        n = TILES // parts
        block = ctx.enter_context(nc.Block())

        @block.gpsimd
        def _(pool):
            for t in range(TILES):
                for r in range(2):
                    pool.indirect_dma_start(out=got[r][:, t, :], out_offset=None, in_=answers,
                                            in_offset=bass.IndirectOffsetOnAxis(ap=place_of[:, r, t:t + 1], axis=0)
                                            ).then_inc(come[t // n], 16)

        @block.vector
        def _(dve):
            for p in range(parts):
                at = slice(p * n, p * n + n)
                dve.wait_ge(come[p], 32 * n)
                for r in range(2):
                    nc.vector.tensor_tensor(got[r][:, at, :], got[r][:, at, :],
                                            wts[r][:, at].unsqueeze(2).broadcast_to([H2, n, D]), ALU.mult).then_inc(scaled, 1)
                for r in range(2):
                    dve.wait_ge(scaled, 2 * p + r + 1)
                    if r:
                        dve.wait_ge(added, p + 1)
                    ins = nc.vector.tensor_tensor(h[:, at, :], h[:, at, :], got[r][:, at, :], ALU.add)
                    if not r:
                        ins.then_inc(added, 1)


def moe(k, name, E, visits, routerT, w_in1, w_in2, w_down, b1, b2):
    answers = k.nc.dram_tensor(f"{name}_answers", (tiles_of(E) * ROWS, D), F32, kind="Internal").ap()
    with ExitStack() as ctx:
        logits = k.sb(f"{name}_logits", [H2, TILES, E], ctx=ctx)
        gate = k.sb(f"{name}_gate", [H2, TILES, E], ctx=ctx)
        wts = [k.sb(f"{name}_wts{r}", [H2, TILES], ctx=ctx) for r in range(2)]
        place_of = k.sb(f"{name}_place_of", [H2, 2, TILES], U32, ctx=ctx)
        expert_of = k.sb(f"{name}_expert_of", [H2, tiles_of(E)], U32, ctx=ctx)
        norm_and_score(k, name, routerT, logits, E, keep=b2 is not None)
        route(k, name, logits, gate, wts, place_of, expert_of, E, probs_first=b2 is not None)
        send(k, name, visits, place_of)
        if b2 is not None:
            add_expert_biases(k, name, gate, b2, E)
        experts(k, name, visits, answers, expert_of, E, w_in1, w_in2, w_down, b1)
        collect(k, name, answers, wts, place_of)



PAD = GROUPS * 128
ROUNDS = 4
HR = HEADS // ROUNDS


def head_rows(x, hd):
    j = hd % 4
    return x[32 * j:32 * j + 32, hd // 4, :]


def project_padded(pe, bank, xT, wqk, wv):
    for g in range(GROUPS):
        for which in range(2):
            c = which * PAD + g * 128
            for d in range(2):
                pe.matmul(bank[:, g, which * N:which * N + N], wqk[:, d, c:c + 128], xT[:, d, :],
                          start=(d == 0), stop=(d == 1))
    for t in range(2):
        for d in range(2):
            last = pe.matmul(bank[0:H2, 3, t * D:t * D + D], xT[:, d, t * H2:t * H2 + H2], wv[:, d, :],
                             start=(d == 0), stop=(d == 1))
    return last


def times_turned(pe, out, turned_rows, w):
    for t in range(2):
        for d in range(2):
            last = pe.matmul(out[:, t, :], turned_rows[:, d, t * H2:t * H2 + H2], w[:, d, :],
                             start=(d == 0), stop=(d == 1))
    return last



def attention1(k, wqk_src, wv_src, wproj_src, bias_src, steps_src):
    nc, h = k.nc, k.h
    LO, HI, TOP = -4.0, 3.0, 7.0
    with ExitStack() as ctx:
        wqk = k.sb("a1_wqk", [H2, 2, 2 * PAD], ctx=ctx)
        wv = k.sb("a1_wv", [H2, 2, D], ctx=ctx)
        wp = k.sb("a1_wp", [H2, 2, D], ctx=ctx)
        bias = k.sb("a1_bias", [H2, D], ctx=ctx)
        s = k.sb("a1_s", [128, 5], ctx=ctx)
        inv = k.sb("a1_inv", [128, 5], ctx=ctx)
        fac = k.sb("a1_fac", [128, 4], ctx=ctx)

        def lanes(name, shape, dt=F32):
            return [k.sb(f"a1_{name}{u}", shape, dt, ctx=ctx) for u in range(LANES)]

        rows, xT = lanes("rows", [H2, 2, D]), lanes("xT", [H2, 2, D])
        qk_s, qk_c = lanes("qk_s", [128, 2 * GROUPS, N]), lanes("qk_c", [128, 2 * GROUPS, N])
        qk = lanes("qk", [128, 2 * GROUPS, N], BF16)
        v_s, v_c = lanes("v_s", [H2, 2, D]), lanes("v_c", [H2, 2, D])
        v = lanes("v", [H2, 2, D], BF16)
        at_s, at_c = lanes("at_s", [H2, HR, 2 * N]), lanes("at_c", [H2, HR, 2 * N])
        at = lanes("at", [H2, HR, 2 * N], BF16)
        o_s, o_c, o = lanes("o_s", [H2, 2, D]), lanes("o_c", [H2, 2, D]), lanes("o", [H2, 2, D])
        oT = lanes("oT", [H2, 2, D])
        bank = [k.ps(f"a1_bank{u}", [128, 4, 512], ctx) for u in range(LANES)]
        S = {x: k.sem(f"a1_{x}") for x in (
            "loaded", "consts", "biased", "rows", "turned", "xT", "qkv", "scaled", "clipped", "qkv_ready", "scores",
            "at_scaled", "at_clipped", "at_ready", "out", "o_scaled", "o_clipped", "o_ready", "o_turned",
            "oT", "projected")}
        block = ctx.enter_context(nc.Block())

        def both(u, j):
            return split2(bank[u][0:H2, j, 0:2 * D])

        @block.sync
        def _(sp):
            sp.dma_start(wqk[:], halves(wqk_src)).then_inc(S["loaded"], 16)
            sp.dma_start(wv[:], halves(wv_src)).then_inc(S["loaded"], 16)
            sp.dma_start(wp[:], halves(wproj_src)).then_inc(S["loaded"], 16)
            sp.dma_start(bias[:], bias_src.broadcast_to([H2, D])).then_inc(S["loaded"], 16)
            sp.dma_start(s[:], steps_src.broadcast_to([128, 5])).then_inc(S["loaded"], 16)

        @block.gpsimd
        def _(pool):
            pool.wait_ge(S["loaded"], 80)
            nc.gpsimd.tensor_tensor(h[:], h[:], bias[:].unsqueeze(1).broadcast_to([H2, TILES, D]),
                                    ALU.add).then_inc(S["biased"], 1)

        @block.tensor
        def _(pe):
            pe.wait_ge(S["loaded"], 80)
            with pe.Fori(0, TURNS) as i:
                for u in range(LANES):
                    pe.wait_ge(S["rows"], i * LANES + u + 1)
                    turn(pe, k, bank[u][0:H2, 3, :], rows[u]).then_inc(S["turned"], 1)
                for u in range(LANES):
                    pe.wait_ge(S["xT"], i * LANES + u + 1)
                    project_padded(pe, bank[u], xT[u], wqk, wv).then_inc(S["qkv"], 1)
                for r in range(ROUNDS):
                    for u in range(LANES):
                        if r == 0:
                            pe.wait_ge(S["qkv_ready"], i * LANES + u + 1)
                        for n in range(HR):
                            hd = r * HR + n
                            q, kk = (head_rows(qk[u][:, w * GROUPS:(w + 1) * GROUPS, :], hd) for w in range(2))
                            for m in range(2):
                                last = pe.matmul(bank[u][0:H2, n, m * N:m * N + N], kk[:, m * H2:m * H2 + H2], q,
                                                 start=True, stop=True)
                        last.then_inc(S["scores"], 1)
                    for u in range(LANES):
                        pe.wait_ge(S["at_ready"], (i * ROUNDS + r) * LANES + u + 1)
                        for n in range(HR):
                            c = (r * HR + n) * DH
                            for t in range(2):
                                for m in range(2):
                                    last = pe.matmul(bank[u][0:H2, 3, t * D + c:t * D + c + DH],
                                                     at[u][:, n, m * N + t * H2:m * N + t * H2 + H2],
                                                     v[u][:, m, c:c + DH], start=(m == 0), stop=(m == 1))
                        if r == ROUNDS - 1:
                            last.then_inc(S["out"], 1)
                for u in range(LANES):
                    pe.wait_ge(S["o_ready"], i * LANES + u + 1)
                    turn(pe, k, bank[u][0:H2, 0, :], o[u]).then_inc(S["o_turned"], 1)
                for u in range(LANES):
                    pe.wait_ge(S["oT"], i * LANES + u + 1)
                    times_turned(pe, both(u, 1), oT[u], wp).then_inc(S["projected"], 1)

        @block.scalar
        def _(act):
            act.wait_ge(S["consts"], 2)
            with act.Fori(0, TURNS) as i:
                for u in range(LANES):
                    act.wait_ge(S["turned"], i * LANES + u + 1)
                    nc.scalar.activation(xT[u][:], both(u, 3), ACT.Copy).then_inc(S["xT"], 1)
                for u in range(LANES):
                    act.wait_ge(S["qkv"], i * LANES + u + 1)
                    for w in range(2):
                        nc.scalar.activation(qk_s[u][:, w * GROUPS:(w + 1) * GROUPS, :],
                                             bank[u][:, 0:GROUPS, w * N:w * N + N], ACT.Identity, scale=inv[:, w:w + 1])
                    nc.scalar.activation(v_s[u][:], both(u, 3), ACT.Identity, scale=inv[0:H2, 2:3]).then_inc(S["scaled"], 1)
                for r in range(ROUNDS):
                    for u in range(LANES):
                        act.wait_ge(S["scores"], (i * ROUNDS + r) * LANES + u + 1)
                        nc.scalar.activation(at_s[u][:], bank[u][0:H2, 0:HR, 0:2 * N], ACT.Relu,
                                             scale=fac[0:H2, 1:2]).then_inc(S["at_scaled"], 1)
                for u in range(LANES):
                    act.wait_ge(S["out"], i * LANES + u + 1)
                    nc.scalar.activation(o_s[u][:], both(u, 3), ACT.Identity, scale=fac[0:H2, 3:4]).then_inc(S["o_scaled"], 1)
                for u in range(LANES):
                    act.wait_ge(S["o_turned"], i * LANES + u + 1)
                    nc.scalar.activation(oT[u][:], both(u, 0), ACT.Copy).then_inc(S["oT"], 1)

        @block.vector
        def _(dve):
            def rounded(out, x):
                return nc.vector.tensor_scalar(out, x, ROUND, ROUND, ALU.add, ALU.subtract)

            dve.wait_ge(S["loaded"], 80)
            nc.vector.reciprocal(inv[:], s[:]).then_inc(S["consts"], 1)
            nc.vector.tensor_scalar(fac[:, 0:1], s[:, 0:1], s[:, 1:2], DH ** -0.5 / N, ALU.mult, ALU.mult)
            nc.vector.tensor_scalar(fac[:, 2:3], s[:, 3:4], s[:, 2:3], None, ALU.mult).then_inc(S["clipped"], LANES)
            dve.wait_ge(S["consts"], 1)
            dve.wait_ge(S["clipped"], LANES)
            nc.vector.tensor_scalar(fac[:, 1:2], fac[:, 0:1], inv[:, 3:4], None, ALU.mult)
            nc.vector.tensor_scalar(fac[:, 3:4], fac[:, 2:3], inv[:, 4:5], None, ALU.mult).then_inc(S["consts"], 1)
            with dve.Fori(0, TURNS) as i:
                for u in range(LANES):
                    normed_rows(k, rows[u], i, u).then_inc(S["rows"], 1)
                for u in range(LANES):
                    dve.wait_ge(S["scaled"], i * LANES + u + 1)
                    nc.vector.tensor_scalar(qk_c[u][:], qk_s[u][:], LO, HI, ALU.max, ALU.min)
                    nc.vector.tensor_scalar(v_c[u][:], v_s[u][:], LO, HI, ALU.max, ALU.min).then_inc(S["clipped"], 1)
                for u in range(LANES):
                    dve.wait_ge(S["clipped"], LANES + i * LANES + u + 1)
                    rounded(qk[u][:], qk_c[u][:])
                    rounded(v[u][:], v_c[u][:]).then_inc(S["qkv_ready"], 1)
                for r in range(ROUNDS):
                    for u in range(LANES):
                        n = (i * ROUNDS + r) * LANES + u
                        dve.wait_ge(S["at_scaled"], n + 1)
                        nc.vector.tensor_scalar(at_c[u][:], at_s[u][:], TOP, ROUND, ALU.min, ALU.add).then_inc(S["at_clipped"], 1)
                        dve.wait_ge(S["at_clipped"], n + 1)
                        nc.vector.tensor_scalar(at[u][:], at_c[u][:], ROUND, None, ALU.subtract).then_inc(S["at_ready"], 1)
                for u in range(LANES):
                    dve.wait_ge(S["o_scaled"], i * LANES + u + 1)
                    nc.vector.tensor_scalar(o_c[u][:], o_s[u][:], LO, HI, ALU.max, ALU.min).then_inc(S["o_clipped"], 1)
                for u in range(LANES):
                    dve.wait_ge(S["o_clipped"], i * LANES + u + 1)
                    rounded(o[u][:], o_c[u][:]).then_inc(S["o_ready"], 1)
                for u in range(LANES):
                    dve.wait_ge(S["projected"], i * LANES + u + 1)
                    dve.wait_ge(S["biased"], 1)
                    hb = h[:, ds((i * LANES + u) * 2, 2), :]
                    nc.vector.scalar_tensor_tensor(out=hb, in0=both(u, 1), scalar=s[0:H2, 4:5], in1=hb,
                                                   op0=ALU.mult, op1=ALU.add)



VA = DH + 1


def attention3(k, wqk_src, wv_src, wproj_src, bias_src):
    nc, h = k.nc, k.h
    SCALE = DH ** -0.5
    with ExitStack() as ctx:
        wqk = k.sb("a3_wqk", [H2, 2, 2 * PAD], ctx=ctx)
        wv = k.sb("a3_wv", [H2, 2, D], ctx=ctx)
        wp = k.sb("a3_wp", [H2, 2, D], ctx=ctx)
        bias = k.sb("a3_bias", [H2, D], ctx=ctx)

        def lanes(name, shape, dt=F32):
            return [k.sb(f"a3_{name}{u}", shape, dt, ctx=ctx) for u in range(LANES)]

        rows, xT = lanes("rows", [H2, 2, D]), lanes("xT", [H2, 2, D])
        qT, kT = lanes("qT", [128, GROUPS, N]), lanes("kT", [128, GROUPS, N])
        v = lanes("v", [H2, 2, HEADS, VA])
        top = lanes("top", [H2, HR, 2])
        below, prob, probT = (lanes(x, [H2, HR, 2 * N]) for x in ("below", "prob", "probT"))
        rden, o, oT = lanes("rden", [H2, 2, HEADS]), lanes("o", [H2, 2, D]), lanes("oT", [H2, 2, D])
        bank = [k.ps(f"a3_bank{u}", [128, 4, 512], ctx) for u in range(LANES)]
        S = {x: k.sem(f"a3_{x}") for x in (
            "loaded", "biased", "ones", "rows", "turned", "xT", "qkv", "qkv_copied", "scores", "top", "below",
            "prob", "p_turned", "probT", "out", "rden", "o", "o_turned", "oT", "projected")}
        block = ctx.enter_context(nc.Block())

        def both(u, j):
            return split2(bank[u][0:H2, j, 0:2 * D])

        def three(u):
            return bank[u][0:H2, 0:HR, 0:2 * N]

        def sums(u):
            return bank[u][0:H2, 3, 0:2 * HEADS * VA].rearrange("p (t h e) -> p t h e", t=2, h=HEADS)

        @block.sync
        def _(sp):
            sp.dma_start(wqk[:], halves(wqk_src)).then_inc(S["loaded"], 16)
            sp.dma_start(wv[:], halves(wv_src)).then_inc(S["loaded"], 16)
            sp.dma_start(wp[:], halves(wproj_src)).then_inc(S["loaded"], 16)
            sp.dma_start(bias[:], bias_src.broadcast_to([H2, D])).then_inc(S["loaded"], 16)

        @block.gpsimd
        def _(pool):
            for u in range(LANES):
                nc.gpsimd.memset(v[u][:], 1.0).then_inc(S["ones"], 1)
            pool.wait_ge(S["loaded"], 64)
            nc.gpsimd.tensor_tensor(h[:], h[:], bias[:].unsqueeze(1).broadcast_to([H2, TILES, D]),
                                    ALU.add).then_inc(S["biased"], 1)

        @block.tensor
        def _(pe):
            pe.wait_ge(S["loaded"], 64)
            with pe.Fori(0, TURNS) as i:
                for u in range(LANES):
                    pe.wait_ge(S["rows"], i * LANES + u + 1)
                    turn(pe, k, bank[u][0:H2, 3, :], rows[u]).then_inc(S["turned"], 1)
                for u in range(LANES):
                    pe.wait_ge(S["xT"], i * LANES + u + 1)
                    project_padded(pe, bank[u], xT[u], wqk, wv).then_inc(S["qkv"], 1)
                for r in range(ROUNDS):
                    for u in range(LANES):
                        if r == 0:
                            pe.wait_ge(S["qkv_copied"], i * LANES + u + 1)
                        for n in range(HR):
                            q, kk = head_rows(qT[u], r * HR + n), head_rows(kT[u], r * HR + n)
                            for t in range(2):
                                last = pe.matmul(bank[u][0:H2, n, t * N:t * N + N], q[:, t * H2:t * H2 + H2], kk,
                                                 start=True, stop=True)
                        last.then_inc(S["scores"], 1)
                    for u in range(LANES):
                        pe.wait_ge(S["prob"], (i * ROUNDS + r) * LANES + u + 1)
                        for n in range(HR):
                            last = turn(pe, k, bank[u][0:H2, n, :], split2(prob[u][:, n, :]))
                        last.then_inc(S["p_turned"], 1)
                    for u in range(LANES):
                        pe.wait_ge(S["probT"], (i * ROUNDS + r) * LANES + u + 1)
                        for n in range(HR):
                            hd = r * HR + n
                            for t in range(2):
                                for m in range(2):
                                    last = pe.matmul(sums(u)[:, t, hd, :],
                                                     probT[u][:, n, m * N + t * H2:m * N + t * H2 + H2],
                                                     v[u][:, m, hd, :], start=(m == 0), stop=(m == 1))
                        if r == ROUNDS - 1:
                            last.then_inc(S["out"], 1)
                for u in range(LANES):
                    pe.wait_ge(S["o"], i * LANES + u + 1)
                    turn(pe, k, bank[u][0:H2, 0, :], o[u]).then_inc(S["o_turned"], 1)
                for u in range(LANES):
                    pe.wait_ge(S["oT"], i * LANES + u + 1)
                    times_turned(pe, both(u, 1), oT[u], wp).then_inc(S["projected"], 1)

        @block.scalar
        def _(act):
            act.wait_ge(S["ones"], LANES)
            with act.Fori(0, TURNS) as i:
                for u in range(LANES):
                    act.wait_ge(S["turned"], i * LANES + u + 1)
                    nc.scalar.activation(xT[u][:], both(u, 3), ACT.Copy).then_inc(S["xT"], 1)
                for u in range(LANES):
                    act.wait_ge(S["qkv"], i * LANES + u + 1)
                    nc.scalar.activation(qT[u][:], bank[u][:, 0:GROUPS, 0:N], ACT.Copy)
                    nc.scalar.activation(kT[u][:], bank[u][:, 0:GROUPS, N:2 * N], ACT.Copy)
                    nc.scalar.activation(v[u][:, :, :, 0:DH], both(u, 3).rearrange("p t (h e) -> p t h e", h=HEADS),
                                         ACT.Copy).then_inc(S["qkv_copied"], 1)
                for r in range(ROUNDS):
                    for u in range(LANES):
                        act.wait_ge(S["below"], (i * ROUNDS + r) * LANES + u + 1)
                        nc.scalar.activation(prob[u][:], below[u][:], ACT.Exp, scale=SCALE).then_inc(S["prob"], 1)
                    for u in range(LANES):
                        act.wait_ge(S["p_turned"], (i * ROUNDS + r) * LANES + u + 1)
                        nc.scalar.activation(probT[u][:], three(u), ACT.Copy).then_inc(S["probT"], 1)
                for u in range(LANES):
                    act.wait_ge(S["o_turned"], i * LANES + u + 1)
                    nc.scalar.activation(oT[u][:], both(u, 0), ACT.Copy).then_inc(S["oT"], 1)

        @block.vector
        def _(dve):
            with dve.Fori(0, TURNS) as i:
                for u in range(LANES):
                    normed_rows(k, rows[u], i, u).then_inc(S["rows"], 1)
                for r in range(ROUNDS):
                    for u in range(LANES):
                        n = (i * ROUNDS + r) * LANES + u
                        dve.wait_ge(S["scores"], n + 1)
                        s4 = three(u).rearrange("p n (t m) -> p n t m", t=2)
                        nc.vector.tensor_reduce(top[u][:], s4, AXX, ALU.max).then_inc(S["top"], 1)
                        dve.wait_ge(S["top"], n + 1)
                        nc.vector.tensor_tensor(below[u][:].rearrange("p n (t m) -> p n t m", t=2), s4,
                                                top[u][:].unsqueeze(3).broadcast_to([H2, HR, 2, N]),
                                                ALU.subtract).then_inc(S["below"], 1)
                for u in range(LANES):
                    dve.wait_ge(S["out"], i * LANES + u + 1)
                    nc.vector.reciprocal(rden[u][:], sums(u)[:, :, :, DH]).then_inc(S["rden"], 1)
                    dve.wait_ge(S["rden"], i * LANES + u + 1)
                    nc.vector.tensor_tensor(o[u][:].rearrange("p t (h e) -> p t h e", h=HEADS),
                                            sums(u)[:, :, :, 0:DH],
                                            rden[u][:].unsqueeze(3).broadcast_to([H2, 2, HEADS, DH]),
                                            ALU.mult).then_inc(S["o"], 1)
                for u in range(LANES):
                    dve.wait_ge(S["projected"], i * LANES + u + 1)
                    dve.wait_ge(S["biased"], 1)
                    hb = h[:, ds((i * LANES + u) * 2, 2), :]
                    nc.vector.tensor_tensor(hb, both(u, 1), hb, ALU.add)



FEATURES = 64
HALF_HEADS = HEADS // 2
PAIRS = HEADS // 2


def attention2(k, wqkv_src, feat_src, wproj_src, bias_src):
    nc, cent = k.nc, k.cent
    EPS_N = 1e-6 * FEATURES
    with ExitStack() as ctx:
        w = k.sb("a2_w", [H2, 2, 3 * D], ctx=ctx)
        wp = k.sb("a2_wp", [H2, 2, D], ctx=ctx)
        bias = k.sb("a2_bias", [H2, D], ctx=ctx)
        feat = k.sb("a2_feat", [H2, HALF_HEADS * FEATURES], ctx=ctx)
        less = k.sb("a2_less", [H2, HALF_HEADS * FEATURES], ctx=ctx)

        def lanes(name, shape, dt=F32):
            return [k.sb(f"a2_{name}{u}", shape, dt, ctx=ctx) for u in range(LANES)]

        rows, xT, qT, kT, q2, k2 = (lanes(x, [H2, 2, D]) for x in ("rows", "xT", "qT", "kT", "q2", "k2"))
        v = lanes("v", [H2, 2, HEADS, VA])
        qp = lanes("qp", [128, PAIRS, N])
        kp = lanes("kp", [H2, 2, HEADS * FEATURES])
        kv = lanes("kv", [128, PAIRS, 2 * VA])
        den, rden = lanes("den", [H2, 2, HEADS]), lanes("rden", [H2, 2, HEADS])
        o, oT, y = lanes("o", [H2, 2, D]), lanes("oT", [H2, 2, D]), lanes("y", [H2, 2, D])
        bank = [k.ps(f"a2_bank{u}", [128, 4, 512], ctx) for u in range(LANES)]
        S = {x: k.sem(f"a2_{x}") for x in (
            "loaded", "preset", "rows", "turned", "xT", "qkv", "copied", "q_feat", "qp", "k_feat", "kp", "kv_sums",
            "kv", "out", "den", "rden", "o", "o_turned", "oT", "projected", "y")}
        block = ctx.enter_context(nc.Block())

        def both(u, j):
            return split2(bank[u][0:H2, j, 0:2 * D])

        def sums(u):
            return bank[u][0:H2, 1, 0:2 * HEADS * VA].rearrange("p (t h e) -> p t h e", t=2, h=HEADS)

        @block.sync
        def _(sp):
            sp.dma_start(w[:], halves(wqkv_src)).then_inc(S["loaded"], 16)
            sp.dma_start(wp[:], halves(wproj_src)).then_inc(S["loaded"], 16)
            sp.dma_start(bias[:], bias_src.broadcast_to([H2, D])).then_inc(S["loaded"], 16)
            sp.dma_start(feat[:], feat_src[0]).then_inc(S["loaded"], 16)
            sp.dma_start(less[:], feat_src[1]).then_inc(S["loaded"], 16)

        @block.gpsimd
        def _(pool):
            for u in range(LANES):
                nc.gpsimd.memset(v[u][:], 1.0).then_inc(S["preset"], 1)
                nc.gpsimd.memset(kv[u][:], 0.0).then_inc(S["preset"], 1)

        @block.tensor
        def _(pe):
            pe.wait_ge(S["loaded"], 80)
            with pe.Fori(0, TURNS) as i:
                for u in range(LANES):
                    pe.wait_ge(S["rows"], i * LANES + u + 1)
                    turn(pe, k, bank[u][0:H2, 0, :], rows[u]).then_inc(S["turned"], 1)
                for u in range(LANES):
                    pe.wait_ge(S["xT"], i * LANES + u + 1)
                    for j in range(2):
                        for e in range(2):
                            for d in range(2):
                                c = j * D + e * H2
                                pe.matmul(both(u, j)[:, e, :], w[:, d, c:c + H2], xT[u][:, d, :],
                                          start=(d == 0), stop=(d == 1))
                    times_turned(pe, both(u, 2), xT[u], w[:, :, 2 * D:3 * D]).then_inc(S["qkv"], 1)
                for u in range(LANES):
                    pe.wait_ge(S["copied"], i * LANES + u + 1)
                    for pair in range(PAIRS):
                        e, c = pair // 3, pair % 3 * 128
                        out = bank[u][:, pair // 2, pair % 2 * N:pair % 2 * N + N]
                        pe.matmul(out, feat[:, c:c + 128], qT[u][:, e, :], start=True, stop=False)
                        last = pe.matmul(out, less[:, c:c + 128], q2[u][:, e, :], start=False, stop=True)
                    last.then_inc(S["q_feat"], 1)
                for u in range(LANES):
                    pe.wait_ge(S["qp"], i * LANES + u + 1)
                    for t in range(2):
                        for e in range(2):
                            out = bank[u][0:H2, 2 * t + e, 0:384]
                            pe.matmul(out, kT[u][:, e, t * H2:t * H2 + H2], feat[:], start=True, stop=False)
                            last = pe.matmul(out, k2[u][:, e, t * H2:t * H2 + H2], less[:], start=False, stop=True)
                    last.then_inc(S["k_feat"], 1)
                for u in range(LANES):
                    pe.wait_ge(S["kp"], i * LANES + u + 1)
                    for pair in range(PAIRS):
                        for m in range(2):
                            last = pe.matmul(bank[u][:, 0, pair * 2 * VA:(pair + 1) * 2 * VA],
                                             kp[u][:, m, pair * 128:pair * 128 + 128],
                                             v[u][:, m, 2 * pair:2 * pair + 2, :].rearrange("p h e -> p (h e)"),
                                             start=(m == 0), stop=(m == 1))
                    last.then_inc(S["kv_sums"], 1)
                for u in range(LANES):
                    pe.wait_ge(S["kv"], i * LANES + u + 1)
                    for t in range(2):
                        for pair in range(PAIRS):
                            c = (t * PAIRS + pair) * 2 * VA
                            last = pe.matmul(bank[u][0:H2, 1, c:c + 2 * VA], qp[u][:, pair, t * H2:t * H2 + H2],
                                             kv[u][:, pair, :], start=True, stop=True)
                    last.then_inc(S["out"], 1)
                for u in range(LANES):
                    pe.wait_ge(S["o"], i * LANES + u + 1)
                    turn(pe, k, bank[u][0:H2, 2, :], o[u]).then_inc(S["o_turned"], 1)
                for u in range(LANES):
                    pe.wait_ge(S["oT"], i * LANES + u + 1)
                    times_turned(pe, both(u, 3), oT[u], wp).then_inc(S["projected"], 1)

        @block.scalar
        def _(act):
            act.wait_ge(S["preset"], 2 * LANES)
            with act.Fori(0, TURNS) as i:
                for u in range(LANES):
                    act.wait_ge(S["turned"], i * LANES + u + 1)
                    nc.scalar.activation(xT[u][:], both(u, 0), ACT.Copy).then_inc(S["xT"], 1)
                for u in range(LANES):
                    act.wait_ge(S["qkv"], i * LANES + u + 1)
                    nc.scalar.activation(qT[u][:], both(u, 0), ACT.Copy)
                    nc.scalar.activation(kT[u][:], both(u, 1), ACT.Copy)
                    nc.scalar.activation(q2[u][:], both(u, 0), ACT.Square)
                    nc.scalar.activation(k2[u][:], both(u, 1), ACT.Square)
                    nc.scalar.activation(v[u][:, :, :, 0:DH], both(u, 2).rearrange("p t (h e) -> p t h e", h=HEADS),
                                         ACT.Copy).then_inc(S["copied"], 1)
                for u in range(LANES):
                    act.wait_ge(S["q_feat"], i * LANES + u + 1)
                    nc.scalar.activation(qp[u][:].rearrange("p (b a) n -> p b (a n)", a=2),
                                         bank[u][:, 0:3, 0:2 * N], ACT.Exp).then_inc(S["qp"], 1)
                for u in range(LANES):
                    act.wait_ge(S["k_feat"], i * LANES + u + 1)
                    nc.scalar.activation(kp[u][:].rearrange("p t (e n) -> p (t e) n", e=2),
                                         bank[u][0:H2, :, 0:384], ACT.Exp).then_inc(S["kp"], 1)
                for u in range(LANES):
                    act.wait_ge(S["o_turned"], i * LANES + u + 1)
                    nc.scalar.activation(oT[u][:], both(u, 2), ACT.Copy).then_inc(S["oT"], 1)

        @block.vector
        def _(dve):
            dve.wait_ge(S["preset"], 2 * LANES)
            with dve.Fori(0, TURNS) as i:
                for u in range(LANES):
                    normed_rows(k, rows[u], i, u).then_inc(S["rows"], 1)
                for u in range(LANES):
                    dve.wait_ge(S["kv_sums"], i * LANES + u + 1)
                    src = bank[u][:, 0, 0:PAIRS * 2 * VA].rearrange("p (a e) -> p a e", a=PAIRS)
                    nc.vector.tensor_copy(kv[u][0:64, :, 0:VA], src[0:64, :, 0:VA])
                    nc.vector.tensor_copy(kv[u][64:128, :, VA:2 * VA], src[64:128, :, VA:2 * VA]).then_inc(S["kv"], 1)
                for u in range(LANES):
                    dve.wait_ge(S["out"], i * LANES + u + 1)
                    nc.vector.tensor_scalar(den[u][:], sums(u)[:, :, :, DH], EPS_N, None, ALU.add).then_inc(S["den"], 1)
                    dve.wait_ge(S["den"], i * LANES + u + 1)
                    nc.vector.reciprocal(rden[u][:], den[u][:]).then_inc(S["rden"], 1)
                    dve.wait_ge(S["rden"], i * LANES + u + 1)
                    nc.vector.tensor_tensor(o[u][:].rearrange("p t (h e) -> p t h e", h=HEADS),
                                            sums(u)[:, :, :, 0:DH],
                                            rden[u][:].unsqueeze(3).broadcast_to([H2, 2, HEADS, DH]),
                                            ALU.mult).then_inc(S["o"], 1)
                for u in range(LANES):
                    dve.wait_ge(S["projected"], i * LANES + u + 1)
                    nc.vector.tensor_tensor(y[u][:], both(u, 3), rows[u][:], ALU.add).then_inc(S["y"], 1)
                    dve.wait_ge(S["y"], i * LANES + u + 1)
                    nc.vector.tensor_tensor(cent[:, ds((i * LANES + u) * 2, 2), :], y[u][:],
                                            bias[:].unsqueeze(1).broadcast_to([H2, 2, D]), ALU.add)


def add_normed(k, gamma_src, beta_src, parts=4):
    nc, h, cent = k.nc, k.h, k.cent
    with ExitStack() as ctx:
        gamma = k.sb("gamma", [H2, D], ctx=ctx)
        beta = k.sb("beta", [H2, D], ctx=ctx)
        scaled = k.sb("an_scaled", [H2, TILES, D], ctx=ctx)
        loaded, step, moved = k.sem("an_loaded"), k.sem("an_step"), k.sem("an_moved")
        n = TILES // parts
        block = ctx.enter_context(nc.Block())

        @block.sync
        def _(sp):
            sp.dma_start(gamma[:], gamma_src.broadcast_to([H2, D])).then_inc(loaded, 16)
            sp.dma_start(beta[:], beta_src.broadcast_to([H2, D])).then_inc(loaded, 16)

        @block.gpsimd
        def _(pool):
            pool.wait_ge(loaded, 32)
            for p in range(parts):
                at = slice(p * n, p * n + n)
                nc.gpsimd.tensor_tensor(h[:, at, :], h[:, at, :], beta[:].unsqueeze(1).broadcast_to([H2, n, D]),
                                        ALU.add).then_inc(moved, 1)

        @block.vector
        def _(dve):
            for p in range(parts):
                at = slice(p * n, p * n + n)
                nc.vector.tensor_tensor(scaled[:, at, :], cent[:, at, :],
                                        k.rstd[:, at].unsqueeze(2).broadcast_to([H2, n, D]), ALU.mult).then_inc(step, 1)
            dve.wait_ge(loaded, 32)
            for p in range(parts):
                at = slice(p * n, p * n + n)
                dve.wait_ge(step, p + 1)
                nc.vector.tensor_tensor(cent[:, at, :], scaled[:, at, :], gamma[:].unsqueeze(1).broadcast_to([H2, n, D]),
                                        ALU.mult).then_inc(step, 1)
            for p in range(parts):
                at = slice(p * n, p * n + n)
                dve.wait_ge(step, parts + p + 1)
                dve.wait_ge(moved, p + 1)
                nc.vector.tensor_tensor(h[:, at, :], h[:, at, :], cent[:, at, :], ALU.add)



NODES = 21
DEPTH = 11


def walk_tree(k, logits, coeff):
    nc = k.nc
    LAST = NODES - 1
    with ExitStack() as ctx:
        def big(x, n=NODES):
            return k.sb(f"tree_{x}", [H2, TILES, n], ctx=ctx)

        seen, right, act, got = big("seen"), big("right"), big("gelu"), big("got")
        a, b = big("a", 1), big("b", 1)
        step, gelued = k.sem("tree_step"), k.sem("tree_gelued")
        block = ctx.enter_context(nc.Block())

        @block.scalar
        def _(eng):
            nc.scalar.activation(act[:], logits[:], ACT.Gelu).then_inc(gelued, 1)

        @block.vector
        def _(dve):
            done = [0]

            def link(ins):
                done[0] += 1
                ins.then_inc(step, 1)
                dve.wait_ge(step, done[0])

            tt = nc.vector.tensor_tensor
            link(nc.vector.tensor_scalar(right[:], logits[:], 0.0, None, ALU.is_gt))
            link(nc.vector.memset(coeff[:], 0.0))
            link(nc.vector.memset(seen[:], 1.0))
            dve.wait_ge(gelued, 1)
            first, level = 0, 0
            while first <= LAST:
                end = min(2 * first + 1, NODES)
                here = slice(first, end)
                link(tt(got[:, :, here], seen[:, :, here], act[:, :, here], ALU.mult))
                whole = min(end, (NODES - 1) // 2)
                if whole > first:
                    up = slice(first, whole)
                    lo, hi = 2 * first + 1, 2 * whole + 1
                    for x, out in ((seen, seen), (got, coeff)):
                        link(tt(out[:, :, lo + 1:hi:2], x[:, :, up], right[:, :, up], ALU.mult))
                        link(tt(out[:, :, lo:hi:2], x[:, :, up], out[:, :, lo + 1:hi:2], ALU.subtract))
                if end > max(whole, first):
                    up = slice(max(whole, first), end)
                    if 2 * first + 1 <= LAST:
                        link(nc.vector.tensor_reduce(a[:], seen[:, :, up], AXX, ALU.add))
                        link(tt(seen[:, :, LAST:NODES], seen[:, :, LAST:NODES], a[:], ALU.add))
                    link(nc.vector.tensor_reduce(b[:], got[:, :, up], AXX, ALU.add))
                    link(tt(coeff[:, :, LAST:NODES], coeff[:, :, LAST:NODES], b[:], ALU.add))
                first, level = 2 * first + 1, level + 1
            link(nc.vector.scalar_tensor_tensor(out=coeff[:, :, LAST:NODES], in0=act[:, :, LAST:NODES],
                                                scalar=float(DEPTH - 1 - level), in1=coeff[:, :, LAST:NODES],
                                                op0=ALU.mult, op1=ALU.add))


def tree_ffn(k, in_T, out_w):
    with ExitStack() as ctx:
        logits = k.sb("tree_logits", [H2, TILES, NODES], ctx=ctx)
        coeff = k.sb("tree_coeff", [H2, TILES, NODES], ctx=ctx)
        norm_and_score(k, "tree", in_T, logits, NODES, keep=False)
        walk_tree(k, logits, coeff)
        add_expert_biases(k, "tree", coeff, out_w, NODES)


EXPERTS3, PER = 64, 16
SLOTS = EXPERTS3 * PER



QUARTERS = 4
QE = EXPERTS3 // QUARTERS
QS = SLOTS // QUARTERS
QC = QS // 128
HID3 = 2 * D
HC3 = HID3 // 128
XA = D + 1


def slots_prepare(k, phiT, xnT, xr, phi, token_row):
    nc = k.nc
    EPS_PHI = 1e-6
    with ExitStack() as ctx:
        sq = k.sb("sp_sq", [H2, 2, SLOTS], ctx=ctx)
        norm, root, scale = (k.sb(f"sp_{x}", [H2, 2, PER], ctx=ctx) for x in ("norm", "root", "scale"))
        rows = [k.sb(f"sp_rows{u}", [H2, 2, D], ctx=ctx) for u in range(LANES)]
        xT = [k.sb(f"sp_xT{u}", [H2, 2, D], ctx=ctx) for u in range(LANES)]
        low = [k.sb(f"sp_low{u}", [H2, 2], ctx=ctx) for u in range(LANES)]
        bank = [k.ps(f"sp_bank{u}", [128, 4, 512], ctx) for u in range(LANES)]
        S = {x: k.sem(f"sp_{x}") for x in ("loaded", "squared", "normed", "step", "rooted", "scaled", "ones", "rows",
                                          "turned", "xT", "kept", "logits", "low", "low_turned")}
        raw = k.sb("sp_raw", [H2, 2, SLOTS], ctx=ctx)
        block = ctx.enter_context(nc.Block())

        @block.sync
        def _(sp):
            sp.dma_start(raw[:], halves(phiT)).then_inc(S["loaded"], 16)

        @block.scalar
        def _(act):
            act.wait_ge(S["loaded"], 16)
            nc.scalar.activation(sq[:], raw[:], ACT.Square).then_inc(S["squared"], 1)
            act.wait_ge(S["normed"], 1)
            nc.scalar.activation(root[:], norm[:], ACT.Sqrt).then_inc(S["rooted"], 1)
            with act.Fori(0, TURNS) as i:
                for u in range(LANES):
                    act.wait_ge(S["turned"], i * LANES + u + 1)
                    act.wait_ge(S["kept"], i * LANES + u + 1)
                    nc.scalar.activation(xT[u][:], split2(bank[u][0:H2, 0, 0:2 * D]), ACT.Copy).then_inc(S["xT"], 1)

        @block.gpsimd
        def _(pool):
            nc.gpsimd.memset(xr[:, :, D:XA], 1.0).then_inc(S["kept"], LANES)
            with pool.Fori(0, TURNS) as i:
                for u in range(LANES):
                    b = i * LANES + u
                    pool.wait_ge(S["rows"], b + 1)
                    nc.gpsimd.tensor_copy(xr[:, ds(b * 2, 2), 0:D], rows[u][:])
                    pool.wait_ge(S["xT"], b + 1)
                    nc.gpsimd.tensor_copy(xnT[:, :, ds(b * N, N)], xT[u][:]).then_inc(S["kept"], 1)

        @block.tensor
        def _(pe):
            with pe.Fori(0, TURNS) as i:
                for u in range(LANES):
                    pe.wait_ge(S["rows"], i * LANES + u + 1)
                    turn(pe, k, bank[u][0:H2, 0, :], rows[u]).then_inc(S["turned"], 1)
                for u in range(LANES):
                    pe.wait_ge(S["scaled"], 1)
                    pe.wait_ge(S["xT"], i * LANES + u + 1)
                    for t in range(2):
                        for s in range(2):
                            for d in range(2):
                                last = pe.matmul(bank[u][0:H2, 2 * t + s, :], xT[u][:, d, t * H2:t * H2 + H2],
                                                 phi[:, d, s * 512:s * 512 + 512], start=(d == 0), stop=(d == 1))
                    last.then_inc(S["logits"], 1)
                for u in range(LANES):
                    pe.wait_ge(S["low"], i * LANES + u + 1)
                    pe.transpose(bank[u][0:2, 0, 0:H2], low[u][:], k.ident[0:H2, 0:H2]).then_inc(S["low_turned"], 1)

        @block.vector
        def _(dve):
            dve.wait_ge(S["squared"], 1)
            nc.vector.tensor_reduce(scale[:], sq[:].rearrange("c a (n p) -> c a p n", p=PER), AXX, ALU.add).then_inc(S["step"], 1)
            dve.wait_ge(S["step"], 1)
            nc.vector.tensor_scalar(norm[:], scale[:], EPS_PHI, None, ALU.add).then_inc(S["normed"], 1)
            dve.wait_ge(S["rooted"], 1)
            nc.vector.reciprocal(scale[:], root[:]).then_inc(S["step"], 1)
            dve.wait_ge(S["step"], 2)
            for a in range(2):
                last = nc.vector.tensor_tensor(phi[:, a, :].rearrange("c (n p) -> c n p", p=PER),
                                               raw[:, a, :].rearrange("c (n p) -> c n p", p=PER),
                                               scale[:, a, :].unsqueeze(1).broadcast_to([H2, EXPERTS3, PER]), ALU.mult)
            last.then_inc(S["scaled"], 1)
            with dve.Fori(0, TURNS) as i:
                for u in range(LANES):
                    dve.wait_ge(S["kept"], i * LANES + u + 1)
                    normed_rows(k, rows[u], i, u).then_inc(S["rows"], 1)
                for u in range(LANES):
                    dve.wait_ge(S["logits"], i * LANES + u + 1)
                    nc.vector.tensor_reduce(low[u][:], bank[u][0:H2, :, :].rearrange("p (t s) n -> p t s n", t=2),
                                            mybir.AxisListType.XY, ALU.max, negate=True).then_inc(S["low"], 1)
                for u in range(LANES):
                    dve.wait_ge(S["low_turned"], i * LANES + u + 1)
                    b = i * LANES + u
                    nc.vector.tensor_tensor(token_row[:, ds(b, 1), :].rearrange("r o (t n) -> r (o t) n", t=2),
                                            bank[u][0:2, 0, 0:H2].unsqueeze(1).broadcast_to([2, 2, H2]),
                                            k.ident[0:2, 0:2].unsqueeze(2).broadcast_to([2, 2, H2]), ALU.mult)


def slots_ffn(k, a):
    nc, h, cent = k.nc, k.h, k.cent
    with ExitStack() as ctx:
        xnT = k.sb("s_xnT", [H2, 2, T], ctx=ctx)
        xr = k.sb("s_xr", [H2, TILES, XA], ctx=ctx)
        phi = k.sb("s_phi", [H2, 2, SLOTS], ctx=ctx)
        token_row = k.sb("s_token_row", [2, B, N], ctx=ctx)
        slots_prepare(k, a["phiT"], xnT, xr, phi, token_row)

        def lanes(name, shape, dt=F32):
            return [k.sb(f"s_{name}{u}", shape, dt, ctx=ctx) for u in range(LANES)]

        quarter = k.sb("s_quarter", [H2, 2, QS], ctx=ctx)
        combine = k.sb("s_combine", [128, B, QC, N], ctx=ctx)
        rowsT = k.sb("s_rowsT", [H2, 2, QE, B, PER], ctx=ctx)
        total = k.sb("s_total", [H2, TILES], ctx=ctx)
        rtotal = k.sb("s_rtotal", [H2, TILES], ctx=ctx)
        ones = k.sb("s_ones", [2, 128], ctx=ctx)
        half = k.sb("s_half", [128, QC], ctx=ctx)
        ln_g, ln_b, b2 = (k.sb(f"s_{n}", [H2, 2, EXPERTS3], ctx=ctx) for n in ("ln_g", "ln_b", "b2"))
        b1 = k.sb("s_b1", [128, HC3, EXPERTS3], ctx=ctx)
        w1, w2 = lanes("w1_", [H2, 2, HID3]), lanes("w2_", [128, HC3, D])
        xT = lanes("xT", [H2, 2, N])
        slot_low, slot_row = lanes("slot_low", [128, QC]), lanes("slot_row", [2, QC, 128])
        disp = lanes("disp", [H2, 2, QS])
        stats, mv = lanes("stats", [128, QC, 6]), lanes("mv", [128, QC, 2])
        ssum, ssq, var, rstd = (lanes(x, [128, QC]) for x in ("ssum", "ssq", "var", "rstd"))
        work = lanes("work", [128, HC3, B * PER])
        hid = work
        normed, comb = ([w[:].rearrange("p c n -> p (c n)")[:, at * QC * D:(at + 1) * QC * D].rearrange(
            "p (c n) -> p c n", c=QC) for w in work] for at in range(2))
        xa = yT = disp
        ys = lanes("ys", [128, QC, XA])
        bank = [k.ps(f"s_bank{u}", [128, 4, 512], ctx) for u in range(LANES)]
        S = {x: k.sem(f"s_{x}") for x in (
            "small", "ones", "cleared", "quarter", "xT", "logits", "slot_low", "c_shifted", "low_turned", "slot_row",
            "d_shifted", "disp", "slots", "step", "aggr", "var", "rstd", "normed", "normed_turned", "rowsT",
            "affine", "lifted", "hid", "lowered", "outT", "yT", "comb", "y_turned", "ys", "summed",
            "added", "finish")}
        loaded = [k.sem(f"s_loaded{r}") for r in range(2)]
        block = ctx.enter_context(nc.Block())

        def pair(u, j, rows=128, n=N):
            return bank[u][0:rows, j, 0:2 * n].rearrange("p (a n) -> p a n", a=2)

        @block.sync
        def _(sp):
            for x, n in ((ln_g, "ln_g"), (ln_b, "ln_b"), (b2, "b2"), (b1, "b1")):
                sp.dma_start(x[:], a[n]).then_inc(S["small"], 16)
            with sp.Fori(0, EXPERTS3 // 2) as i:
                for r in range(2):
                    e = i * 2 + r
                    sp.wait_ge(S["lowered"], e + 1)
                    sp.dma_start(w1[r][:], a["w1"][ds(e, 1)].rearrange("o (a p) n -> p (o a) n", p=H2)).then_inc(loaded[r], 16)
                    sp.dma_start(w2[r][:], a["w2"][ds(e, 1)].rearrange("o (c p) n -> p (o c) n", p=128)).then_inc(loaded[r], 16)

        @block.gpsimd
        def _(pool):
            nc.gpsimd.memset(ones[:], 1.0)
            nc.gpsimd.memset(half[:], -0.5)
            for u in range(LANES):
                nc.gpsimd.memset(ys[u][:, :, D:XA], 1.0).then_inc(S["ones"], 1)
            pool.wait_ge(S["ones"], LANES)
            with pool.Fori(0, QUARTERS) as q:
                with pool.Fori(0, TURNS) as i:
                    for u in range(LANES):
                        n = q * B + i * LANES + u
                        pool.wait_ge(S["slots"], n + 1)
                        nc.gpsimd.tensor_copy(xT[u][:], xnT[:, :, ds((i * LANES + u) * N, N)]).then_inc(S["xT"], 1)
                    for u in range(LANES):
                        n = q * B + i * LANES + u
                        pool.wait_ge(S["var"], n + 1)
                        nc.gpsimd.tensor_tensor(rstd[u][:], var[u][:], half[:], ALU.pow).then_inc(S["rstd"], 1)
                with pool.Fori(0, TURNS) as i:
                    for u in range(LANES):
                        n = q * B + i * LANES + u
                        pool.wait_ge(S["summed"], n + 1)
                        pool.wait_ge(S["outT"], (q + 1) * QE)
                        nc.gpsimd.tensor_copy(comb[u][:], combine[:, ds(i * LANES + u, 1), :, :].rearrange(
                            "p o c n -> p (o c) n")).then_inc(S["comb"], 1)

        @block.tensor
        def _(pe):
            pe.wait_ge(S["ones"], LANES)
            with pe.Fori(0, QUARTERS) as q:
                with pe.Fori(0, TURNS) as i:
                    for u in range(LANES):
                        pe.wait_ge(S["quarter"], q + 1)
                        pe.wait_ge(S["xT"], q * B + i * LANES + u + 1)
                        for c in range(QC):
                            for d in range(2):
                                pe.matmul(pair(u, 0)[:, c, :], quarter[:, d, c * 128:c * 128 + 128], xT[u][:, d, :],
                                          start=(c == 0 and d == 0), stop=False, skip_group_check=True)
                        for t in range(2):
                            for d in range(2):
                                last = pe.matmul(pair(u, 1, H2, QS)[:, t, :], xT[u][:, d, t * H2:t * H2 + H2],
                                                 quarter[:, d, :], start=(t == 0 and d == 0), stop=False,
                                                 skip_group_check=True)
                        last.then_inc(S["logits"], 1)
                    for u in range(LANES):
                        pe.wait_ge(S["slot_low"], q * B + i * LANES + u + 1)
                        for c in range(QC):
                            last = pe.matmul(pair(u, 0)[:, c, :], ones[:],
                                             token_row[:, ds(i * LANES + u, 1), :].rearrange("r o n -> r (o n)"),
                                             start=False, stop=(c == QC - 1), skip_group_check=True)
                        last.then_inc(S["c_shifted"], 1)
                        pe.transpose(bank[u][0:QC, 2, 0:128], slot_low[u][:], k.ident[:]).then_inc(S["low_turned"], 1)
                    for u in range(LANES):
                        pe.wait_ge(S["slot_row"], q * B + i * LANES + u + 1)
                        for t in range(2):
                            last = pe.matmul(pair(u, 1, H2, QS)[:, t, :], ones[:, 0:H2],
                                             slot_row[u][:].rearrange("r c n -> r (c n)"),
                                             start=False, stop=(t == 1), skip_group_check=True)
                        last.then_inc(S["d_shifted"], 1)
                    for u in range(LANES):
                        pe.wait_ge(S["disp"], q * B + i * LANES + u + 1)
                        for c in range(QC):
                            for t in range(2):
                                last = pe.matmul(pair(u, 2, 128, XA)[:, c, :], disp[u][:, t, c * 128:c * 128 + 128],
                                                 xr[:, ds((i * LANES + u) * 2 + t, 1), :].rearrange("p o n -> p (o n)"),
                                                 start=(t == 0), stop=(t == 1))
                        last.then_inc(S["slots"], 1)
                    for u in range(LANES):
                        pe.wait_ge(S["normed"], q * B + i * LANES + u + 1)
                        for d in range(2):
                            for c in range(QC):
                                last = pe.transpose(pair(u, 3, H2, QS)[:, d, c * 128:c * 128 + 128],
                                                    normed[u][:, c, d * H2:d * H2 + H2], k.ident[:])
                        last.then_inc(S["normed_turned"], 1)
                with pe.Fori(0, QE // 2) as i:
                    for r in range(2):
                        n = q * QE + i * 2 + r
                        pe.wait_ge(loaded[r], (q * (QE // 2) + i + 1) * 32)
                        pe.wait_ge(S["affine"], n + 1)
                        for c in range(HC3):
                            for d in range(2):
                                last = pe.matmul(bank[r][:, c // 2, c % 2 * 256:c % 2 * 256 + 256],
                                                 w1[r][:, d, c * 128:c * 128 + 128], xa[r][:, d, :],
                                                 start=(d == 0), stop=(d == 1))
                        last.then_inc(S["lifted"], 1)
                    for r in range(2):
                        n = q * QE + i * 2 + r
                        pe.wait_ge(S["hid"], n + 1)
                        for d in range(2):
                            for c in range(HC3):
                                last = pe.matmul(pair(r, 2, H2, 256)[:, d, :], w2[r][:, c, d * H2:d * H2 + H2],
                                                 hid[r][:, c, :], start=(c == 0), stop=(c == HC3 - 1))
                        last.then_inc(S["lowered"], 1)
                with pe.Fori(0, TURNS) as i:
                    for u in range(LANES):
                        pe.wait_ge(S["yT"], q * B + i * LANES + u + 1)
                        for c in range(QC):
                            for d in range(2):
                                last = pe.transpose(pair(u, 0)[:, c, d * H2:d * H2 + H2],
                                                    yT[u][:, d, c * 128:c * 128 + 128], k.ident[0:H2, 0:H2])
                        last.then_inc(S["y_turned"], 1)
                    for u in range(LANES):
                        pe.wait_ge(S["ys"], q * B + i * LANES + u + 1)
                        pe.wait_ge(S["comb"], q * B + i * LANES + u + 1)
                        for t in range(2):
                            for c in range(QC):
                                last = pe.matmul(pair(u, 1, H2, XA)[:, t, :], comb[u][:, c, t * H2:t * H2 + H2],
                                                 ys[u][:, c, :], start=(c == 0), stop=(c == QC - 1))
                        last.then_inc(S["summed"], 1)

        @block.scalar
        def _(act):
            act.wait_ge(S["small"], 64)
            with act.Fori(0, QUARTERS) as q:
                with act.Fori(0, TURNS) as i:
                    for u in range(LANES):
                        act.wait_ge(S["c_shifted"], q * B + i * LANES + u + 1)
                        nc.scalar.activation(combine[:, ds(i * LANES + u, 1), :, :].rearrange("p o c n -> p (o c) n"),
                                             pair(u, 0), ACT.Exp)
                    for u in range(LANES):
                        act.wait_ge(S["d_shifted"], q * B + i * LANES + u + 1)
                        nc.scalar.activation(disp[u][:], pair(u, 1, H2, QS), ACT.Exp).then_inc(S["disp"], 1)
                    for u in range(LANES):
                        act.wait_ge(S["normed_turned"], q * B + i * LANES + u + 1)
                        nc.scalar.activation(rowsT[:, :, :, ds(i * LANES + u, 1), :].rearrange("c a n o p -> c (a n) (o p)"),
                                             bank[u][0:H2, 3, :].rearrange("c (n p) -> c n p", p=PER),
                                             ACT.Copy).then_inc(S["rowsT"], 1)
                with act.Fori(0, QE // 2) as i:
                    for r in range(2):
                        n = q * QE + i * 2 + r
                        act.wait_ge(S["lifted"], n + 1)
                        for c in range(HC3):
                            last = nc.scalar.activation(hid[r][:, c, :], bank[r][:, c // 2, c % 2 * 256:c % 2 * 256 + 256],
                                                        ACT.Gelu, bias=b1[:, c, ds(n, 1)])
                        last.then_inc(S["hid"], 1)
                    for r in range(2):
                        n = q * QE + i * 2 + r
                        act.wait_ge(S["lowered"], 2 + n + 1)
                        for d in range(2):
                            last = nc.scalar.activation(rowsT[:, d, ds(i * 2 + r, 1), :, :].rearrange("c o b p -> c (o b p)"),
                                                        pair(r, 2, H2, 256)[:, d, :], ACT.Identity, bias=b2[:, d, ds(n, 1)])
                        last.then_inc(S["outT"], 1)
                with act.Fori(0, TURNS) as i:
                    for u in range(LANES):
                        act.wait_ge(S["y_turned"], q * B + i * LANES + u + 1)
                        nc.scalar.activation(ys[u][:, :, 0:D], pair(u, 0), ACT.Copy).then_inc(S["ys"], 1)

        @block.vector
        def _(dve):
            nc.vector.memset(cent[:], 0.0)
            nc.vector.memset(total[:], 0.0).then_inc(S["cleared"], 1)
            nc.vector.memset(ssum[0][:], 0.0).then_inc(S["slots"], LANES)
            nc.vector.memset(ssum[1][:], 0.0).then_inc(S["summed"], LANES)
            nc.vector.memset(ssq[0][:], 0.0).then_inc(S["lowered"], 2)
            dve.wait_ge(S["small"], 64)
            dve.wait_ge(S["cleared"], 1)
            with dve.Fori(0, QUARTERS) as q:
                nc.vector.tensor_copy(quarter[:], phi[:, :, ds(q * QS, QS)]).then_inc(S["quarter"], 1)
                with dve.Fori(0, TURNS) as i:
                    for u in range(LANES):
                        dve.wait_ge(S["logits"], q * B + i * LANES + u + 1)
                        nc.vector.tensor_reduce(slot_low[u][:], pair(u, 0), AXX, ALU.max, negate=True).then_inc(S["slot_low"], 1)
                    for u in range(LANES):
                        dve.wait_ge(S["low_turned"], q * B + i * LANES + u + 1)
                        nc.vector.tensor_tensor(slot_row[u][:], bank[u][0:QC, 2, 0:128].unsqueeze(1).broadcast_to([QC, QC, 128]),
                                                k.ident[0:QC, 0:QC].unsqueeze(2).broadcast_to([QC, QC, 128]),
                                                ALU.mult).then_inc(S["slot_row"], 1)
                    for u in range(LANES):
                        n = q * B + i * LANES + u
                        dve.wait_ge(S["slots"], LANES + n + 1)
                        for c in range(QC):
                            nc.vector.bn_stats(stats[u][:, c, :], pair(u, 2, 128, XA)[:, c, 0:D])
                        nc.vector.tensor_copy(ssum[u][:], pair(u, 2, 128, XA)[:, :, D]).then_inc(S["step"], 1)
                        dve.wait_ge(S["step"], n + 1)
                        nc.vector.scalar_tensor_tensor(out=ssq[u][:], in0=ssum[u][:], scalar=EPS, in1=ssum[u][:],
                                                       op0=ALU.mult, op1=ALU.mult)
                        for c in range(QC):
                            last = nc.vector.bn_aggr(mv[u][:, c, :], stats[u][:, c, :])
                        last.then_inc(S["aggr"], 1)
                    for u in range(LANES):
                        n = q * B + i * LANES + u
                        dve.wait_ge(S["aggr"], n + 1)
                        nc.vector.tensor_tensor(var[u][:], mv[u][:, :, 1], ssq[u][:], ALU.add).then_inc(S["var"], 1)
                    for u in range(LANES):
                        n = q * B + i * LANES + u
                        dve.wait_ge(S["rstd"], n + 1)
                        for c in range(QC):
                            last = nc.vector.tensor_scalar(normed[u][:, c, :], pair(u, 2, 128, XA)[:, c, 0:D],
                                                           mv[u][:, c, 0:1], rstd[u][:, c:c + 1], ALU.subtract, ALU.mult)
                        last.then_inc(S["normed"], 1)
                with dve.Fori(0, QE // 2) as i:
                    for r in range(2):
                        dve.wait_ge(S["rowsT"], (q + 1) * B)
                        e = q * QE + i * 2 + r
                        dve.wait_ge(S["lowered"], e + 1)
                        for d in range(2):
                            last = nc.vector.tensor_scalar(xa[r][:, d, :],
                                                           rowsT[:, d, ds(i * 2 + r, 1), :, :].rearrange("c o b p -> c (o b p)"),
                                                           ln_g[:, d, ds(e, 1)], ln_b[:, d, ds(e, 1)], ALU.mult, ALU.add)
                        last.then_inc(S["affine"], 1)
                with dve.Fori(0, TURNS) as i:
                    for u in range(LANES):
                        dve.wait_ge(S["outT"], (q + 1) * QE)
                        nc.vector.tensor_copy(yT[u][:].rearrange("c a (n p) -> c (a n) p", p=PER),
                                              rowsT[:, :, :, ds(i * LANES + u, 1), :].rearrange("c a n o p -> c (a n) (o p)"),
                                              ).then_inc(S["yT"], 1)
                    for u in range(LANES):
                        n = q * B + i * LANES + u
                        dve.wait_ge(S["summed"], LANES + n + 1)
                        at = ds((i * LANES + u) * 2, 2)
                        got = pair(u, 1, H2, XA)
                        nc.vector.tensor_tensor(cent[:, at, :], cent[:, at, :], got[:, :, 0:D], ALU.add)
                        nc.vector.tensor_tensor(total[:, at], total[:, at], got[:, :, D], ALU.add).then_inc(S["added"], 1)
            dve.wait_ge(S["added"], QUARTERS * B)
            nc.vector.reciprocal(rtotal[:], total[:]).then_inc(S["finish"], 1)
            dve.wait_ge(S["finish"], 1)
            nc.vector.tensor_tensor(cent[:], cent[:], rtotal[:].unsqueeze(2).broadcast_to([H2, TILES, D]),
                                    ALU.mult).then_inc(S["finish"], 1)
            dve.wait_ge(S["finish"], 2)
            nc.vector.tensor_tensor(h[:], h[:], cent[:], ALU.add)



def build(nc, a, out):
    with ExitStack() as ctx:
        k = Core(nc, ctx)
        rows = tiles_of(16) * ROWS
        visits = nc.dram_tensor("visits", (rows, D), F32, kind="Internal").ap()
        steps = [
            lambda: embed(k, a["patchesT"], a["L0_tok_wT"], a["L0_tok_b"], a["txt"], visits),
            lambda: center(k, "n0"),
            lambda: attention0(k, a["L0_attn_WqT"], a["L0_attn_WkT"], a["L0_attn_WvT"]),
            lambda: center(k, "n1"),
            lambda: moe(k, "f0", 8, visits, a["L0_ffn_router_wT"], a["L0_ffn_WgT"], a["L0_ffn_WuT"], a["L0_ffn_WdT"], None, None),
            lambda: center(k, "n2"),
            lambda: attention1(k, a["L1_attn_WqkT"], a["L1_attn_WvT"], a["L1_attn_WprojT"], a["L1_attn_bproj"], a["L1_attn_steps"]),
            lambda: center(k, "n3"),
            lambda: moe(k, "f1", 16, visits, a["L1_ffn_WrT"], a["L1_ffn_W1"], None, a["L1_ffn_W2"], a["L1_ffn_b1"], a["L1_ffn_b2"]),
            lambda: center(k, "n4"),
            lambda: attention2(k, a["L2_attn_Wqkv"], a["L2_attn_features"], a["L2_attn_Wproj"], a["L2_attn_b_proj"]),
            lambda: center(k, "n5", src=k.cent),
            lambda: add_normed(k, a["L2_attn_gamma"], a["L2_attn_beta"]),
            lambda: center(k, "n6"),
            lambda: tree_ffn(k, a["L2_ffn_weights_inT"], a["L2_ffn_weights_out"]),
            lambda: center(k, "n7"),
            lambda: attention3(k, a["L3_attn_WqkT"], a["L3_attn_WvT"], a["L3_attn_WprojT"], a["L3_attn_b_proj"]),
            lambda: center(k, "n8"),
            lambda: slots_ffn(k, a),
        ]
        for step in steps:
            step()
            if len(nc.free_semaphores) < 60:
                k.layer_done()
        stored = k.sem("out_stored")
        block = ctx.enter_context(nc.Block())

        @block.sync
        def _(sp):
            sp.dma_start(out.rearrange("b (a p) d -> p (b a) d", p=H2), k.h[:]).then_inc(stored, 16)
            sp.wait_ge(stored, 16)



def layout(x):
    x = {n: np.asarray(v) for n, v in x.items()}
    P, G = 32, 8
    img = x["x"].reshape(B, G, P, G, P)
    a = {
        "patchesT": img.transpose(2, 4, 0, 1, 3).reshape(P * P, B * G * G),
        "txt": x["txt"],
        "L0_tok_wT": x["L0_tok_w"].T,
        "L0_tok_b": x["L0_tok_b"].reshape(1, D),
    }
    for n in ("Wq", "Wk", "Wv"):
        a[f"L0_attn_{n}T"] = x[f"L0_attn_{n}"].T
    for n in ("router_w", "Wg", "Wu", "Wd"):
        a[f"L0_ffn_{n}T"] = np.swapaxes(x[f"L0_ffn_{n}"], -1, -2)
    a["L1_ffn_WrT"] = x["L1_ffn_Wr"].T
    a["L1_ffn_b1"] = x["L1_ffn_b1"].reshape(16, FC, 128).transpose(0, 2, 1)
    for n in ("W1", "W2", "b2"):
        a[f"L1_ffn_{n}"] = x[f"L1_ffn_{n}"]
    def padded(w):
        z = np.zeros((2 * HEADS, 32, D), w.dtype)
        z[:, 0:DH] = w.reshape(2 * HEADS, DH, D)
        return z.reshape(2 * PAD, D).T

    for at, qkv, proj, bias in (("L1_attn", "Wqkv", "Wproj", "bproj"), ("L3_attn", "w_qkv", "w_proj", "b_proj")):
        a[f"{at}_WqkT"] = padded(x[f"{at}_{qkv}"][0:2 * D])
        a[f"{at}_WvT"] = x[f"{at}_{qkv}"][2 * D:].T
        a[f"{at}_WprojT"] = x[f"{at}_{proj}"].T
        a[f"{at}_{bias}"] = x[f"{at}_{bias}"].reshape(1, D)
    a["L2_attn_Wqkv"], a["L2_attn_Wproj"] = x["L2_attn_W_qkv"], x["L2_attn_W_proj"]
    for n in ("b_proj", "gamma", "beta"):
        a[f"L2_attn_{n}"] = x[f"L2_attn_{n}"].reshape(1, D)
    f = x["L2_attn_random_features"]
    blocks = np.zeros((2, HALF_HEADS, DH, HALF_HEADS, FEATURES), f.dtype)
    for n in range(HALF_HEADS):
        blocks[0, n, :, n, :] = f.T
        blocks[1, n, :, n, :] = -0.5
    a["L2_attn_features"] = blocks.reshape(2, H2, HALF_HEADS * FEATURES)
    a["L2_ffn_weights_inT"] = x["L2_ffn_weights_in"].T
    a["L2_ffn_weights_out"] = x["L2_ffn_weights_out"]
    a["phiT"] = x["L3_ffn_phi"].transpose(2, 0, 1).reshape(D, SLOTS)
    for n in ("w1", "w2"):
        a[n] = x[f"L3_ffn_{n}"]
    for n, c in (("ln_g", H2), ("ln_b", H2), ("b1", 128), ("b2", H2)):
        w = x[f"L3_ffn_{n}"]
        a[n] = w.reshape(EXPERTS3, -1, c).transpose(2, 1, 0)
    a["L1_attn_steps"] = np.stack([x[f"L1_attn_{n}"] for n in ("s_q", "s_k", "s_v", "s_attn", "s_after")]).reshape(1, 5)
    return {n: np.ascontiguousarray(v) for n, v in a.items()}


def kernel(**inputs):
    import concourse.bacc as bacc
    from concourse.bass_utils import run_bass_kernel_spmd

    nc = bacc.Bacc("TRN2", target_bir_lowering=False, num_devices=1)
    arrays = layout(inputs)
    aps = {n: nc.dram_tensor(f"in_{n}", v.shape, mybir.dt.from_np(v.dtype), kind="ExternalInput").ap()
           for n, v in arrays.items()}
    out = nc.dram_tensor("out", (B, N, D), F32, kind="ExternalOutput").ap()
    build(nc, aps, out)
    r = run_bass_kernel_spmd(nc, [{f"in_{n}": v for n, v in arrays.items()}], core_ids=[0])
    return r.results[0]["out"]
```

```python
from contextlib import ExitStack

import numpy as np

import concourse.bass as bass
from concourse import mybir

F32 = mybir.dt.float32
BF16 = mybir.dt.bfloat16
I32 = mybir.dt.int32
U32 = mybir.dt.uint32
ALU = mybir.AluOpType
ACT = mybir.ActivationFunctionType
AXX = mybir.AxisListType.X

B, N, D = 16, 192, 192
H2 = 96
TILES = 2 * B
T = B * N
LANES = 2
TURNS = B // LANES
HEADS, DH = 12, 16
GROUPS = 3
ROUND = 12582912.0
EPS = 1e-5


def ds(start, size):
    return bass.ds(start, size)


class Core:

    def __init__(self, nc, ctx):
        self.nc, self.ctx, self.sems = nc, ctx, []
        self.h = self.sb("h", [H2, TILES, D])
        self.cent = self.sb("cent", [H2, TILES, D])
        self.stats = self.sb("stats", [H2, TILES, 6])
        self.mean = self.sb("mean", [H2, TILES])
        self.rstd = self.sb("rstd", [H2, TILES])
        self.ident = self.sb("ident", [128, 128])

    def sb(self, name, shape, dt=F32, ctx=None):
        return (ctx or self.ctx).enter_context(self.nc.sbuf_tensor(name, shape, dt))

    def ps(self, name, shape, ctx, dt=F32):
        return ctx.enter_context(self.nc.psum_tensor(name, shape, dt))

    def sem(self, name):
        s = self.nc.alloc_semaphore(name=name)
        self.sems.append(s)
        return s

    def layer_done(self):
        if self.sems:
            self.nc.clear_and_free_semaphores(self.sems)
            self.nc.all_engine_barrier()
        self.sems = []


def halves(w):
    return w.rearrange("(a p) n -> p a n", p=H2)



def embed(k, patchesT, tok_wT, tok_b, txt):
    nc, h = k.nc, k.h
    PF, PT = 1024, 64
    FC = PF // 128
    with ExitStack() as ctx:
        pat = [k.sb(f"pat{u}", [128, FC, 128], ctx=ctx) for u in range(LANES)]
        w = k.sb("tok_w", [128, FC, D], ctx=ctx)
        bias = k.sb("tok_bias", [1, D], ctx=ctx)
        ones = k.sb("tok_ones", [1, 128], ctx=ctx)
        acc = [k.ps(f"tok_ps{u}", [128, 512], ctx) for u in range(LANES)]
        pat_in, w_in, txt_in = [k.sem(f"pat_in{u}") for u in range(LANES)], k.sem("tokw_in"), k.sem("txt_in")
        consts, embedded, stored = k.sem("tok_consts"), k.sem("embedded"), k.sem("emb_stored")
        turns = B // 2 // LANES
        src = patchesT.rearrange("(c p) t -> p c t", p=128)
        block = ctx.enter_context(nc.Block())

        @block.sync
        def _(sp):
            sp.dma_start(w[:], tok_wT.rearrange("(c p) n -> p c n", p=128)).then_inc(w_in, 16)
            sp.dma_start(bias[:], tok_b).then_inc(w_in, 16)
            with sp.Fori(0, turns) as i:
                for u in range(LANES):
                    sp.wait_ge(embedded, i * LANES + u + 1)
                    sp.dma_start(pat[u][:], src[:, :, ds((i * LANES + u) * 128, 128)]).then_inc(pat_in[u], 16)

        @block.scalar
        def _(act):
            tx = txt.rearrange("b t d -> t b d")
            hv = h[:, :, :].rearrange("p (b a) d -> p b a d", a=2)
            act.dma_start(hv[PT:H2, :, 0, :], tx[0:H2 - PT]).then_inc(txt_in, 16)
            act.dma_start(hv[:, :, 1, :], tx[H2 - PT:128]).then_inc(txt_in, 16)
            act.wait_ge(txt_in, 32)

        @block.gpsimd
        def _(pool):
            nc.gpsimd.memset(k.ident[:], 0.0).then_inc(consts, 1)
            pool.wait_ge(consts, 1)
            nc.gpsimd.affine_select(out=k.ident[:], in_=k.ident[:], compare_op=ALU.not_equal, fill=1.0,
                                    base=0, pattern=[[-1, 128]], channel_multiplier=1).then_inc(consts, 1)
            pool.wait_ge(consts, 2)
            nc.gpsimd.memset(ones[:], 1.0).then_inc(consts, 1)

        @block.tensor
        def _(pe):
            pe.wait_ge(w_in, 32)
            pe.wait_ge(consts, 3)
            with pe.Fori(0, turns) as i:
                for u in range(LANES):
                    pe.wait_ge(pat_in[u], i * 16 + 16)
                    pe.wait_ge(stored, i * LANES + u + 1)
                    pe.matmul(acc[u][:, 0:D], ones[:], bias[:], start=True, stop=False)
                    for c in range(FC):
                        last = pe.matmul(acc[u][:, 0:D], pat[u][:, c, :], w[:, c, :], start=False, stop=(c == FC - 1))
                    last.then_inc(embedded, 1)

        @block.vector
        def _(dve):
            nc.vector.memset(k.rstd[:, 0:1], 0.0).then_inc(stored, LANES)
            nc.vector.memset(k.rstd[:, 1:2], 0.0).then_inc(embedded, LANES)
            with dve.Fori(0, turns) as i:
                for u in range(LANES):
                    dve.wait_ge(embedded, LANES + i * LANES + u + 1)
                    t = (i * LANES + u) * 4
                    nc.vector.tensor_copy(h[0:PT, ds(t, 1), :], acc[u][0:PT, None, 0:D])
                    nc.vector.tensor_copy(h[0:PT, ds(t + 2, 1), :], acc[u][PT:2 * PT, None, 0:D]).then_inc(stored, 1)



def take_stats(k, x, b):
    for t in range(2):
        at = ds(b * 2 + t, 1)
        last = k.nc.vector.bn_stats(k.stats[:, at, :].rearrange("p o n -> p (o n)"), x[:, at, :].rearrange("p o n -> p (o n)"))
    return last


def norm_stats(k, name, taken=True):
    nc, stats = k.nc, k.stats
    with ExitStack() as ctx:
        both, apart, squares, spread, within, var, std, warm = (
            k.sb(f"{name}_{x}", [H2, TILES], ctx=ctx) for x in ("both", "apart", "squares", "spread", "within", "var", "std", "warm"))
        stepped, varied, rooted, warmed = (k.sem(f"{name}_{x}") for x in ("stepped", "varied", "rooted", "warmed"))
        block = ctx.enter_context(nc.Block())

        @block.vector
        def _(dve):
            nc.vector.memset(warm[:], 1.0).then_inc(warmed, 1)
            first = 0 if taken else 1
            if not taken:
                for b in range(B):
                    last = take_stats(k, k.h, b)
                last.then_inc(stepped, 1)
                dve.wait_ge(stepped, 1)
            nc.vector.tensor_tensor(both[:], stats[:, :, 1], stats[:, :, 4], ALU.add)
            nc.vector.tensor_tensor(apart[:], stats[:, :, 1], stats[:, :, 4], ALU.subtract)
            nc.vector.tensor_tensor(squares[:], stats[:, :, 2], stats[:, :, 5], ALU.add).then_inc(stepped, 1)
            dve.wait_ge(stepped, first + 1)
            nc.vector.tensor_scalar(k.mean[:], both[:], 0.5, None, ALU.mult)
            nc.vector.scalar_tensor_tensor(out=spread[:], in0=apart[:], scalar=0.25, in1=apart[:],
                                           op0=ALU.mult, op1=ALU.mult)
            nc.vector.tensor_scalar(within[:], squares[:], 1.0 / D, EPS, ALU.mult, ALU.add).then_inc(stepped, 1)
            dve.wait_ge(stepped, first + 2)
            nc.vector.tensor_tensor(var[:], spread[:], within[:], ALU.add).then_inc(varied, 1)
            dve.wait_ge(rooted, 1)
            nc.vector.reciprocal(k.rstd[:], std[:])

        @block.scalar
        def _(act):
            act.wait_ge(warmed, 1)
            nc.scalar.activation(std[:], warm[:], ACT.Sqrt).then_inc(warmed, 1)
            act.wait_ge(warmed, 2)
            act.wait_ge(varied, 1)
            nc.scalar.activation(std[:], var[:], ACT.Sqrt).then_inc(rooted, 1)



def normed_rows(k, out, b):
    for t in range(2):
        at = ds(b * 2 + t, 1)
        last = k.nc.vector.tensor_scalar(out[:, t:t + 1, :], k.h[:, at, :], k.mean[:, at], k.rstd[:, at],
                                         ALU.subtract, ALU.mult)
    return last


def turn(pe, k, out, rows):
    for dh in range(2):
        for th in range(2):
            last = pe.transpose(out[:, dh * N + th * H2:dh * N + th * H2 + H2],
                                rows[:, th, dh * H2:dh * H2 + H2], k.ident[0:H2, 0:H2])
    return last


def split2(x):
    return x.rearrange("p (a n) -> p a n", a=2)


def attention0(k, WqT, WkT, WvT, visits):
    nc, h = k.nc, k.h
    with ExitStack() as ctx:
        wq, wk, wv = (k.sb(f"a0_w{x}", [H2, 2, D], ctx=ctx) for x in "qkv")

        def lanes(name, shape, dt=F32):
            return [k.sb(f"a0_{name}{u}", shape, dt, ctx=ctx) for u in range(LANES)]

        rows, xT, qT, kT, v = (lanes(x, [H2, 2, D]) for x in ("rows", "xT", "qT", "kT", "v"))
        prob, probT = (lanes(x, [H2, 2, N]) for x in ("prob", "probT"))
        nmax, psum_, den, rden = (lanes(x, [H2, 2]) for x in ("nmax", "psum", "den", "rden"))
        bank = [[k.ps(f"a0_bank{u}{j}", [128, 512], ctx) for j in range(4)] for u in range(LANES)]
        zeros = k.sb("a0_zeros", [128, 8 * D], ctx=ctx)
        S = {x: k.sem(f"a0_{x}") for x in (
            "w_in", "zeroed", "visits_zeroed", "rows", "turned", "xT", "qkv", "qT", "kT", "v", "scores", "nmax", "prob", "probs_turned",
            "probT", "out", "den", "rden")}
        block = ctx.enter_context(nc.Block())

        def view(u, j):
            return split2(bank[u][j][0:H2, 0:2 * D])

        @block.sync
        def _(sp):
            for w, src in ((wq, WqT), (wk, WkT), (wv, WvT)):
                sp.dma_start(w[:], halves(src)).then_inc(S["w_in"], 16)
            sp.wait_ge(S["zeroed"], 1)
            for n in range(visits.shape[0] // 1024):
                sp.dma_start(visits[n * 1024:(n + 1) * 1024].rearrange("(p c) d -> p (c d)", p=128),
                             zeros[:]).then_inc(S["visits_zeroed"], 16)
            sp.wait_ge(S["visits_zeroed"], 16 * (visits.shape[0] // 1024))

        @block.gpsimd
        def _(pool):
            nc.gpsimd.memset(zeros[:], 0.0).then_inc(S["zeroed"], 1)

        @block.tensor
        def _(pe):
            pe.wait_ge(S["w_in"], 48)
            with pe.Fori(0, TURNS) as i:
                for u in range(LANES):
                    pe.wait_ge(S["rows"], i * LANES + u + 1)
                    turn(pe, k, bank[u][0][0:H2], rows[u]).then_inc(S["turned"], 1)
                for u in range(LANES):
                    pe.wait_ge(S["xT"], i * LANES + u + 1)
                    for j, w in ((1, wq), (2, wk)):
                        for e in range(2):
                            for d in range(2):
                                pe.matmul(view(u, j)[:, e, :], w[:, d, e * H2:e * H2 + H2], xT[u][:, d, :],
                                          start=(d == 0), stop=(d == 1))
                    for t in range(2):
                        for d in range(2):
                            last = pe.matmul(view(u, 3)[:, t, :], xT[u][:, d, t * H2:t * H2 + H2], wv[:, d, :],
                                             start=(d == 0), stop=(d == 1))
                    last.then_inc(S["qkv"], 1)
                for u in range(LANES):
                    pe.wait_ge(S["qT"], i * LANES + u + 1)
                    pe.wait_ge(S["kT"], i * LANES + u + 1)
                    for t in range(2):
                        for e in range(2):
                            last = pe.matmul(view(u, 0)[:, t, :], qT[u][:, e, t * H2:t * H2 + H2], kT[u][:, e, :],
                                             start=(e == 0), stop=(e == 1))
                    last.then_inc(S["scores"], 1)
                for u in range(LANES):
                    pe.wait_ge(S["prob"], i * LANES + u + 1)
                    turn(pe, k, bank[u][1][0:H2], prob[u]).then_inc(S["probs_turned"], 1)
                for u in range(LANES):
                    pe.wait_ge(S["probT"], i * LANES + u + 1)
                    pe.wait_ge(S["v"], i * LANES + u + 1)
                    for t in range(2):
                        for m in range(2):
                            last = pe.matmul(view(u, 2)[:, t, :], probT[u][:, m, t * H2:t * H2 + H2], v[u][:, m, :],
                                             start=(m == 0), stop=(m == 1))
                    last.then_inc(S["out"], 1)

        @block.scalar
        def _(act):
            with act.Fori(0, TURNS) as i:
                for u in range(LANES):
                    act.wait_ge(S["turned"], i * LANES + u + 1)
                    nc.scalar.activation(xT[u][:], view(u, 0), ACT.Copy).then_inc(S["xT"], 1)
                for u in range(LANES):
                    act.wait_ge(S["qkv"], i * LANES + u + 1)
                    nc.scalar.activation(qT[u][:], view(u, 1), ACT.Copy).then_inc(S["qT"], 1)
                    nc.scalar.activation(v[u][:], view(u, 3), ACT.Copy).then_inc(S["v"], 1)
                for u in range(LANES):
                    act.wait_ge(S["nmax"], i * LANES + u + 1)
                    for t in range(2):
                        last = nc.scalar.activation(prob[u][:, t, :], view(u, 0)[:, t, :], ACT.Exp,
                                                    bias=nmax[u][:, t:t + 1], accum_out=psum_[u][:, t:t + 1])
                    last.then_inc(S["prob"], 1)

        @block.vector
        def _(dve):
            with dve.Fori(0, TURNS) as i:
                for u in range(LANES):
                    normed_rows(k, rows[u], i * LANES + u).then_inc(S["rows"], 1)
                for u in range(LANES):
                    dve.wait_ge(S["qkv"], i * LANES + u + 1)
                    nc.vector.tensor_copy(kT[u][:], view(u, 2)).then_inc(S["kT"], 1)
                for u in range(LANES):
                    dve.wait_ge(S["scores"], i * LANES + u + 1)
                    nc.vector.tensor_reduce(nmax[u][:], view(u, 0), AXX, ALU.max, negate=True).then_inc(S["nmax"], 1)
                for u in range(LANES):
                    dve.wait_ge(S["probs_turned"], i * LANES + u + 1)
                    nc.vector.tensor_copy(probT[u][:], view(u, 1)).then_inc(S["probT"], 1)
                    nc.vector.tensor_scalar(den[u][:], psum_[u][:], float(D) ** 0.5, None, ALU.mult).then_inc(S["den"], 1)
                    dve.wait_ge(S["den"], i * LANES + u + 1)
                    nc.vector.reciprocal(rden[u][:], den[u][:]).then_inc(S["rden"], 1)
                for u in range(LANES):
                    dve.wait_ge(S["out"], i * LANES + u + 1)
                    dve.wait_ge(S["rden"], i * LANES + u + 1)
                    t0 = (i * LANES + u) * 2
                    for t in range(2):
                        nc.vector.scalar_tensor_tensor(out=h[:, ds(t0 + t, 1), :], in0=view(u, 2)[:, t:t + 1, :],
                                                       scalar=rden[u][:, t:t + 1], in1=h[:, ds(t0 + t, 1), :],
                                                       op0=ALU.mult, op1=ALU.add)



FF = 4 * D
FC = FF // 128
SCORE_LANES = 8
ML = 4
ROWS = 256


def tiles_of(E):
    return 2 * T // ROWS + E


def norm_and_score(k, name, routerT, logits, E, keep):
    nc, h = k.nc, k.h
    with ExitStack() as ctx:
        w = k.sb(f"{name}_router", [H2, 2, E], ctx=ctx)
        rows = [k.sb(f"{name}_rows{u}", [H2, 2, D], ctx=ctx) for u in range(SCORE_LANES)]
        xT = [k.sb(f"{name}_xT{u}", [H2, 2, D], ctx=ctx) for u in range(SCORE_LANES)]
        pT = [k.ps(f"{name}_pT{u}", [128, 512], ctx) for u in range(SCORE_LANES)]
        pL = [p[0:H2, 2 * D:2 * D + 2 * E] for p in pT]
        w_in, rowed, turned, copied, kept, scored, logged, added = (
            k.sem(f"{name}_{x}") for x in ("w_in", "rowed", "turned", "copied", "kept", "scored", "logged", "row_added"))
        block = ctx.enter_context(nc.Block())

        @block.sync
        def _(sp):
            sp.dma_start(w[:], halves(routerT)).then_inc(w_in, 16)

        @block.vector
        def _(dve):
            nc.vector.memset(rows[0][:, 0, 0:1], 0.0).then_inc(kept, SCORE_LANES)
            if keep:
                nc.vector.memset(rows[1][:, 0, 0:1], 0.0).then_inc(added, SCORE_LANES)
            with dve.Fori(0, B // SCORE_LANES) as i:
                for u in range(SCORE_LANES):
                    dve.wait_ge(kept, i * SCORE_LANES + u + 1)
                    if keep:
                        dve.wait_ge(added, i * SCORE_LANES + u + 1)
                    normed_rows(k, rows[u], i * SCORE_LANES + u).then_inc(rowed, 1)
                for u in range(SCORE_LANES):
                    if keep:
                        dve.wait_ge(rowed, i * SCORE_LANES + u + 1)
                        hb = h[:, ds((i * SCORE_LANES + u) * 2, 2), :]
                        nc.vector.tensor_tensor(hb, hb, rows[u][:], ALU.add).then_inc(added, 1)
                for u in range(SCORE_LANES):
                    dve.wait_ge(scored, i * SCORE_LANES + u + 1)
                    nc.vector.tensor_copy(logits[:, ds((i * SCORE_LANES + u) * 2, 2), :],
                                          split2(pL[u])).then_inc(logged, 1)

        @block.gpsimd
        def _(pool):
            with pool.Fori(0, B // SCORE_LANES) as i:
                for u in range(SCORE_LANES):
                    pool.wait_ge(rowed, i * SCORE_LANES + u + 1)
                    nc.gpsimd.tensor_copy(k.cent[:, ds((i * SCORE_LANES + u) * 2, 2), :], rows[u][:]).then_inc(kept, 1)

        @block.tensor
        def _(pe):
            pe.wait_ge(w_in, 16)
            with pe.Fori(0, B // SCORE_LANES) as i:
                for u in range(SCORE_LANES):
                    pe.wait_ge(rowed, i * SCORE_LANES + u + 1)
                    turn(pe, k, pT[u][0:H2], rows[u]).then_inc(turned, 1)
                for u in range(SCORE_LANES):
                    pe.wait_ge(copied, i * SCORE_LANES + u + 1)
                    for t in range(2):
                        for d in range(2):
                            last = pe.matmul(pL[u][:, t * E:t * E + E], xT[u][:, d, t * H2:t * H2 + H2],
                                             w[:, d, :], start=(d == 0), stop=(d == 1))
                    last.then_inc(scored, 1)

        @block.scalar
        def _(act):
            with act.Fori(0, B // SCORE_LANES) as i:
                for u in range(SCORE_LANES):
                    act.wait_ge(turned, i * SCORE_LANES + u + 1)
                    nc.scalar.activation(xT[u][:], split2(pT[u][0:H2, 0:2 * D]), ACT.Copy).then_inc(copied, 1)


def route(k, name, logits, gate, wts, place_of, expert_of, E, probs_first):
    nc = k.nc
    NT = tiles_of(E)
    MOST = T // ROWS
    with ExitStack() as ctx:
        def big(x, dt=F32):
            return k.sb(f"{name}_{x}", [H2, TILES, E], dt, ctx=ctx)

        def small(x, n=TILES, dt=F32):
            return k.sb(f"{name}_{x}", [H2, n], dt, ctx=ctx)

        iota_i, tri, ones = small("iota_i", NT, I32), small("tri", H2), small("ones", H2)
        iota, iota_less = small("iota", NT), small("iota_less", E)
        best = [small(f"best{r}") for r in range(2)]
        place = [small(f"place{r}") for r in range(2)]
        hot = [big(f"hot{r}") for r in range(2)]
        score, shifted, same, cand, rest, part = (big(x) for x in ("score", "shifted", "same", "cand", "rest", "part"))
        gap, e, den, rden = (small(x) for x in ("gap", "e", "den", "rden"))
        mask, run0, run1, rank = (big(x) for x in ("mask", "run0", "run1", "rank"))
        over = k.sb(f"{name}_over", [H2, E, MOST], ctx=ctx)
        fills, tiles = k.sb(f"{name}_fills", [H2, MOST], ctx=ctx), small("tiles", E)
        end0, end1, begin = small("end0", E), small("end1", E), small("begin", E)
        past = k.sb(f"{name}_past", [H2, NT, E], ctx=ctx)
        passed, tile_expert = small("passed", NT), small("tile_expert", NT)
        before = k.ps(f"{name}_before", [128, 512], ctx)
        total = k.ps(f"{name}_total", [128, 512], ctx)
        step, counted, to_exp, exped, masked, summed = (
            k.sem(f"{name}_{x}") for x in ("step", "counted", "to_exp", "exped", "masked", "summed"))
        block = ctx.enter_context(nc.Block())

        def over_experts(x):
            return x[:].unsqueeze(2).broadcast_to([H2, TILES, E])

        def over_tiles(x):
            return x[:].unsqueeze(1).broadcast_to([H2, TILES, E])

        def by_tile(x):
            return x[0:H2, 0:TILES * E].rearrange("p (t e) -> p t e", e=E)

        @block.gpsimd
        def _(pool):
            nc.gpsimd.iota(iota_i[:], pattern=[[1, NT]], base=0, channel_multiplier=0).then_inc(counted, 1)
            nc.gpsimd.memset(ones[:], 1.0).then_inc(counted, 1)
            pool.wait_ge(counted, 2)
            nc.gpsimd.affine_select(out=tri[:], in_=ones[:], compare_op=ALU.is_gt, fill=0.0, base=0,
                                    pattern=[[1, H2]], channel_multiplier=-1).then_inc(counted, 1)

        @block.scalar
        def _(act):
            act.wait_ge(to_exp, 1)
            if probs_first:
                nc.scalar.activation(cand[:], shifted[:], ACT.Exp).then_inc(exped, 1)
            else:
                nc.scalar.activation(e[:], gap[:], ACT.Exp).then_inc(exped, 1)

        @block.tensor
        def _(pe):
            pe.wait_ge(masked, 1)
            flat = mask[:].rearrange("p t e -> p (t e)")
            pe.matmul(before[0:H2, 0:TILES * E], tri[:], flat, start=True, stop=True)
            pe.matmul(total[0:H2, 0:TILES * E], ones[:], flat, start=True, stop=True).then_inc(summed, 1)

        @block.vector
        def _(dve):
            done = [0]

            def link(ins):
                done[0] += 1
                ins.then_inc(step, 1)
                dve.wait_ge(step, done[0])

            def running_sum(a, b, n, axis):
                d = 1
                while d < n:
                    at = (lambda x, lo, hi: x[:, lo:hi]) if axis == 1 else None
                    nc.vector.tensor_copy(at(b, 0, d), at(a, 0, d))
                    link(nc.vector.tensor_tensor(at(b, d, n), at(a, d, n), at(a, 0, n - d), ALU.add))
                    a, b, d = b, a, 2 * d
                return a

            dve.wait_ge(counted, 3)
            link(nc.vector.tensor_copy(iota[:], iota_i[:]))
            nc.vector.tensor_scalar(fills[:], iota[:, 0:MOST], float(ROWS), None, ALU.mult)
            link(nc.vector.tensor_scalar(iota_less[:], iota[:, 0:E], float(E), None, ALU.subtract))
            x = logits
            if probs_first:
                link(nc.vector.tensor_reduce(den[:], logits[:], AXX, ALU.max))
                link(nc.vector.tensor_tensor(shifted[:], logits[:], over_experts(den), ALU.subtract))
                nc.vector.memset(place[0][:], 0.0).then_inc(to_exp, 1)
                dve.wait_ge(exped, 1)
                link(nc.vector.tensor_reduce(e[:], cand[:], AXX, ALU.add))
                link(nc.vector.reciprocal(rden[:], e[:]))
                link(nc.vector.tensor_tensor(score[:], cand[:], over_experts(rden), ALU.mult))
                x = score
            for r in range(2):
                top = wts[r] if probs_first else best[r]
                link(nc.vector.tensor_reduce(top[:], x[:], AXX, ALU.max))
                link(nc.vector.tensor_tensor(same[:], x[:], over_experts(top), ALU.is_equal))
                link(nc.vector.tensor_tensor(cand[:], same[:], over_tiles(iota_less), ALU.mult))
                link(nc.vector.tensor_reduce(place[r][:], cand[:], AXX, ALU.min))
                link(nc.vector.tensor_tensor(hot[r][:], over_tiles(iota_less), over_experts(place[r]), ALU.is_equal))
                if r == 0:
                    link(nc.vector.scalar_tensor_tensor(out=rest[:], in0=hot[0][:], scalar=-1e30, in1=x[:],
                                                        op0=ALU.mult, op1=ALU.add))
                    x = rest
            nc.vector.tensor_tensor(mask[:], hot[0][:], hot[1][:], ALU.add).then_inc(masked, 1)
            if not probs_first:
                link(nc.vector.tensor_tensor(gap[:], best[1][:], best[0][:], ALU.subtract))
                nc.vector.memset(score[:, 0, 0:1], 0.0).then_inc(to_exp, 1)
                dve.wait_ge(exped, 1)
                link(nc.vector.tensor_scalar(den[:], e[:], 1.0, None, ALU.add))
                link(nc.vector.reciprocal(wts[0][:], den[:]))
                link(nc.vector.tensor_tensor(wts[1][:], wts[0][:], e[:], ALU.mult))
            link(nc.vector.tensor_tensor(part[:], hot[1][:], over_experts(wts[1]), ALU.mult))
            link(nc.vector.tensor_tensor(same[:], hot[0][:], over_experts(wts[0]), ALU.mult))
            nc.vector.tensor_tensor(gate[:], same[:], part[:], ALU.add)

            dve.wait_ge(summed, 1)
            link(nc.vector.tensor_copy(run0[:], by_tile(total)))
            run = running_sum(run0, run1, TILES, 1)
            other = run1 if run is run0 else run0
            link(nc.vector.tensor_tensor(over[:], run[:, TILES - 1, :].unsqueeze(2).broadcast_to([H2, E, MOST]),
                                         fills[:].unsqueeze(1).broadcast_to([H2, E, MOST]), ALU.is_gt))
            link(nc.vector.tensor_reduce(tiles[:], over[:], AXX, ALU.add))
            link(nc.vector.tensor_copy(end0[:], tiles[:]))
            end = running_sum(end0, end1, E, 1)
            link(nc.vector.tensor_tensor(begin[:], end[:], tiles[:], ALU.subtract))
            link(nc.vector.tensor_tensor(rank[:], run[:], by_tile(total), ALU.subtract))
            link(nc.vector.tensor_tensor(other[:], rank[:], by_tile(before), ALU.add))
            link(nc.vector.scalar_tensor_tensor(out=rank[:], in0=over_tiles(begin), scalar=float(ROWS), in1=other[:],
                                                op0=ALU.mult, op1=ALU.add))
            for r in range(2):
                link(nc.vector.tensor_tensor(cand[:], hot[r][:], rank[:], ALU.mult))
                link(nc.vector.tensor_reduce(place[r][:], cand[:], AXX, ALU.add))
                nc.vector.tensor_copy(place_of[:, r, :], place[r][:])
            link(nc.vector.tensor_tensor(past[:], iota[:].unsqueeze(2).broadcast_to([H2, NT, E]),
                                         end[:].unsqueeze(1).broadcast_to([H2, NT, E]), ALU.is_ge))
            link(nc.vector.tensor_reduce(passed[:], past[:], AXX, ALU.add))
            link(nc.vector.tensor_scalar(tile_expert[:], passed[:], float(E - 1), None, ALU.min))
            nc.vector.tensor_copy(expert_of[:], tile_expert[:])


def add_expert_biases(k, name, gate, b2, E, on_gpsimd=None, stats=False):
    nc, h = k.nc, k.h
    with ExitStack() as ctx:
        w = k.sb(f"{name}_b2", [E, D], ctx=ctx)
        rows = [k.sb(f"{name}_g{u}", [H2, 2, E], ctx=ctx) for u in range(ML)]
        gT = [k.sb(f"{name}_gT{u}", [E, N], ctx=ctx) for u in range(ML)]
        pT = [k.ps(f"{name}_gp{u}", [128, 512], ctx) for u in range(ML)]
        pO = [k.ps(f"{name}_go{u}", [128, 512], ctx) for u in range(ML)]
        spare = k.sb(f"{name}_gspare", [H2, ML], ctx=ctx)
        w_in, rowed, turned, copied, summed, added = (
            k.sem(f"{name}_g{x}") for x in ("w_in", "rowed", "turned", "copied", "summed", "added"))
        block = ctx.enter_context(nc.Block())

        @block.sync
        def _(sp):
            sp.dma_start(w[:], b2).then_inc(w_in, 16)

        @block.gpsimd
        def _(pool):
            if on_gpsimd is not None:
                on_gpsimd(pool)

        @block.vector
        def _(dve):
            with dve.Fori(0, B // ML) as i:
                for u in range(ML):
                    nc.vector.tensor_copy(rows[u][:], gate[:, ds((i * ML + u) * 2, 2), :]).then_inc(rowed, 1)
                for u in range(ML):
                    dve.wait_ge(summed, i * ML + u + 1)
                    hb = h[:, ds((i * ML + u) * 2, 2), :]
                    nc.vector.tensor_tensor(hb, hb, split2(pO[u][0:H2, 0:2 * D]), ALU.add).then_inc(added, 1)
                for u in range(ML if stats else 0):
                    dve.wait_ge(added, i * ML + u + 1)
                    nc.vector.memset(spare[:, u:u + 1], 0.0)
                    take_stats(k, h, i * ML + u)

        @block.tensor
        def _(pe):
            pe.wait_ge(w_in, 16)
            with pe.Fori(0, B // ML) as i:
                for u in range(ML):
                    pe.wait_ge(rowed, i * ML + u + 1)
                    for t in range(2):
                        last = pe.transpose(pT[u][0:E, t * H2:t * H2 + H2], rows[u][:, t, :], k.ident[0:H2, 0:H2])
                    last.then_inc(turned, 1)
                for u in range(ML):
                    pe.wait_ge(copied, i * ML + u + 1)
                    for t in range(2):
                        last = pe.matmul(pO[u][0:H2, t * D:t * D + D], gT[u][:, t * H2:t * H2 + H2], w[:],
                                         start=True, stop=True)
                    last.then_inc(summed, 1)

        @block.scalar
        def _(act):
            with act.Fori(0, B // ML) as i:
                for u in range(ML):
                    act.wait_ge(turned, i * ML + u + 1)
                    nc.scalar.activation(gT[u][:], pT[u][0:E, 0:N], ACT.Copy).then_inc(copied, 1)


def send_rows(k, pool, sent, visits, place_of):
    for t in range(TILES):
        for r in range(2):
            pool.indirect_dma_start(out=visits, out_offset=bass.IndirectOffsetOnAxis(ap=place_of[:, r, t:t + 1], axis=0),
                                    in_=k.cent[:, t, :], in_offset=None).then_inc(sent, 16)
    pool.wait_ge(sent, 16 * 2 * TILES)


def send(k, name, visits, place_of, gate, b2, E):
    sent = k.sem(f"{name}_sent")
    if b2 is not None:
        add_expert_biases(k, name, gate, b2, E, lambda pool: send_rows(k, pool, sent, visits, place_of))
        return
    with k.nc.Block() as block:
        @block.gpsimd
        def _(pool):
            send_rows(k, pool, sent, visits, place_of)


def experts(k, name, visits, answers, expert_of, E, w_in1, w_in2, w_down, b1):
    nc = k.nc
    gated = w_in2 is not None
    NT = tiles_of(E)
    RC = ROWS // 128
    with ExitStack() as ctx:
        def two(x, shape):
            return [k.sb(f"{name}_{x}{r}", shape, ctx=ctx) for r in range(2)]

        w1, wd = two("w1_", [H2, 2, FF]), two("wd_", [128, FC, D])
        w2 = two("w2_", [H2, 2, FF]) if gated else None
        bias = None if gated else two("b1_", [128, FC])
        rows, xT = two("vrows", [128, RC, D]), two("vxT", [H2, 2, ROWS])
        hid, out = two("hid", [128, FC, ROWS]), two("vout", [128, RC, D])
        silu = two("silu", [128, ROWS]) if gated else None
        pt = [k.ps(f"{name}_pt{r}", [128, 512], ctx) for r in range(2)]
        pg = [k.ps(f"{name}_pg{j}", [128, 512], ctx) for j in range(3)]
        po = [k.ps(f"{name}_po{r}", [128, 512], ctx) for r in range(2)]
        loaded = [k.sem(f"{name}_loaded{r}") for r in range(2)]
        down_loaded = [k.sem(f"{name}_down_loaded{r}") for r in range(2)]
        rowed = [k.sem(f"{name}_vrowed{r}") for r in range(2)]
        stored = [k.sem(f"{name}_vstored{r}") for r in range(2)]
        turned, copied, lifted, gates, hidden, lowered, outed = (
            k.sem(f"{name}_v{x}") for x in ("turned", "copied", "lifted", "gates", "hidden", "lowered", "outed"))
        block = ctx.enter_context(nc.Block())

        @block.sync
        def _(sp):
            with sp.Fori(0, NT // 2) as i:
                expert = [sp.value_load(expert_of[0:1, ds(i * 2 + r, 1)], min_val=0, max_val=E - 1) for r in range(2)]
                for r in range(2):
                    n = i * 2 + r
                    sp.wait_ge(turned, n + 1)
                    sp.dma_start(rows[r][:], visits[ds(n * ROWS, ROWS), :].rearrange("(c p) d -> p c d", p=128)).then_inc(rowed[r], 16)
                for r in range(2):
                    n = i * 2 + r
                    sp.wait_ge(lifted, (n + 1) * FC)
                    e = expert[r]
                    sp.dma_start(w1[r][:], w_in1[ds(e, 1)].rearrange("o (a p) n -> p (o a) n", p=H2)).then_inc(loaded[r], 16)
                    if gated:
                        sp.dma_start(w2[r][:], w_in2[ds(e, 1)].rearrange("o (a p) n -> p (o a) n", p=H2)).then_inc(loaded[r], 16)
                    else:
                        sp.wait_ge(hidden, (n + 1) * FC + 3)
                        sp.dma_start(bias[r][:], b1[ds(e, 1)].rearrange("o p c -> p (o c)")).then_inc(loaded[r], 16)
                for r in range(2):
                    n = i * 2 + r
                    sp.wait_ge(lowered, n + 1)
                    e = expert[r]
                    sp.dma_start(wd[r][:], w_down[ds(e, 1)].rearrange("o (c p) n -> p (o c) n", p=128)).then_inc(down_loaded[r], 16)

        def over_tiles(engine, step):
            with engine.Fori(0, NT // 2 - 1) as i:
                step(i, True)
            step(NT // 2 - 1, False)

        @block.tensor
        def _(pe):
            def turn_rows(i, r):
                pe.wait_ge(rowed[r], i * 16 + 16)
                for d in range(2):
                    for c in range(RC):
                        last = pe.transpose(pt[r][0:H2, d * ROWS + c * 128:d * ROWS + c * 128 + 128],
                                            rows[r][:, c, d * H2:d * H2 + H2], k.ident[:])
                last.then_inc(turned, 1)

            def step(i, ahead):
                for r in range(2):
                    n = i * 2 + r
                    pe.wait_ge(loaded[r], (i + 1) * 32)
                    pe.wait_ge(copied, n + 1)
                    for j in range(FC):
                        pe.wait_ge(hidden, (n + 2) * FC + j + 1)
                        for a, w in enumerate((w1, w2) if gated else (w1,)):
                            for d in range(2):
                                last = pe.matmul(pg[j % 3][:, a * ROWS:(a + 1) * ROWS], w[r][:, d, j * 128:(j + 1) * 128],
                                                 xT[r][:, d, :], start=(d == 0), stop=(d == 1))
                        last.then_inc(lifted, 1)
                if ahead:
                    for r in range(2):
                        turn_rows(i + 1, r)
                for r in range(2):
                    n = i * 2 + r
                    pe.wait_ge(down_loaded[r], i * 16 + 16)
                    pe.wait_ge(hidden, (n + 3) * FC + 3)
                    pe.wait_ge(outed, n + 1)
                    for c in range(RC):
                        for j in range(FC):
                            last = pe.matmul(po[r][:, c * D:c * D + D], hid[r][:, j, c * 128:c * 128 + 128],
                                             wd[r][:, j, :], start=(j == 0), stop=(j == FC - 1))
                    last.then_inc(lowered, 1)

            for r in range(2):
                turn_rows(0, r)
            over_tiles(pe, step)

        @block.scalar
        def _(act):
            def keep_turned(i):
                for r in range(2):
                    act.wait_ge(turned, 2 + i * 2 + r + 1)
                    nc.scalar.activation(xT[r][:], pt[r][0:H2, 0:2 * ROWS].rearrange("p (a n) -> p a n", a=2), ACT.Copy).then_inc(copied, 1)

            def step(i, ahead):
                for r in range(2):
                    n = i * 2 + r
                    for j in range(FC):
                        act.wait_ge(lifted, (n + 2) * FC + j + 1)
                        if gated:
                            act.wait_ge(hidden, (n + 2) * FC + j + 2)
                            nc.scalar.activation(silu[j % 2][:], pg[j % 3][:, 0:ROWS], ACT.Silu).then_inc(gates, 1)
                        else:
                            nc.scalar.activation(hid[r][:, j, :], pg[j % 3][:, 0:ROWS], ACT.Gelu,
                                                 bias=bias[r][:, j:j + 1]).then_inc(hidden, 1)
                if ahead:
                    keep_turned(i + 1)
                for r in range(2):
                    act.wait_ge(outed, 2 + i * 2 + r + 1)
                    act.dma_start(answers[ds((i * 2 + r) * ROWS, ROWS), :].rearrange("(c p) d -> p c d", p=128),
                                  out[r][:]).then_inc(stored[r], 16)

            keep_turned(0)
            over_tiles(act, step)
            for r in range(2):
                act.wait_ge(stored[r], 16 + 16 * (NT // 2))

        @block.vector
        def _(dve):
            for at, (of, ahead) in enumerate(((stored[0], 16), (stored[1], 16), (turned, 2), (lifted, 2 * FC), (lowered, 2),
                                                  (outed, 2), (hidden, 2 * FC + 3))):
                nc.vector.memset(out[0][:, 0, at:at + 1], 0.0).then_inc(of, ahead)
            with dve.Fori(0, NT // 2) as i:
                for r in range(2):
                    n = i * 2 + r
                    if gated:
                        for j in range(FC):
                            dve.wait_ge(gates, n * FC + j + 1)
                            nc.vector.tensor_tensor(hid[r][:, j, :], silu[j % 2][:], pg[j % 3][:, ROWS:2 * ROWS],
                                                    ALU.mult).then_inc(hidden, 1)
                for r in range(2):
                    n = i * 2 + r
                    dve.wait_ge(lowered, 2 + n + 1)
                    dve.wait_ge(stored[r], i * 16 + 16)
                    nc.vector.tensor_copy(out[r][:], po[r][:, 0:RC * D].rearrange("p (c d) -> p c d", c=RC)).then_inc(outed, 1)


def collect(k, name, answers, wts, place_of, parts=4):
    nc, h = k.nc, k.h
    with ExitStack() as ctx:
        got = [k.sb(f"{name}_got{r}", [H2, TILES, D], ctx=ctx) for r in range(2)]
        come = [k.sem(f"{name}_come{p}") for p in range(parts)]
        scaled, added = k.sem(f"{name}_scaled"), k.sem(f"{name}_added")
        n = TILES // parts
        block = ctx.enter_context(nc.Block())

        @block.gpsimd
        def _(pool):
            for t in range(TILES):
                for r in range(2):
                    pool.indirect_dma_start(out=got[r][:, t, :], out_offset=None, in_=answers,
                                            in_offset=bass.IndirectOffsetOnAxis(ap=place_of[:, r, t:t + 1], axis=0)
                                            ).then_inc(come[t // n], 16)

        @block.vector
        def _(dve):
            for p in range(parts):
                at = slice(p * n, p * n + n)
                dve.wait_ge(come[p], 32 * n)
                for r in range(2):
                    nc.vector.tensor_tensor(got[r][:, at, :], got[r][:, at, :],
                                            wts[r][:, at].unsqueeze(2).broadcast_to([H2, n, D]), ALU.mult).then_inc(scaled, 1)
                for r in range(2):
                    dve.wait_ge(scaled, 2 * p + r + 1)
                    if r:
                        dve.wait_ge(added, 2 * p + 1)
                    nc.vector.tensor_tensor(h[:, at, :], h[:, at, :], got[r][:, at, :], ALU.add).then_inc(added, 1)
                dve.wait_ge(added, 2 * p + 2)
                for b in range(p * n // 2, (p + 1) * n // 2):
                    take_stats(k, h, b)


def moe(k, name, E, visits, routerT, w_in1, w_in2, w_down, b1, b2):
    answers = k.nc.dram_tensor(f"{name}_answers", (tiles_of(E) * ROWS, D), F32, kind="Internal").ap()
    with ExitStack() as ctx:
        logits = k.sb(f"{name}_logits", [H2, TILES, E], ctx=ctx)
        gate = k.sb(f"{name}_gate", [H2, TILES, E], ctx=ctx)
        wts = [k.sb(f"{name}_wts{r}", [H2, TILES], ctx=ctx) for r in range(2)]
        place_of = k.sb(f"{name}_place_of", [H2, 2, TILES], U32, ctx=ctx)
        expert_of = k.sb(f"{name}_expert_of", [H2, tiles_of(E)], U32, ctx=ctx)
        norm_and_score(k, name, routerT, logits, E, keep=b2 is not None)
        route(k, name, logits, gate, wts, place_of, expert_of, E, probs_first=b2 is not None)
        send(k, name, visits, place_of, gate, b2, E)
        experts(k, name, visits, answers, expert_of, E, w_in1, w_in2, w_down, b1)
        collect(k, name, answers, wts, place_of)



PAD = GROUPS * 128
VA = DH + 1


def thirds(bank):
    return bank[:].rearrange("p b (a n) -> p (b a) n", n=256)[:, 0:GROUPS, 0:N]


def times_turned(pe, out, turned_rows, w):
    for t in range(2):
        for d in range(2):
            last = pe.matmul(out[:, t, :], turned_rows[:, d, t * H2:t * H2 + H2], w[:, d, :],
                             start=(d == 0), stop=(d == 1))
    return last



def attention1(k, wqk_src, wv_src, wproj_src, bias_src, steps_src):
    nc, h = k.nc, k.h
    LO, HI, TOP = -4.0, 3.0, 7.0
    S_RING, A_RING, L_RING = 2, 4, 8
    with ExitStack() as ctx:
        def one(name, shape, dt=F32):
            return k.sb(f"a1_{name}", shape, dt, ctx=ctx)

        def ring(n, name, shape, dt=F32):
            return [one(f"{name}{r}", shape, dt) for r in range(n)]

        wqk, wv, wp, bias = one("wqk", [H2, 2, 2 * PAD]), one("wv", [H2, 2, D]), one("wp", [128, GROUPS, D]), one("bias", [H2, D])
        s = one("s", [128, 5])
        inv, fac = one("inv", [128, 5]), one("fac", [128, 4])
        rows, xT = one("rows", [H2, 2, D]), one("xT", [H2, 2, D])
        qk_s, qk_c = one("qk_s", [128, 2, GROUPS, N]), one("qk_c", [128, 2, GROUPS, N])
        q, k_head = ring(2, "q", [128, GROUPS, N], BF16), ring(2, "k_head", [128, HEADS, N], BF16)
        v_s, v_c, v = one("v_s", [H2, 2, D]), one("v_c", [H2, 2, D]), ring(2, "v", [H2, 2, HEADS, 32], BF16)
        at_s, at_c, at = ring(A_RING, "at_s", [H2, 2 * N]), ring(L_RING, "at_c", [H2, 2 * N]), ring(L_RING, "at", [H2, 2 * N], BF16)
        spare = one("spare", [H2, 1])
        o_s, o_c, o = (one(x, [128, GROUPS, N]) for x in ("o_s", "o_c", "o"))
        p_bank = k.ps("a1_p_bank", [128, GROUPS, 512], ctx)
        s_bank = k.ps("a1_s_bank", [128, S_RING, 512], ctx)
        o_bank = k.ps("a1_o_bank", [128, 2, 512], ctx)
        turns = k.ps("a1_turns", [128, 512], ctx)
        S = {x: k.sem(f"a1_{x}") for x in (
            "loaded", "cleared", "consts", "biased", "rows", "turned", "xT", "v_in", "v_scaled", "v_clipped", "v",
            "qk_in", "qk_scaled", "qk_clipped", "qk", "scores", "at_scaled", "at_clipped", "at", "weighed",
            "o_scaled", "o_clipped", "o", "projected", "added")}
        block = ctx.enter_context(nc.Block())
        both = split2(turns[0:H2, 0:2 * D])

        def all_steps(engine, step):
            step(0, 0, True, False, True)
            with engine.Fori(0, (B - 4) // 2) as i:
                step(i * 2 + 1, 1, True, True, True)
                step(i * 2 + 2, 0, True, True, True)
            step(B - 3, 1, True, True, True)
            step(B - 2, 0, True, True, True)
            step(B - 1, 1, True, True, False)
            step(B, 0, False, True, False)

        @block.sync
        def _(sp):
            sp.dma_start(wqk[:], halves(wqk_src)).then_inc(S["loaded"], 16)
            sp.dma_start(wv[:], halves(wv_src)).then_inc(S["loaded"], 16)
            sp.dma_start(wp[:], wproj_src.rearrange("(g p) n -> p g n", p=128)).then_inc(S["loaded"], 16)
            sp.dma_start(bias[:], bias_src.broadcast_to([H2, D])).then_inc(S["loaded"], 16)
            sp.dma_start(s[:], steps_src.broadcast_to([128, 5])).then_inc(S["loaded"], 16)

        @block.gpsimd
        def _(pool):
            for u in range(2):
                nc.gpsimd.memset(k_head[u][:], 0.0)
                nc.gpsimd.memset(v[u][:], 0.0).then_inc(S["cleared"], 1)
            pool.wait_ge(S["loaded"], 80)
            with pool.Fori(0, B) as n:
                pool.wait_ge(S["rows"], n + 1)
                hb = h[:, ds(n * 2, 2), :]
                nc.gpsimd.tensor_tensor(hb, hb, bias[:].unsqueeze(1).broadcast_to([H2, 2, D]),
                                        ALU.add).then_inc(S["biased"], 1)

        @block.tensor
        def _(pe):
            def project_part(which, g):
                c = which * PAD + g * 128
                for d in range(2):
                    last = pe.matmul(p_bank[:, g, which * N:which * N + N], wqk[:, d, c:c + 128], xT[:, d, :],
                                     start=(d == 0), stop=(d == 1))
                return last

            def weigh(u, g):
                for m in range(2):
                    for j in range(4):
                        hd = 4 * g + j
                        last = pe.matmul(thirds(o_bank)[32 * j:32 * j + 32, g, :], v[u][:, m, hd, :],
                                         at[(HEADS * u + hd) % L_RING][:, m * N:m * N + N], start=(m == 0), stop=(m == 1),
                                         skip_group_check=True)
                last.then_inc(S["weighed"], 1)

            def step(n, u, front, back, ahead):
                if front:
                    pe.wait_ge(S["qk"], n + 1)
                for hd in range(HEADS):
                    if front:
                        pe.wait_ge(S["at_scaled"], n * HEADS + hd + 1)
                        for m in range(2):
                            last = pe.matmul(s_bank[0:H2, hd % S_RING, m * N:m * N + N],
                                             k_head[u][:, hd, m * H2:m * H2 + H2], q[u][:, hd % 3, :], start=True, stop=True)
                        last.then_inc(S["scores"], 1)
                    if ahead and hd == 0:
                        pe.wait_ge(S["rows"], n + 2)
                        if back:
                            pe.wait_ge(S["added"], n)
                        pe.wait_ge(S["v_scaled"], n + 1)
                        turn(pe, k, turns[0:H2], rows).then_inc(S["turned"], 1)
                    if ahead and 2 <= hd < 2 + 2 * GROUPS:
                        if hd == 2:
                            pe.wait_ge(S["xT"], n + 2)
                        last = project_part((hd - 2) // GROUPS, (hd - 2) % GROUPS)
                        if hd == 1 + 2 * GROUPS:
                            last.then_inc(S["qk_in"], 1)
                            times_turned(pe, both, xT, wv).then_inc(S["v_in"], 1)
                    if front and hd in (7, 11):
                        pe.wait_ge(S["at"], n * HEADS + hd - 3)
                        if back and hd == 7:
                            pe.wait_ge(S["o_scaled"], n)
                        if hd == 7:
                            pe.wait_ge(S["v"], n + 1)
                        weigh(u, (hd - 7) // 4)
                    if back and hd == 10:
                        pe.wait_ge(S["o"], n)
                        if ahead:
                            pe.wait_ge(S["v_scaled"], n + 2)
                        for t in range(2):
                            for g in range(GROUPS):
                                last = pe.matmul(both[:, t, :], o[:, g, t * H2:t * H2 + H2], wp[:, g, :],
                                                 start=(g == 0), stop=(g == GROUPS - 1))
                        last.then_inc(S["projected"], 1)
                if front:
                    pe.wait_ge(S["at"], n * HEADS + HEADS)
                    weigh(u, GROUPS - 1)

            pe.wait_ge(S["loaded"], 80)
            pe.wait_ge(S["rows"], 1)
            turn(pe, k, turns[0:H2], rows).then_inc(S["turned"], 1)
            pe.wait_ge(S["xT"], 1)
            for which in range(2):
                for g in range(GROUPS):
                    last = project_part(which, g)
            last.then_inc(S["qk_in"], 1)
            times_turned(pe, both, xT, wv).then_inc(S["v_in"], 1)
            all_steps(pe, step)

        @block.scalar
        def _(act):
            def keep_x(n):
                act.wait_ge(S["turned"], n + 1)
                nc.scalar.activation(xT[:], both, ACT.Copy).then_inc(S["xT"], 1)

            def scale_v(n):
                act.wait_ge(S["v_in"], n + 1)
                nc.scalar.activation(v_s[:], both, ACT.Identity, scale=inv[0:H2, 2:3]).then_inc(S["v_scaled"], 1)

            def scale_qk(n):
                act.wait_ge(S["qk_in"], n + 1)
                for w in range(2):
                    last = nc.scalar.activation(qk_s[:, w, :, :], p_bank[:, :, w * N:w * N + N], ACT.Identity, scale=inv[:, w:w + 1])
                last.then_inc(S["qk_scaled"], 1)

            def step(n, u, front, back, ahead):
                for hd in range(HEADS):
                    if front:
                        act.wait_ge(S["scores"], n * HEADS + hd + 1)
                        act.wait_ge(S["at_clipped"], n * HEADS + hd + 1)
                        nc.scalar.activation(at_s[hd % A_RING][:], s_bank[0:H2, hd % S_RING, 0:2 * N], ACT.Relu,
                                             scale=fac[0:H2, 1:2]).then_inc(S["at_scaled"], 1)
                    if ahead and hd == 0:
                        keep_x(n + 1)
                    if back and hd == 2:
                        act.wait_ge(S["weighed"], 2 + n * GROUPS)
                        nc.scalar.activation(o_s[:], thirds(o_bank), ACT.Identity, scale=fac[:, 3:4]).then_inc(S["o_scaled"], 1)
                    if ahead and hd == 8:
                        scale_qk(n + 1)
                        scale_v(n + 1)

            act.wait_ge(S["consts"], 2)
            keep_x(0)
            scale_qk(0)
            scale_v(0)
            all_steps(act, step)

        @block.vector
        def _(dve):
            def clipped(out, x):
                return nc.vector.tensor_scalar(out, x, LO, HI, ALU.max, ALU.min)

            def rounded(out, x):
                return nc.vector.tensor_scalar(out, x, ROUND, ROUND, ALU.add, ALU.subtract)

            def clip_qk(n):
                dve.wait_ge(S["qk_scaled"], n + 1)
                clipped(qk_c[:], qk_s[:]).then_inc(S["qk_clipped"], 1)

            def clip_v(n):
                dve.wait_ge(S["v_scaled"], n + 1)
                clipped(v_c[:], v_s[:]).then_inc(S["v_clipped"], 1)

            def round_v(n, u):
                dve.wait_ge(S["v_clipped"], n + 1)
                rounded(v[u][:, :, :, 0:DH], v_c[:].rearrange("p t (h e) -> p t h e", h=HEADS)).then_inc(S["v"], 1)

            def round_qk(n, u):
                dve.wait_ge(S["qk_clipped"], n + 1)
                rounded(q[u][:], qk_c[:, 0, :, :])
                for j in range(4):
                    at = slice(32 * j, 32 * j + 32)
                    last = rounded(k_head[u][at, 3 * j:3 * j + 3, :], qk_c[at, 1, :, :])
                last.then_inc(S["qk"], 1)

            def unshift(n, u, hd):
                dve.wait_ge(S["at_clipped"], A_RING + n * HEADS + hd + 1)
                r = (HEADS * u + hd) % L_RING
                nc.vector.tensor_scalar(at[r][:], at_c[r][:], ROUND, None, ALU.subtract).then_inc(S["at"], 1)

            def step(n, u, front, back, ahead):
                w = 1 - u
                for hd in range(HEADS):
                    if ahead and hd == 9:
                        clip_qk(n + 1)
                    if front:
                        if hd % 4 == 0:
                            dve.wait_ge(S["weighed"], n * GROUPS + hd // 4 + 1)
                        dve.wait_ge(S["at_scaled"], S_RING + n * HEADS + hd + 1)
                        nc.vector.tensor_scalar(at_c[(HEADS * u + hd) % L_RING][:], at_s[hd % A_RING][:], TOP, ROUND,
                                                ALU.min, ALU.add).then_inc(S["at_clipped"], 1)
                        if hd:
                            unshift(n, u, hd - 1)
                    if back and hd == 4:
                        dve.wait_ge(S["o_scaled"], n)
                        clipped(o_c[:], o_s[:]).then_inc(S["o_clipped"], 1)
                    if ahead and hd == 6 and (not isinstance(n, int) or n < B - 2):
                        dve.wait_ge(S["turned"], n + 2)
                        normed_rows(k, rows, n + 2).then_inc(S["rows"], 1)
                    if back and hd == 5:
                        dve.wait_ge(S["o_clipped"], n)
                        rounded(o[:], o_c[:]).then_inc(S["o"], 1)
                    if ahead and hd == 9:
                        round_qk(n + 1, w)
                if front:
                    unshift(n, u, HEADS - 1)
                if ahead:
                    clip_v(n + 1)
                if back:
                    dve.wait_ge(S["projected"], n)
                    dve.wait_ge(S["biased"], n)
                    hb = h[:, ds(n * 2 - 2, 2), :]
                    nc.vector.scalar_tensor_tensor(out=hb, in0=both, scalar=s[0:H2, 4:5], in1=hb,
                                                   op0=ALU.mult, op1=ALU.add).then_inc(S["added"], 1)
                if ahead:
                    round_v(n + 1, w)
                if back:
                    dve.wait_ge(S["added"], n + 1)
                    nc.vector.memset(spare[:], 0.0)
                    take_stats(k, h, n - 1)

            dve.wait_ge(S["loaded"], 80)
            for c, (of, ahead) in enumerate((("weighed", 2), ("at_scaled", S_RING), ("at_clipped", A_RING), ("added", 1))):
                nc.vector.memset(o_c[:, 0, c:c + 1], 0.0).then_inc(S[of], ahead)
            nc.vector.reciprocal(inv[:], s[:]).then_inc(S["consts"], 1)
            dve.wait_ge(S["consts"], 1)
            nc.vector.tensor_scalar(fac[:, 0:1], s[:, 0:1], s[:, 1:2], DH ** -0.5 / N, ALU.mult, ALU.mult)
            nc.vector.tensor_scalar(fac[:, 2:3], s[:, 3:4], s[:, 2:3], None, ALU.mult).then_inc(S["cleared"], 1)
            dve.wait_ge(S["cleared"], 3)
            nc.vector.tensor_scalar(fac[:, 1:2], fac[:, 0:1], inv[:, 3:4], None, ALU.mult)
            nc.vector.tensor_scalar(fac[:, 3:4], fac[:, 2:3], inv[:, 4:5], None, ALU.mult).then_inc(S["consts"], 1)
            normed_rows(k, rows, 0).then_inc(S["rows"], 1)
            clip_qk(0)
            clip_v(0)
            round_qk(0, 0)
            round_v(0, 0)
            normed_rows(k, rows, 1).then_inc(S["rows"], 1)
            all_steps(dve, step)



def attention3(k, wqk_src, wv_src, wproj_src):
    nc, h = k.nc, k.h
    SCALE = DH ** -0.5
    S_RING, T_RING, P_RING = 3, 2, 6
    with ExitStack() as ctx:
        wqk = k.sb("a3_wqk", [H2, 2, 2 * PAD], ctx=ctx)
        wv = k.sb("a3_wv", [H2, 2, D], ctx=ctx)
        wp = k.sb("a3_wp", [128, GROUPS, D], ctx=ctx)

        def two(name, shape):
            return [k.sb(f"a3_{name}{u}", shape, ctx=ctx) for u in range(2)]

        rows, xT = two("rows", [H2, 2, D]), two("xT", [H2, 2, D])
        k_head, v = two("k_head", [128, HEADS, N]), two("v", [H2, 2, HEADS, 32])
        q, q_low = k.sb("a3_q", [128, GROUPS, N], ctx=ctx), k.sb("a3_q_low", [128, GROUPS, N], ctx=ctx)
        low = k.sb("a3_low", [H2, 2, HEADS, 32], ctx=ctx)
        seventeenth = k.sb("a3_seventeenth", [128, 1], ctx=ctx)
        pick = k.sb("a3_pick", [128, 128], ctx=ctx)
        warm, spare = k.sb("a3_warm", [128, 1], ctx=ctx), k.sb("a3_spare", [H2, 1], ctx=ctx)
        probT = [k.sb(f"a3_probT{r}", [H2, 2 * N], ctx=ctx) for r in range(P_RING)]
        raw, rden, oT = (k.sb(f"a3_{x}", [128, GROUPS, N], ctx=ctx) for x in ("raw", "rden", "oT"))
        s_bank = k.ps("a3_s_bank", [128, S_RING, 512], ctx)
        t_bank = k.ps("a3_t_bank", [128, T_RING, 512], ctx)
        o_bank = k.ps("a3_o_bank", [128, 2, 512], ctx)
        turns = k.ps("a3_turns", [128, 512], ctx)
        S = {x: k.sem(f"a3_{x}") for x in (
            "loaded", "cleared", "preset", "rows", "turned", "xT", "q_in", "k_in", "v_in", "q", "k", "v", "scores", "low",
            "low_turned", "q_low", "scoresT", "prob", "out", "raw", "spread", "rden", "oT", "projected", "added")}
        block = ctx.enter_context(nc.Block())
        both = split2(turns[0:H2, 0:2 * D])

        def all_steps(engine, step):
            step(0, 0, True, False, False, True)
            step(1, 1, True, True, False, True)
            with engine.Fori(0, (B - 4) // 2) as i:
                step(i * 2 + 2, 0, True, True, True, True)
                step(i * 2 + 3, 1, True, True, True, True)
            step(B - 2, 0, True, True, True, True)
            step(B - 1, 1, True, True, True, False)
            step(B, 0, False, True, True, False)
            step(B + 1, 1, False, False, True, False)

        @block.sync
        def _(sp):
            sp.dma_start(wqk[:], halves(wqk_src)).then_inc(S["loaded"], 16)
            sp.dma_start(wv[:], halves(wv_src)).then_inc(S["loaded"], 16)
            sp.dma_start(wp[:], wproj_src.rearrange("(g p) n -> p g n", p=128)).then_inc(S["loaded"], 16)

        @block.gpsimd
        def _(pool):
            for u in range(2):
                nc.gpsimd.memset(v[u][:], 0.0).then_inc(S["cleared"], 1)
                nc.gpsimd.memset(k_head[u][:], 0.0)
            nc.gpsimd.memset(low[:], 0.0)
            pool.wait_ge(S["cleared"], 2)
            for u in range(2):
                nc.gpsimd.memset(v[u][:, :, :, DH:VA], 1.0).then_inc(S["preset"], 1)

        @block.tensor
        def _(pe):
            def project(u):
                for w, (sem, out) in enumerate(((S["q_in"], s_bank[:, :, 0:N]), (S["k_in"], thirds(t_bank)))):
                    for g in range(GROUPS):
                        c = w * PAD + g * 128
                        for d in range(2):
                            last = pe.matmul(out[:, g, :], wqk[:, d, c:c + 128], xT[u][:, d, :], start=(d == 0), stop=(d == 1))
                    last.then_inc(sem, 1)
                times_turned(pe, both, xT[u], wv).then_inc(S["v_in"], 1)

            def weigh(u, g):
                for m in range(2):
                    for j in range(4):
                        hd = 4 * g + j
                        last = pe.matmul(thirds(o_bank)[32 * j:32 * j + 32, g, :], v[u][:, m, hd, :],
                                         probT[hd % P_RING][:, m * N:m * N + N], start=(m == 0), stop=(m == 1),
                                         skip_group_check=True)
                return last

            def step(n, u, front, back, late, ahead):
                w = 1 - u
                for hd in range(HEADS + 2):
                    if front and hd < HEADS:
                        if hd == 0:
                            pe.wait_ge(S["q"], n + 1)
                        if hd % 3 == 0:
                            pe.wait_ge(S["k"], n * 4 + hd // 3 + 1)
                        if hd >= S_RING:
                            pe.wait_ge(S["low"], n * HEADS + hd - S_RING + 1)
                        for t in range(2):
                            last = pe.matmul(s_bank[0:H2, hd % S_RING, t * N:t * N + N], q[:, hd % 3, t * H2:t * H2 + H2],
                                             k_head[u][:, hd, :], start=True, stop=True)
                        last.then_inc(S["scores"], 1)
                    if back and hd >= 2:
                        tn = hd - 2
                        if tn == 0:
                            pe.wait_ge(S["q_low"], n)
                            if front:
                                pe.wait_ge(S["k"], n * 4 + 4)
                        if tn >= T_RING:
                            pe.wait_ge(S["prob"], (n - 1) * HEADS + tn - T_RING + 1)
                        for m in range(2):
                            last = pe.matmul(t_bank[0:H2, tn % T_RING, m * N:m * N + N],
                                             k_head[w][:, tn, m * H2:m * H2 + H2], q_low[:, tn % 3, :], start=True, stop=True)
                        last.then_inc(S["scoresT"], 1)
                    if late and hd == 6:
                        pe.wait_ge(S["oT"], (n - 1) * GROUPS)
                        if front:
                            pe.wait_ge(S["v"], n + 1)
                        else:
                            pe.wait_ge(S["added"], n - 2)
                        for t in range(2):
                            for g in range(GROUPS):
                                last = pe.matmul(both[:, t, :], oT[:, g, t * H2:t * H2 + H2], wp[:, g, :],
                                                 start=(g == 0), stop=(g == GROUPS - 1))
                        last.then_inc(S["projected"], 1)
                    if back and hd in (7, 11):
                        pe.wait_ge(S["prob"], (n - 1) * HEADS + hd - 3)
                        if hd == 7 and late:
                            pe.wait_ge(S["rden"], (n - 1) * GROUPS)
                        weigh(w, (hd - 7) // 4)
                    if ahead and hd == 10:
                        pe.wait_ge(S["rows"], n + 2)
                        pe.wait_ge(S["v"], n + 1)
                        if late:
                            pe.wait_ge(S["added"], n - 1)
                        turn(pe, k, turns[0:H2], rows[w]).then_inc(S["turned"], 1)
                if front:
                    pe.wait_ge(S["low"], n * HEADS + HEADS)
                    for g in range(GROUPS):
                        for t in range(2):
                            last = pe.matmul(s_bank[:, g, t * H2:t * H2 + H2],
                                             low[:, t, 4 * g:4 * g + 4, :].rearrange("p h e -> p (h e)"),
                                             k.ident[0:H2, 0:H2], start=True, stop=True)
                    last.then_inc(S["low_turned"], 1)
                if back:
                    pe.wait_ge(S["prob"], n * HEADS)
                    weigh(w, GROUPS - 1).then_inc(S["out"], 1)
                if ahead:
                    pe.wait_ge(S["xT"], n + 2)
                    pe.wait_ge(S["q_low"], n + 1)
                    project(w)
                if back:
                    pe.wait_ge(S["raw"], n)
                    for g in range(GROUPS):
                        last = pe.matmul(thirds(o_bank)[:, g, :], pick[:], raw[:, g, :], start=True, stop=True)
                    last.then_inc(S["spread"], 1)

            pe.wait_ge(S["loaded"], 48)
            pe.wait_ge(S["rows"], 1)
            turn(pe, k, turns[0:H2], rows[0]).then_inc(S["turned"], 1)
            pe.wait_ge(S["xT"], 1)
            project(0)
            all_steps(pe, step)

        @block.scalar
        def _(act):
            def keep_x(n, u):
                act.wait_ge(S["turned"], n + 1)
                nc.scalar.activation(xT[u][:], both, ACT.Copy).then_inc(S["xT"], 1)

            def keep_kv(n, u):
                act.wait_ge(S["k_in"], n + 1)
                for j in range(4):
                    at = slice(32 * j, 32 * j + 32)
                    nc.scalar.activation(k_head[u][at, 3 * j:3 * j + 3, :], thirds(t_bank)[at], ACT.Identity,
                                         bias=seventeenth[at, :]).then_inc(S["k"], 1)
                    if j == 0:
                        act.wait_ge(S["v_in"], n + 1)
                        nc.scalar.activation(v[u][:, :, :, 0:DH], both.rearrange("p t (h e) -> p t h e", h=HEADS),
                                             ACT.Copy).then_inc(S["v"], 1)

            def step(n, u, front, back, late, ahead):
                w = 1 - u
                for hd in range(HEADS):
                    if back:
                        act.wait_ge(S["scoresT"], (n - 1) * HEADS + hd + 1)
                        nc.scalar.activation(probT[hd % P_RING][:], t_bank[0:H2, hd % T_RING, 0:2 * N], ACT.Exp,
                                             scale=SCALE).then_inc(S["prob"], 1)
                    if ahead and hd == 8:
                        keep_x(n + 1, w)
                if back:
                    act.wait_ge(S["out"], n)
                    nc.scalar.activation(raw[:], thirds(o_bank), ACT.Copy).then_inc(S["raw"], 1)
                if ahead:
                    keep_kv(n + 1, w)

            act.wait_ge(S["preset"], 4)
            nc.scalar.activation(warm[:], seventeenth[:], ACT.Exp)
            keep_x(0, 0)
            keep_kv(0, 0)
            all_steps(act, step)

        @block.vector
        def _(dve):
            def keep_q(n):
                dve.wait_ge(S["q_in"], n + 1)
                nc.vector.tensor_copy(q[:], s_bank[:, :, 0:N]).then_inc(S["q"], 1)

            def step(n, u, front, back, late, ahead):
                w = 1 - u
                if ahead:
                    normed_rows(k, rows[w], n + 1).then_inc(S["rows"], 1)
                for hd in range(HEADS):
                    if front:
                        dve.wait_ge(S["scores"], n * HEADS + hd + 1)
                        nc.vector.tensor_reduce(low[:, :, hd % 3 * 4 + hd // 3, DH], split2(s_bank[0:H2, hd % S_RING, 0:2 * N]),
                                                AXX, ALU.max, negate=True).then_inc(S["low"], 1)
                    if late and hd < GROUPS:
                        dve.wait_ge(S["spread"], n - 1)
                        nc.vector.reciprocal(rden[:, hd, :], thirds(o_bank)[:, hd, :]).then_inc(S["rden"], 1)
                        dve.wait_ge(S["rden"], (n - 2) * GROUPS + hd + 1)
                        nc.vector.tensor_tensor(oT[:, hd, :], raw[:, hd, :], rden[:, hd, :], ALU.mult).then_inc(S["oT"], 1)
                    if late and hd == 8:
                        dve.wait_ge(S["projected"], n - 1)
                        hb = h[:, ds(n * 2 - 4, 2), :]
                        nc.vector.tensor_tensor(hb, both, hb, ALU.add).then_inc(S["added"], 1)
                    if late and hd == 10:
                        dve.wait_ge(S["added"], n - 1)
                        nc.vector.memset(spare[:], 0.0)
                        take_stats(k, h, n - 2)
                if front:
                    dve.wait_ge(S["low_turned"], n + 1)
                    nc.vector.tensor_tensor(q_low[:], q[:], s_bank[:, :, 0:N], ALU.add).then_inc(S["q_low"], 1)
                if ahead:
                    keep_q(n + 1)

            nc.vector.tensor_reduce(seventeenth[:], k.ident[:, DH:128:32], AXX, ALU.add).then_inc(S["preset"], 1)
            nc.vector.tensor_copy(pick[:].rearrange("p (j e) -> p j e", e=32),
                                  k.ident[:, DH:128:32].unsqueeze(2).broadcast_to([128, 4, 32])).then_inc(S["preset"], 1)
            dve.wait_ge(S["preset"], 4)
            normed_rows(k, rows[0], 0).then_inc(S["rows"], 1)
            keep_q(0)
            all_steps(dve, step)



FEATURES = 64
HALF_HEADS = HEADS // 2
PAIRS = HEADS // 2


def attention2(k, wqkv_src, feat_src, halves_src, wproj_src, bias_src):
    nc, cent = k.nc, k.cent
    EPS_N = 1e-6 * FEATURES
    with ExitStack() as ctx:
        def one(name, shape):
            return k.sb(f"a2_{name}", shape, ctx=ctx)

        w, wp, bias = one("w", [H2, 2, 3 * D]), one("wp", [H2, 2, D]), one("bias", [H2, D])
        feat, minus_half = one("feat", [128, HALF_HEADS * FEATURES]), one("minus_half", [H2, 32])
        rows, xT, v = one("rows", [H2, 2, D]), one("xT", [H2, 2, D]), one("v", [H2, 2, HEADS, VA])
        qk, squares = one("qk", [128, 2, 2, N]), one("squares", [H2, 2, 2, N])
        qp, kp = one("qp", [128, PAIRS, N]), one("kp", [H2, 2, HEADS * FEATURES])
        kv = one("kv", [128, PAIRS, 2 * VA])
        den, rden = one("den", [H2, 2, HEADS]), one("rden", [H2, 2, HEADS])
        o, oT, warm = one("o", [H2, 2, D]), one("oT", [H2, 2, D]), one("warm", [128, 1])
        spare = one("spare", [H2, 1])
        front = k.ps("a2_front", [128, 6, 512], ctx)
        back = k.ps("a2_back", [128, 2, 512], ctx)
        S = {x: k.sem(f"a2_{x}") for x in (
            "loaded", "preset", "rows", "based", "turned", "xT", "qkv", "squares", "qk_kept", "v", "lengths", "lengths_kept",
            "q_feat", "qp", "k_feat", "kp", "kv_sums", "kv", "out", "den", "rden", "o", "o_turned", "oT", "projected", "added")}
        block = ctx.enter_context(nc.Block())

        def both(bank, j):
            return split2(bank[0:H2, j, 0:2 * D])

        sums = back[0:H2, 1, 0:2 * HEADS * VA].rearrange("p (t h e) -> p t h e", t=2, h=HEADS)

        def all_steps(engine, step):
            step(0, True, False, True)
            with engine.Fori(0, B - 2) as i:
                step(i + 1, True, True, True)
            step(B - 1, True, True, False)
            step(B, False, True, False)

        @block.sync
        def _(sp):
            sp.dma_start(w[:], halves(wqkv_src)).then_inc(S["loaded"], 16)
            sp.dma_start(wp[:], halves(wproj_src)).then_inc(S["loaded"], 16)
            sp.dma_start(bias[:], bias_src.broadcast_to([H2, D])).then_inc(S["loaded"], 16)
            sp.dma_start(feat[:], feat_src).then_inc(S["loaded"], 16)
            sp.dma_start(minus_half[:], halves_src).then_inc(S["loaded"], 16)

        @block.gpsimd
        def _(pool):
            nc.gpsimd.memset(v[:], 1.0).then_inc(S["preset"], 1)
            nc.gpsimd.memset(kv[:], 0.0).then_inc(S["preset"], 1)
            pool.wait_ge(S["loaded"], 80)
            with pool.Fori(0, B) as n:
                pool.wait_ge(S["rows"], n + 1)
                nc.gpsimd.tensor_tensor(cent[:, ds(n * 2, 2), :], rows[:], bias[:].unsqueeze(1).broadcast_to([H2, 2, D]),
                                        ALU.add).then_inc(S["based"], 1)

        @block.tensor
        def _(pe):
            def keys_by_values(pair):
                for m in range(2):
                    last = pe.matmul(back[:, 0, pair * 2 * VA:(pair + 1) * 2 * VA], kp[:, m, pair * 128:pair * 128 + 128],
                                     v[:, m, 2 * pair:2 * pair + 2, :].rearrange("p h e -> p (h e)"),
                                     start=(m == 0), stop=(m == 1))
                return last

            def queries_by_them(pair):
                for t in range(2):
                    c = (t * PAIRS + pair) * 2 * VA
                    last = pe.matmul(back[0:H2, 1, c:c + 2 * VA], qp[:, pair, t * H2:t * H2 + H2], kv[:, pair, :],
                                     start=True, stop=True)
                return last

            def k_features(t, e):
                return pe.matmul(front[0:H2, 2 * t + e, 0:384], qk[:, 1, e, t * H2:t * H2 + H2], feat[:], start=True, stop=True)

            def step(n, first, second, ahead):
                pe.wait_ge(S["kp"], n + 1)
                if first:
                    pe.wait_ge(S["rows"], n + 1)
                    turn(pe, k, front[0:H2, 3, :], rows).then_inc(S["turned"], 1)
                if second:
                    pe.wait_ge(S["v"], n)
                    keys_by_values(0)
                    keys_by_values(1)
                if first:
                    pe.wait_ge(S["xT"], n + 1)
                for part in range(4):
                    if first:
                        j, e = part // 2, part % 2
                        for d in range(2):
                            c = j * D + e * H2
                            pe.matmul(both(front, j)[:, e, :], w[:, d, c:c + H2], xT[:, d, :], start=(d == 0), stop=(d == 1))
                    if second:
                        last = keys_by_values(2 + part)
                if second:
                    last.then_inc(S["kv_sums"], 1)
                if first:
                    times_turned(pe, both(front, 2), xT, w[:, :, 2 * D:3 * D]).then_inc(S["qkv"], 1)
                if second:
                    pe.wait_ge(S["kv"], n)
                    pe.wait_ge(S["added"], n)
                    queries_by_them(0)
                    queries_by_them(1)
                if first:
                    pe.wait_ge(S["squares"], n + 1)
                    for j in range(2):
                        for e in range(2):
                            last = pe.matmul(front[H2:128, 4 + j, e * N:e * N + N], minus_half[:], squares[:, j, e, :],
                                             start=True, stop=True)
                    last.then_inc(S["lengths"], 1)
                if second:
                    for pair in range(2, PAIRS):
                        last = queries_by_them(pair)
                    last.then_inc(S["out"], 1)
                if first:
                    pe.wait_ge(S["lengths_kept"], n + 1)
                    pe.wait_ge(S["qk_kept"], n + 1)
                    for pair in range(PAIRS):
                        last = pe.matmul(front[:, 3 + pair // 2, pair % 2 * N:pair % 2 * N + N],
                                         feat[:, pair % 3 * 128:pair % 3 * 128 + 128], qk[:, 0, pair // 3, :],
                                         start=True, stop=True)
                    last.then_inc(S["q_feat"], 1)
                if first:
                    pe.wait_ge(S["v"], n + 1)
                    k_features(0, 0)
                    k_features(0, 1)
                    k_features(1, 0)
                if second:
                    pe.wait_ge(S["o"], n)
                    turn(pe, k, back[0:H2, 0, :], o).then_inc(S["o_turned"], 1)
                if first:
                    pe.wait_ge(S["qp"], n + 1)
                    k_features(1, 1).then_inc(S["k_feat"], 1)
                if second:
                    pe.wait_ge(S["oT"], n)
                    times_turned(pe, both(back, 1), oT, wp).then_inc(S["projected"], 1)

            pe.wait_ge(S["loaded"], 80)
            all_steps(pe, step)

        @block.scalar
        def _(act):
            def step(n, first, second, ahead):
                if first:
                    act.wait_ge(S["turned"], n + 1)
                    nc.scalar.activation(xT[:], both(front, 3), ACT.Copy).then_inc(S["xT"], 1)
                    act.wait_ge(S["qkv"], n + 1)
                    q_and_k = front[0:H2, 0:2, 0:2 * D]
                    nc.scalar.activation(squares[:].rearrange("p j e n -> p j (e n)"), q_and_k, ACT.Square).then_inc(S["squares"], 1)
                    nc.scalar.activation(qk[0:H2].rearrange("p j e n -> p j (e n)"), q_and_k, ACT.Copy).then_inc(S["qk_kept"], 1)
                if first:
                    act.wait_ge(S["q_feat"], n + 1)
                    nc.scalar.activation(qp[:].rearrange("p (b a) n -> p b (a n)", a=2),
                                         front[:, 3:6, 0:2 * N], ACT.Exp).then_inc(S["qp"], 1)
                if second:
                    act.wait_ge(S["o_turned"], n)
                    nc.scalar.activation(oT[:], both(back, 0), ACT.Copy).then_inc(S["oT"], 1)
                if first:
                    act.wait_ge(S["k_feat"], n + 1)
                    nc.scalar.activation(kp[:].rearrange("p t (e n) -> p (t e) n", e=2),
                                         front[0:H2, 0:4, 0:384], ACT.Exp).then_inc(S["kp"], 1)

            act.wait_ge(S["preset"], 2)
            nc.scalar.activation(warm[:], k.ident[:, 0:1], ACT.Exp)
            all_steps(act, step)

        @block.vector
        def _(dve):
            def step(n, first, second, ahead):
                if second:
                    dve.wait_ge(S["kv_sums"], n)
                    src = back[:, 0, 0:PAIRS * 2 * VA].rearrange("p (a e) -> p a e", a=PAIRS)
                    nc.vector.tensor_copy(kv[0:64, :, 0:VA], src[0:64, :, 0:VA])
                    nc.vector.tensor_copy(kv[64:128, :, VA:2 * VA], src[64:128, :, VA:2 * VA]).then_inc(S["kv"], 1)
                if first:
                    dve.wait_ge(S["qkv"], n + 1)
                    nc.vector.tensor_copy(v[:, :, :, 0:DH], both(front, 2).rearrange("p t (h e) -> p t h e", h=HEADS)
                                          ).then_inc(S["v"], 1)
                if first:
                    dve.wait_ge(S["lengths"], n + 1)
                    nc.vector.tensor_copy(qk[H2:128].rearrange("p j e n -> p j (e n)"), front[H2:128, 4:6, 0:2 * N]
                                          ).then_inc(S["lengths_kept"], 1)
                if second:
                    dve.wait_ge(S["out"], n)
                    nc.vector.tensor_scalar(den[:], sums[:, :, :, DH], EPS_N, None, ALU.add).then_inc(S["den"], 1)
                    dve.wait_ge(S["den"], n)
                    nc.vector.reciprocal(rden[:], den[:]).then_inc(S["rden"], 1)
                    dve.wait_ge(S["rden"], n)
                    nc.vector.tensor_tensor(o[:].rearrange("p t (h e) -> p t h e", h=HEADS), sums[:, :, :, 0:DH],
                                            rden[:].unsqueeze(3).broadcast_to([H2, 2, HEADS, DH]),
                                            ALU.mult).then_inc(S["o"], 1)
                if ahead:
                    dve.wait_ge(S["based"], n + 1)
                    normed_rows(k, rows, n + 1).then_inc(S["rows"], 1)
                if second:
                    dve.wait_ge(S["projected"], n)
                    dve.wait_ge(S["based"], n)
                    at = cent[:, ds(n * 2 - 2, 2), :]
                    nc.vector.tensor_tensor(at, at, both(back, 1), ALU.add).then_inc(S["added"], 1)
                    dve.wait_ge(S["added"], n + 1)
                    nc.vector.memset(spare[:], 0.0)
                    take_stats(k, cent, n - 1)

            dve.wait_ge(S["preset"], 2)
            nc.vector.memset(o[:, 0, 0:1], 0.0).then_inc(S["kp"], 1)
            nc.vector.memset(o[:, 0, 1:2], 0.0).then_inc(S["added"], 1)
            normed_rows(k, rows, 0).then_inc(S["rows"], 1)
            all_steps(dve, step)


def add_normed(k, gamma_src, beta_src, parts=4):
    nc, h, cent = k.nc, k.h, k.cent
    with ExitStack() as ctx:
        gamma = k.sb("gamma", [H2, D], ctx=ctx)
        beta = k.sb("beta", [H2, D], ctx=ctx)
        scaled = k.sb("an_scaled", [H2, TILES, D], ctx=ctx)
        loaded, scaled_, moved, grown, added = (k.sem(f"an_{x}") for x in ("loaded", "scaled_up", "moved", "grown", "added"))
        n = TILES // parts
        block = ctx.enter_context(nc.Block())

        @block.sync
        def _(sp):
            sp.dma_start(gamma[:], gamma_src.broadcast_to([H2, D])).then_inc(loaded, 16)
            sp.dma_start(beta[:], beta_src.broadcast_to([H2, D])).then_inc(loaded, 16)

        @block.gpsimd
        def _(pool):
            pool.wait_ge(loaded, 32)
            for p in range(parts):
                at = slice(p * n, p * n + n)
                nc.gpsimd.tensor_tensor(h[:, at, :], h[:, at, :], beta[:].unsqueeze(1).broadcast_to([H2, n, D]),
                                        ALU.add).then_inc(moved, 1)

        @block.vector
        def _(dve):
            for p in range(parts):
                for t in range(p * n, p * n + n):
                    last = nc.vector.tensor_scalar(scaled[:, t, :], cent[:, t, :], k.mean[:, t:t + 1], k.rstd[:, t:t + 1],
                                                   ALU.subtract, ALU.mult)
                last.then_inc(scaled_, 1)
            dve.wait_ge(loaded, 32)
            for p in range(parts):
                at = slice(p * n, p * n + n)
                dve.wait_ge(scaled_, p + 1)
                nc.vector.tensor_tensor(cent[:, at, :], scaled[:, at, :], gamma[:].unsqueeze(1).broadcast_to([H2, n, D]),
                                        ALU.mult).then_inc(grown, 1)
            for p in range(parts):
                at = slice(p * n, p * n + n)
                dve.wait_ge(grown, p + 1)
                dve.wait_ge(moved, p + 1)
                nc.vector.tensor_tensor(h[:, at, :], h[:, at, :], cent[:, at, :], ALU.add).then_inc(added, 1)
            for b in range(B):
                if b * 2 % n == 0:
                    dve.wait_ge(added, b * 2 // n + 1)
                take_stats(k, h, b)



NODES = 21
DEPTH = 11


def walk_tree(k, logits, coeff):
    nc = k.nc
    LAST = NODES - 1
    with ExitStack() as ctx:
        def big(x, n=NODES):
            return k.sb(f"tree_{x}", [H2, TILES, n], ctx=ctx)

        seen, right, act, got = big("seen"), big("right"), big("gelu"), big("got")
        a, b = big("a", 1), big("b", 1)
        step, gelued = k.sem("tree_step"), k.sem("tree_gelued")
        block = ctx.enter_context(nc.Block())

        @block.scalar
        def _(eng):
            nc.scalar.activation(act[:], logits[:], ACT.Gelu).then_inc(gelued, 1)

        @block.vector
        def _(dve):
            done = [0]

            def link(ins):
                done[0] += 1
                ins.then_inc(step, 1)
                dve.wait_ge(step, done[0])

            tt = nc.vector.tensor_tensor
            link(nc.vector.tensor_scalar(right[:], logits[:], 0.0, None, ALU.is_gt))
            link(nc.vector.memset(coeff[:], 0.0))
            link(nc.vector.memset(seen[:], 1.0))
            dve.wait_ge(gelued, 1)
            first, level = 0, 0
            while first <= LAST:
                end = min(2 * first + 1, NODES)
                here = slice(first, end)
                link(tt(got[:, :, here], seen[:, :, here], act[:, :, here], ALU.mult))
                whole = min(end, (NODES - 1) // 2)
                if whole > first:
                    up = slice(first, whole)
                    lo, hi = 2 * first + 1, 2 * whole + 1
                    for x, out in ((seen, seen), (got, coeff)):
                        link(tt(out[:, :, lo + 1:hi:2], x[:, :, up], right[:, :, up], ALU.mult))
                        link(tt(out[:, :, lo:hi:2], x[:, :, up], out[:, :, lo + 1:hi:2], ALU.subtract))
                if end > max(whole, first):
                    up = slice(max(whole, first), end)
                    if 2 * first + 1 <= LAST:
                        link(nc.vector.tensor_reduce(a[:], seen[:, :, up], AXX, ALU.add))
                        link(tt(seen[:, :, LAST:NODES], seen[:, :, LAST:NODES], a[:], ALU.add))
                    link(nc.vector.tensor_reduce(b[:], got[:, :, up], AXX, ALU.add))
                    link(tt(coeff[:, :, LAST:NODES], coeff[:, :, LAST:NODES], b[:], ALU.add))
                first, level = 2 * first + 1, level + 1
            link(nc.vector.scalar_tensor_tensor(out=coeff[:, :, LAST:NODES], in0=act[:, :, LAST:NODES],
                                                scalar=float(DEPTH - 1 - level), in1=coeff[:, :, LAST:NODES],
                                                op0=ALU.mult, op1=ALU.add))


def tree_ffn(k, in_T, out_w):
    with ExitStack() as ctx:
        logits = k.sb("tree_logits", [H2, TILES, NODES], ctx=ctx)
        coeff = k.sb("tree_coeff", [H2, TILES, NODES], ctx=ctx)
        norm_and_score(k, "tree", in_T, logits, NODES, keep=False)
        walk_tree(k, logits, coeff)
        add_expert_biases(k, "tree", coeff, out_w, NODES, stats=True)


EXPERTS3, PER = 64, 16
SLOTS = EXPERTS3 * PER



QUARTERS = 4
QE = EXPERTS3 // QUARTERS
QS = SLOTS // QUARTERS
QC = QS // 128
HID3 = 2 * D
HC3 = HID3 // 128
SL = 4
RING = 4
XA = D + 1


def slots_prepare(k, phiT, xnT, phi, token_low):
    nc = k.nc
    EPS_PHI = 1e-6
    with ExitStack() as ctx:
        sq = k.sb("sp_sq", [H2, 2, SLOTS], ctx=ctx)
        norm, root, scale = (k.sb(f"sp_{x}", [H2, 2, PER], ctx=ctx) for x in ("norm", "root", "scale"))
        rows = [k.sb(f"sp_rows{u}", [H2, 2, D], ctx=ctx) for u in range(LANES)]
        xT = [k.sb(f"sp_xT{u}", [H2, 2, D], ctx=ctx) for u in range(LANES)]
        rough_xT = [k.sb(f"sp_rough_xT{u}", [H2, 2, D], BF16, ctx=ctx) for u in range(LANES)]
        rough_phi = k.sb("sp_rough_phi", [H2, 2, SLOTS], BF16, ctx=ctx)
        low = [k.sb(f"sp_low{u}", [H2, 2], ctx=ctx) for u in range(LANES)]
        turns = [k.ps(f"sp_turns{u}", [128, 512], ctx) for u in range(LANES)]
        logits = [k.ps(f"sp_logits{t}", [128, 2, 512], ctx) for t in range(2)]
        spread = [k.ps(f"sp_spread{u}", [128, 512], ctx) for u in range(LANES)]
        S = {x: k.sem(f"sp_{x}") for x in ("loaded", "squared", "normed", "step", "rooted", "scaled", "ones", "rows",
                                          "turned", "rough", "xT", "kept", "logits", "low", "spread", "spread_kept")}
        raw = k.sb("sp_raw", [H2, 2, SLOTS], ctx=ctx)
        spare = k.sb("sp_spare", [H2, 1], ctx=ctx)
        block = ctx.enter_context(nc.Block())

        @block.sync
        def _(sp):
            sp.dma_start(raw[:], halves(phiT)).then_inc(S["loaded"], 16)

        @block.scalar
        def _(act):
            act.wait_ge(S["loaded"], 16)
            nc.scalar.activation(sq[:], raw[:], ACT.Square).then_inc(S["squared"], 1)
            act.wait_ge(S["normed"], 1)
            nc.scalar.activation(root[:], norm[:], ACT.Sqrt).then_inc(S["rooted"], 1)
            with act.Fori(0, TURNS) as i:
                for u in range(LANES):
                    act.wait_ge(S["turned"], i * LANES + u + 1)
                    act.wait_ge(S["kept"], i * LANES + u + 1)
                    rows_T = split2(turns[u][0:H2, 0:2 * D])
                    nc.scalar.activation(rough_xT[u][:], rows_T, ACT.Copy).then_inc(S["rough"], 1)
                    nc.scalar.activation(xT[u][:], rows_T, ACT.Copy).then_inc(S["xT"], 1)

        @block.gpsimd
        def _(pool):
            nc.gpsimd.memset(spare[:], 0.0).then_inc(S["kept"], LANES)
            with pool.Fori(0, TURNS) as i:
                for u in range(LANES):
                    b = i * LANES + u
                    pool.wait_ge(S["xT"], b + 1)
                    nc.gpsimd.tensor_copy(xnT[:, :, ds(b * N, N)], xT[u][:]).then_inc(S["kept"], 1)

        @block.tensor
        def _(pe):
            def turn_rows(b, u):
                pe.wait_ge(S["rows"], b + 1)
                turn(pe, k, turns[u][0:H2], rows[u]).then_inc(S["turned"], 1)

            def step(i, ahead):
                for u in range(LANES):
                    b = i * LANES + u
                    pe.wait_ge(S["rough"], b + 1)
                    for t in range(2):
                        pe.wait_ge(S["low"], b * 2 + t + 1)
                        for s in range(2):
                            for d in range(2):
                                last = pe.matmul(logits[t][0:H2, s, :], rough_xT[u][:, d, t * H2:t * H2 + H2],
                                                 rough_phi[:, d, s * 512:s * 512 + 512], start=(d == 0), stop=(d == 1))
                        last.then_inc(S["logits"], 1)
                for u in range(LANES):
                    if ahead:
                        pe.wait_ge(S["xT"], i * LANES + u + 1)
                        turn_rows((i + 1) * LANES + u, u)
                for u in range(LANES):
                    b = i * LANES + u
                    pe.wait_ge(S["low"], b * 2 + 4)
                    pe.wait_ge(S["spread_kept"], b + 1)
                    for t in range(2):
                        last = pe.matmul(spread[u][:, t * H2:t * H2 + H2], low[u][:, t:t + 1].broadcast_to([H2, 128]),
                                         k.ident[0:H2, 0:H2], start=True, stop=True)
                    last.then_inc(S["spread"], 1)

            for u in range(LANES):
                turn_rows(u, u)
            pe.wait_ge(S["scaled"], 1)
            with pe.Fori(0, TURNS - 1) as i:
                step(i, True)
            step(TURNS - 1, False)

        @block.vector
        def _(dve):
            nc.vector.memset(low[0][:], 0.0).then_inc(S["low"], 2)
            nc.vector.memset(low[1][:], 0.0).then_inc(S["spread_kept"], LANES)
            for u in range(LANES):
                normed_rows(k, rows[u], u).then_inc(S["rows"], 1)
            dve.wait_ge(S["squared"], 1)
            nc.vector.tensor_reduce(scale[:], sq[:].rearrange("c a (n p) -> c a p n", p=PER), AXX, ALU.add).then_inc(S["step"], 1)
            dve.wait_ge(S["step"], 1)
            nc.vector.tensor_scalar(norm[:], scale[:], EPS_PHI, None, ALU.add).then_inc(S["normed"], 1)
            dve.wait_ge(S["rooted"], 1)
            nc.vector.reciprocal(scale[:], root[:]).then_inc(S["step"], 1)
            dve.wait_ge(S["step"], 2)
            for a in range(2):
                last = nc.vector.tensor_tensor(phi[:, a, :].rearrange("c (n p) -> c n p", p=PER),
                                               raw[:, a, :].rearrange("c (n p) -> c n p", p=PER),
                                               scale[:, a, :].unsqueeze(1).broadcast_to([H2, EXPERTS3, PER]), ALU.mult)
            last.then_inc(S["step"], 1)
            dve.wait_ge(S["step"], 3)
            nc.vector.tensor_copy(rough_phi[:], phi[:]).then_inc(S["scaled"], 1)

            def step(i, ahead):
                for u in range(LANES):
                    b = i * LANES + u
                    for t in range(2):
                        dve.wait_ge(S["logits"], b * 2 + t + 1)
                        nc.vector.tensor_reduce(low[u][:, t:t + 1], logits[t][0:H2, :, :], mybir.AxisListType.XY, ALU.max,
                                                negate=True).then_inc(S["low"], 1)
                    if ahead:
                        normed_rows(k, rows[u], b + LANES).then_inc(S["rows"], 1)
                for u in range(LANES):
                    dve.wait_ge(S["spread"], i * LANES + u + 1)
                    nc.vector.tensor_copy(token_low[:, ds(i * LANES + u, 1), :], spread[u][:, None, 0:N]).then_inc(S["spread_kept"], 1)

            with dve.Fori(0, TURNS - 1) as i:
                step(i, True)
            step(TURNS - 1, False)


def slots_ffn(k, a):
    nc, h, cent = k.nc, k.h, k.cent
    with ExitStack() as ctx:
        xnT = k.sb("s_xnT", [H2, 2, T], ctx=ctx)
        phi = k.sb("s_phi", [H2, 2, SLOTS], ctx=ctx)
        token_low = k.sb("s_token_low", [128, B, N], ctx=ctx)
        slots_prepare(k, a["phiT"], xnT, phi, token_low)

        def lanes(name, shape, n=SL):
            return [k.sb(f"s_{name}{u}", shape, ctx=ctx) for u in range(n)]

        quarter = k.sb("s_quarter", [H2, 2, QS], ctx=ctx)
        combine = k.sb("s_combine", [128, B, QC, N], ctx=ctx)
        rowsT = k.sb("s_rowsT", [H2, 2, QE, B, PER], ctx=ctx)
        total, rtotal = k.stats[:, :, 0], k.stats[:, :, 1]
        half = k.sb("s_half", [128, QC], ctx=ctx)
        warm = k.sb("s_warm", [128, 1], ctx=ctx)
        ln_g, ln_b, b2 = (k.sb(f"s_{n}", [H2, 2, EXPERTS3], ctx=ctx) for n in ("ln_g", "ln_b", "b2"))
        b1 = k.sb("s_b1", [128, HC3, EXPERTS3], ctx=ctx)
        w1 = [k.sb(f"s_w1_{r}", [H2, 2, HID3], ctx=ctx) for r in range(RING)]
        w2 = [k.sb(f"s_w2_{r}", [128, HC3, D], ctx=ctx) for r in range(RING)]
        xT = lanes("xT", [H2, 2, N])
        dispT, disp = lanes("dispT", [128, QC, N]), lanes("disp", [H2, 2, QS])
        stats, mv = lanes("stats", [128, QC, 6]), lanes("mv", [128, QC, 2])
        small = k.sb("s_small", [128, 5, SL, QC], ctx=ctx)
        slot_low, ssum, ssq, var, rstd = ([small[:, j, u, :] for u in range(SL)] for j in range(5))
        normed = comb = dispT
        hid, xa, yT = lanes("hid", [128, HC3, B * PER], 2), disp, disp
        ys = lanes("ys", [128, QC, XA])
        rows = [y[0:H2, :, 0:D] for y in ys]
        bank = [k.ps(f"s_bank{u}", [128, 2, 512], ctx) for u in range(SL)]
        S = {x: k.sem(f"s_{x}") for x in (
            "small", "ones", "cleared", "quarter", "xT", "rows", "logits", "slot_low", "c_shifted", "dispT", "disp_turned",
            "disp", "slots", "step", "aggr", "var", "rstd", "normed", "normed_turned", "rowsT",
            "affine", "lifted", "hid", "lowered", "outT", "yT", "comb0", "comb1", "y_turned", "ys", "summed",
            "added", "finish")}
        loaded = [k.sem(f"s_loaded{r}") for r in range(RING)]
        block = ctx.enter_context(nc.Block())

        def pair(u, j, rows=128, n=N):
            return bank[u][0:rows, j, 0:2 * n].rearrange("p (a n) -> p a n", a=2)

        @block.sync
        def _(sp):
            for x, n in ((ln_g, "ln_g"), (ln_b, "ln_b"), (b2, "b2"), (b1, "b1")):
                sp.dma_start(x[:], a[n]).then_inc(S["small"], 16)
            with sp.Fori(0, EXPERTS3 // RING) as i:
                for r in range(RING):
                    e = i * RING + r
                    sp.wait_ge(S["lowered"], e + 1)
                    sp.dma_start(w1[r][:], a["w1"][ds(e, 1)].rearrange("o (a p) n -> p (o a) n", p=H2)).then_inc(loaded[r], 16)
                    sp.dma_start(w2[r][:], a["w2"][ds(e, 1)].rearrange("o (c p) n -> p (o c) n", p=128)).then_inc(loaded[r], 16)

        def keep_weights(engine, copy, q, i, u, *args):
            engine.wait_ge(S["summed"], q * B + i * SL + u + 1)
            engine.wait_ge(S["outT"], 2 + (q + 1) * QE)
            copy(comb[u][:], combine[:, ds(i * SL + u, 1), :, :].rearrange("p o c n -> p (o c) n"), *args
                 ).then_inc(S[f"comb{u % 2}"], 1)

        @block.gpsimd
        def _(pool):
            nc.gpsimd.memset(half[:], -0.5)
            for u in range(SL):
                nc.gpsimd.memset(ys[u][:, :, D:XA], 1.0).then_inc(S["ones"], 1)
            pool.wait_ge(S["ones"], SL)
            with pool.Fori(0, QUARTERS) as q:
                with pool.Fori(0, B // SL) as i:
                    for u in range(SL):
                        n = q * B + i * SL + u
                        pool.wait_ge(S["slots"], n + 1)
                        nc.gpsimd.tensor_copy(xT[u][:], xnT[:, :, ds((i * SL + u) * N, N)]).then_inc(S["xT"], 1)
                    for u in range(SL):
                        n = q * B + i * SL + u
                        pool.wait_ge(S["var"], n + 1)
                        nc.gpsimd.tensor_tensor(rstd[u][:], var[u][:], half[:], ALU.pow).then_inc(S["rstd"], 1)
                with pool.Fori(0, B // SL) as i:
                    for u in range(0, SL, 2):
                        keep_weights(pool, nc.gpsimd.tensor_copy, q, i, u)

        @block.tensor
        def _(pe):
            pe.wait_ge(S["ones"], SL)
            with pe.Fori(0, QUARTERS) as q:
                with pe.Fori(0, B // SL) as i:
                    for u in range(SL):
                        pe.wait_ge(S["quarter"], q + 1)
                        pe.wait_ge(S["xT"], q * B + i * SL + u + 1)
                        for c in range(QC):
                            for d in range(2):
                                last = pe.matmul(pair(u, 0)[:, c, :], quarter[:, d, c * 128:c * 128 + 128], xT[u][:, d, :],
                                                 start=(d == 0), stop=(d == 1))
                        last.then_inc(S["logits"], 1)
                    for u in range(SL):
                        pe.wait_ge(S["dispT"], q * B + i * SL + u + 1)
                        for t in range(2):
                            for c in range(QC):
                                last = pe.transpose(pair(u, 1, H2, QS)[:, t, c * 128:c * 128 + 128],
                                                    dispT[u][:, c, t * H2:t * H2 + H2], k.ident[:])
                        last.then_inc(S["disp_turned"], 1)
                    for u in range(SL):
                        pe.wait_ge(S["rows"], q * B + i * SL + u + 1)
                        pe.wait_ge(S["disp"], q * B + i * SL + u + 1)
                        for c in range(QC):
                            for t in range(2):
                                last = pe.matmul(pair(u, 0)[:, c, :], disp[u][:, t, c * 128:c * 128 + 128],
                                                 rows[u][:, t, :],
                                                 start=(t == 0), stop=(t == 1))
                        last.then_inc(S["slots"], 1)
                    for u in range(SL):
                        pe.wait_ge(S["normed"], q * B + i * SL + u + 1)
                        for d in range(2):
                            for c in range(QC):
                                last = pe.transpose(pair(u, 1, H2, QS)[:, d, c * 128:c * 128 + 128],
                                                    normed[u][:, c, d * H2:d * H2 + H2], k.ident[:])
                        last.then_inc(S["normed_turned"], 1)
                with pe.Fori(0, QE // RING) as i:
                    for pairs in range(RING // 2):
                        for r in (2 * pairs, 2 * pairs + 1):
                            pe.wait_ge(loaded[r], (q * (QE // RING) + i + 1) * 32)
                            pe.wait_ge(S["affine"], q * QE + i * RING + r + 1)
                            for c in range(HC3):
                                for d in range(2):
                                    last = pe.matmul(bank[r % 2 * 2][:, c // 2, c % 2 * 256:c % 2 * 256 + 256],
                                                     w1[r][:, d, c * 128:c * 128 + 128], xa[r % 2][:, d, :],
                                                     start=(d == 0), stop=(d == 1))
                            last.then_inc(S["lifted"], 1)
                        for r in (2 * pairs, 2 * pairs + 1):
                            n = q * QE + i * RING + r
                            pe.wait_ge(S["hid"], n + 1)
                            pe.wait_ge(S["outT"], n + 1)
                            for d in range(2):
                                for c in range(HC3):
                                    last = pe.matmul(pair(r % 2 * 2 + 1, 0, H2, 256)[:, d, :], w2[r][:, c, d * H2:d * H2 + H2],
                                                     hid[r % 2][:, c, :], start=(c == 0), stop=(c == HC3 - 1))
                            last.then_inc(S["lowered"], 1)
                with pe.Fori(0, B // SL) as i:
                    for u in range(SL):
                        pe.wait_ge(S["yT"], q * B + i * SL + u + 1)
                        for c in range(QC):
                            for d in range(2):
                                last = pe.transpose(pair(u, 0)[:, c, d * H2:d * H2 + H2],
                                                    yT[u][:, d, c * 128:c * 128 + 128], k.ident[0:H2, 0:H2])
                        last.then_inc(S["y_turned"], 1)
                    for u in range(SL):
                        pe.wait_ge(S["ys"], q * B + i * SL + u + 1)
                        pe.wait_ge(S[f"comb{u % 2}"], q * (B // 2) + i * (SL // 2) + u // 2 + 1)
                        for t in range(2):
                            for c in range(QC):
                                last = pe.matmul(pair(u, 1, H2, XA)[:, t, :], comb[u][:, c, t * H2:t * H2 + H2],
                                                 ys[u][:, c, :], start=(c == 0), stop=(c == QC - 1))
                        last.then_inc(S["summed"], 1)

        @block.scalar
        def _(act):
            act.wait_ge(S["small"], 64)
            act.wait_ge(S["ones"], SL)
            with act.Fori(0, QUARTERS) as q:
                nc.scalar.activation(warm[:], half[:, 0:1], ACT.Exp)
                with act.Fori(0, B // SL) as i:
                    for u in range(SL):
                        n = q * B + i * SL + u
                        act.wait_ge(S["c_shifted"], n + 1)
                        for c in range(QC):
                            last = nc.scalar.activation(dispT[u][:, c, :], pair(u, 0)[:, c, :], ACT.Exp,
                                                        bias=slot_low[u][:, c:c + 1], accum_out=ssum[u][:, c:c + 1])
                        last.then_inc(S["dispT"], 1)
                    for u in range(SL):
                        act.wait_ge(S["disp_turned"], q * B + i * SL + u + 1)
                        nc.scalar.activation(disp[u][:], pair(u, 1, H2, QS), ACT.Copy).then_inc(S["disp"], 1)
                    for u in range(SL):
                        at = combine[:, ds(i * SL + u, 1), :, :]
                        nc.scalar.activation(at, at, ACT.Exp)
                    for u in range(SL):
                        act.wait_ge(S["normed_turned"], q * B + i * SL + u + 1)
                        nc.scalar.activation(rowsT[:, :, :, ds(i * SL + u, 1), :].rearrange("c a n o p -> c (a n) (o p)"),
                                             bank[u][0:H2, 1, :].rearrange("c (n p) -> c n p", p=PER),
                                             ACT.Copy).then_inc(S["rowsT"], 1)
                nc.scalar.activation(warm[:], half[:, 0:1], ACT.Gelu)
                with act.Fori(0, QE // RING) as i:
                    for r in range(RING):
                        n = q * QE + i * RING + r
                        act.wait_ge(S["lifted"], 2 + n + 1)
                        act.wait_ge(S["lowered"], RING - 2 + n + 1)
                        for c in range(HC3):
                            last = nc.scalar.activation(hid[r % 2][:, c, :], bank[r % 2 * 2][:, c // 2, c % 2 * 256:c % 2 * 256 + 256],
                                                        ACT.Gelu, bias=b1[:, c, ds(n, 1)])
                        last.then_inc(S["hid"], 1)
                with act.Fori(0, B // SL) as i:
                    for u in range(1, SL, 2):
                        keep_weights(act, nc.scalar.activation, q, i, u, ACT.Copy)
                    for u in range(SL):
                        act.wait_ge(S["y_turned"], q * B + i * SL + u + 1)
                        nc.scalar.activation(ys[u][:, :, 0:D], pair(u, 0), ACT.Copy).then_inc(S["ys"], 1)

        @block.vector
        def _(dve):
            nc.vector.memset(cent[:], 0.0)
            nc.vector.memset(total[:], 0.0).then_inc(S["cleared"], 1)
            nc.vector.memset(ssum[0][:], 0.0).then_inc(S["slots"], SL)
            nc.vector.memset(ssum[1][:], 0.0).then_inc(S["summed"], SL)
            nc.vector.memset(ssq[0][:], 0.0).then_inc(S["lowered"], RING)
            nc.vector.memset(ssq[1][:], 0.0).then_inc(S["lifted"], 2)
            nc.vector.memset(var[0][:], 0.0).then_inc(S["outT"], 2)
            dve.wait_ge(S["small"], 64)
            dve.wait_ge(S["cleared"], 1)

            def put_inputs(q, i, r):
                e = q * QE + i * RING + r
                dve.wait_ge(S["lifted"], e + 1)
                for d in range(2):
                    last = nc.vector.tensor_scalar(xa[r % 2][:, d, :],
                                                   rowsT[:, d, ds(i * RING + r, 1), :, :].rearrange("c o b p -> c (o b p)"),
                                                   ln_g[:, d, ds(e, 1)], ln_b[:, d, ds(e, 1)], ALU.mult, ALU.add)
                last.then_inc(S["affine"], 1)

            def put_outputs(q, i, r):
                n = q * QE + i * RING + r
                dve.wait_ge(S["lowered"], RING + n + 1)
                for d in range(2):
                    last = nc.vector.tensor_scalar(rowsT[:, d, ds(i * RING + r, 1), :, :].rearrange("c o b p -> c (o b p)"),
                                                   pair(r % 2 * 2 + 1, 0, H2, 256)[:, d, :], b2[:, d, ds(n, 1)], None, ALU.add)
                last.then_inc(S["outT"], 1)

            with dve.Fori(0, QUARTERS) as q:
                nc.vector.tensor_copy(quarter[:], phi[:, :, ds(q * QS, QS)]).then_inc(S["quarter"], 1)
                with dve.Fori(0, B // SL) as i:
                    for u in range(SL):
                        normed_rows(k, rows[u], i * SL + u).then_inc(S["rows"], 1)
                        dve.wait_ge(S["logits"], q * B + i * SL + u + 1)
                        nc.vector.tensor_reduce(slot_low[u][:], pair(u, 0), AXX, ALU.max, negate=True)
                        nc.vector.tensor_tensor(combine[:, ds(i * SL + u, 1), :, :].rearrange("p o c n -> p (o c) n"), pair(u, 0),
                                                token_low[:, ds(i * SL + u, 1), :].broadcast_to([128, QC, N]),
                                                ALU.add).then_inc(S["c_shifted"], 1)
                    for u in range(SL):
                        n = q * B + i * SL + u
                        dve.wait_ge(S["slots"], SL + n + 1)
                        for c in range(QC):
                            last = nc.vector.bn_stats(stats[u][:, c, :], pair(u, 0)[:, c, :])
                        last.then_inc(S["step"], 1)
                        dve.wait_ge(S["step"], n + 1)
                        nc.vector.scalar_tensor_tensor(out=ssq[u][:], in0=ssum[u][:], scalar=EPS, in1=ssum[u][:],
                                                       op0=ALU.mult, op1=ALU.mult)
                        for c in range(QC):
                            last = nc.vector.bn_aggr(mv[u][:, c, :], stats[u][:, c, :])
                        last.then_inc(S["aggr"], 1)
                    for u in range(SL):
                        n = q * B + i * SL + u
                        dve.wait_ge(S["aggr"], n + 1)
                        nc.vector.tensor_tensor(var[u][:], mv[u][:, :, 1], ssq[u][:], ALU.add).then_inc(S["var"], 1)
                    for u in range(SL):
                        n = q * B + i * SL + u
                        dve.wait_ge(S["rstd"], n + 1)
                        for c in range(QC):
                            last = nc.vector.tensor_scalar(normed[u][:, c, :], pair(u, 0)[:, c, :],
                                                           mv[u][:, c, 0:1], rstd[u][:, c:c + 1], ALU.subtract, ALU.mult)
                        last.then_inc(S["normed"], 1)
                dve.wait_ge(S["rowsT"], (q + 1) * B)
                for r in range(2):
                    put_inputs(q, 0, r)
                with dve.Fori(0, QE // RING - 1) as i:
                    for r in range(RING):
                        put_inputs(q, i, r + 2)
                        if r % 2:
                            put_outputs(q, i, r - 1)
                            put_outputs(q, i, r)
                for r in range(RING):
                    if r + 2 < RING:
                        put_inputs(q, QE // RING - 1, r + 2)
                    if r % 2:
                        put_outputs(q, QE // RING - 1, r - 1)
                        put_outputs(q, QE // RING - 1, r)
                with dve.Fori(0, B // SL) as i:
                    for u in range(SL):
                        dve.wait_ge(S["outT"], 2 + (q + 1) * QE)
                        nc.vector.tensor_copy(yT[u][:].rearrange("c a (n p) -> c (a n) p", p=PER),
                                              rowsT[:, :, :, ds(i * SL + u, 1), :].rearrange("c a n o p -> c (a n) (o p)"),
                                              ).then_inc(S["yT"], 1)
                    for u in range(SL):
                        n = q * B + i * SL + u
                        dve.wait_ge(S["summed"], SL + n + 1)
                        at = ds((i * SL + u) * 2, 2)
                        got = pair(u, 1, H2, XA)
                        nc.vector.tensor_tensor(cent[:, at, :], cent[:, at, :], got[:, :, 0:D], ALU.add)
                        nc.vector.tensor_tensor(total[:, at], total[:, at], got[:, :, D], ALU.add).then_inc(S["added"], 1)
            dve.wait_ge(S["added"], QUARTERS * B)
            nc.vector.reciprocal(rtotal[:], total[:]).then_inc(S["finish"], 1)
            dve.wait_ge(S["finish"], 1)
            nc.vector.tensor_tensor(cent[:], cent[:], rtotal[:].unsqueeze(2).broadcast_to([H2, TILES, D]),
                                    ALU.mult).then_inc(S["finish"], 1)
            dve.wait_ge(S["finish"], 2)
            nc.vector.tensor_tensor(h[:], h[:], cent[:], ALU.add)



def build(nc, a, out):
    with ExitStack() as ctx:
        k = Core(nc, ctx)
        rows = tiles_of(16) * ROWS
        visits = nc.dram_tensor("visits", (rows, D), F32, kind="Internal").ap()
        steps = [
            lambda: embed(k, a["patchesT"], a["L0_tok_wT"], a["L0_tok_b"], a["txt"]),
            lambda: norm_stats(k, "n0", taken=False),
            lambda: attention0(k, a["L0_attn_WqT"], a["L0_attn_WkT"], a["L0_attn_WvT"], visits),
            lambda: norm_stats(k, "n1", taken=False),
            lambda: moe(k, "f0", 8, visits, a["L0_ffn_router_wT"], a["L0_ffn_WgT"], a["L0_ffn_WuT"], a["L0_ffn_WdT"], None, None),
            lambda: norm_stats(k, "n2"),
            lambda: attention1(k, a["L1_attn_WqkT"], a["L1_attn_WvT"], a["L1_attn_WprojT"], a["L1_attn_bproj"], a["L1_attn_steps"]),
            lambda: norm_stats(k, "n3"),
            lambda: moe(k, "f1", 16, visits, a["L1_ffn_WrT"], a["L1_ffn_W1"], None, a["L1_ffn_W2"], a["L1_ffn_b1"], a["L1_ffn_b2"]),
            lambda: norm_stats(k, "n4"),
            lambda: attention2(k, a["L2_attn_Wqkv"], a["L2_attn_features"], a["L2_attn_minus_half"], a["L2_attn_Wproj"], a["L2_attn_b_proj"]),
            lambda: norm_stats(k, "n5"),
            lambda: add_normed(k, a["L2_attn_gamma"], a["L2_attn_beta"]),
            lambda: norm_stats(k, "n6"),
            lambda: tree_ffn(k, a["L2_ffn_weights_inT"], a["L2_ffn_weights_out"]),
            lambda: norm_stats(k, "n7"),
            lambda: attention3(k, a["L3_attn_WqkT"], a["L3_attn_WvT"], a["L3_attn_WprojT"]),
            lambda: norm_stats(k, "n8"),
            lambda: slots_ffn(k, a),
        ]
        for step in steps:
            step()
            if len(nc.free_semaphores) < 60:
                k.layer_done()
        stored = k.sem("out_stored")
        block = ctx.enter_context(nc.Block())

        @block.sync
        def _(sp):
            sp.dma_start(out.rearrange("b (a p) d -> p (b a) d", p=H2), k.h[:]).then_inc(stored, 16)
            sp.wait_ge(stored, 16)



def layout(x):
    x = {n: np.asarray(v) for n, v in x.items()}
    P, G = 32, 8
    img = x["x"].reshape(B, G, P, G, P)
    a = {
        "patchesT": img.transpose(2, 4, 0, 1, 3).reshape(P * P, B * G * G),
        "txt": x["txt"],
        "L0_tok_wT": x["L0_tok_w"].T,
        "L0_tok_b": x["L0_tok_b"].reshape(1, D),
    }
    for n in ("Wq", "Wk", "Wv"):
        a[f"L0_attn_{n}T"] = x[f"L0_attn_{n}"].T
    for n in ("router_w", "Wg", "Wu", "Wd"):
        a[f"L0_ffn_{n}T"] = np.swapaxes(x[f"L0_ffn_{n}"], -1, -2)
    a["L1_ffn_WrT"] = x["L1_ffn_Wr"].T
    a["L1_ffn_b1"] = x["L1_ffn_b1"].reshape(16, FC, 128).transpose(0, 2, 1)
    for n in ("W1", "W2", "b2"):
        a[f"L1_ffn_{n}"] = x[f"L1_ffn_{n}"]
    def padded(w):
        z = np.zeros((2 * HEADS, 32, D), w.dtype)
        z[:, 0:DH] = w.reshape(2 * HEADS, DH, D)
        return z.reshape(2 * PAD, D).T

    for at, qkv, proj in (("L1_attn", "Wqkv", "Wproj"), ("L3_attn", "w_qkv", "w_proj")):
        w = x[f"{at}_{qkv}"]
        a[f"{at}_WqkT"] = padded(w[0:2 * D].reshape(2, 4, GROUPS, DH, D).transpose(0, 2, 1, 3, 4).reshape(2 * D, D))
        a[f"{at}_WvT"] = w[2 * D:].T
        w = np.zeros((HEADS, 32, D), x[f"{at}_{proj}"].dtype)
        w[:, 0:DH] = x[f"{at}_{proj}"].T.reshape(HEADS, DH, D)
        if at == "L3_attn":
            w[0, DH] = x["L3_attn_b_proj"]
        a[f"{at}_WprojT"] = w.reshape(HEADS * 32, D)
    a["L1_attn_bproj"] = x["L1_attn_bproj"].reshape(1, D)
    a["L2_attn_Wqkv"], a["L2_attn_Wproj"] = x["L2_attn_W_qkv"], x["L2_attn_W_proj"]
    for n in ("b_proj", "gamma", "beta"):
        a[f"L2_attn_{n}"] = x[f"L2_attn_{n}"].reshape(1, D)
    f = x["L2_attn_random_features"]
    blocks = np.zeros((128, HALF_HEADS, FEATURES), f.dtype)
    minus_half = np.zeros((HALF_HEADS, DH, 32), f.dtype)
    for n in range(HALF_HEADS):
        blocks[n * DH:(n + 1) * DH, n] = f.T
        blocks[H2 + n, n] = 1.0
        minus_half[n, :, n] = -0.5
    a["L2_attn_features"] = blocks.reshape(128, HALF_HEADS * FEATURES)
    a["L2_attn_minus_half"] = minus_half.reshape(H2, 32)
    a["L2_ffn_weights_inT"] = x["L2_ffn_weights_in"].T
    a["L2_ffn_weights_out"] = x["L2_ffn_weights_out"]
    a["phiT"] = x["L3_ffn_phi"].transpose(2, 0, 1).reshape(D, SLOTS)
    for n in ("w1", "w2"):
        a[n] = x[f"L3_ffn_{n}"]
    for n, c in (("ln_g", H2), ("ln_b", H2), ("b1", 128), ("b2", H2)):
        w = x[f"L3_ffn_{n}"]
        a[n] = w.reshape(EXPERTS3, -1, c).transpose(2, 1, 0)
    a["L1_attn_steps"] = np.stack([x[f"L1_attn_{n}"] for n in ("s_q", "s_k", "s_v", "s_attn", "s_after")]).reshape(1, 5)
    return {n: np.ascontiguousarray(v) for n, v in a.items()}


def kernel(**inputs):
    import concourse.bacc as bacc
    from concourse.bass_utils import run_bass_kernel_spmd

    nc = bacc.Bacc("TRN2", target_bir_lowering=False, num_devices=1)
    arrays = layout(inputs)
    aps = {n: nc.dram_tensor(f"in_{n}", v.shape, mybir.dt.from_np(v.dtype), kind="ExternalInput").ap()
           for n, v in arrays.items()}
    out = nc.dram_tensor("out", (B, N, D), F32, kind="ExternalOutput").ap()
    build(nc, aps, out)
    r = run_bass_kernel_spmd(nc, [{f"in_{n}": v for n, v in arrays.items()}], core_ids=[0])
    return r.results[0]["out"]
```
